# Optimizing a Trainium2 kernel written in Bass

```python
import numpy as np
import jax
import jax.numpy as jnp

def _softmax(x, axis=-1):
    return jax.nn.softmax(x, axis=axis)

def _gelu(x):
    return jax.nn.gelu(x, approximate=True)

def _silu(x):
    return jax.nn.silu(x)

def _sigmoid(x):
    return jax.nn.sigmoid(x)

def _layernorm(x, axis=-1, eps=1e-05):
    m = jnp.mean(x, axis=axis, keepdims=True)
    v = jnp.var(x, axis=axis, keepdims=True)
    return (x - m) / jnp.sqrt(v + eps)

def _scatter_add(tgt, idx, src, axis=0):
    return tgt.at[idx].add(src)

def _segment_sum(src, seg, n):
    return jax.ops.segment_sum(src, seg, n)
kernel_name = 'mk_xattn_seq_d1_seqx_r4_2646a0'

def setup_inputs(seed: int=0):
    np.random.seed(seed)
    _w = jnp.asarray

    def _rec_inputs():
        import jax
        import jax.numpy as jnp
        _rk = jax.random.key(seed)
        x = -0.0002928 + 1 * jax.random.normal(jax.random.fold_in(_rk, 1), (2, 1024, 256), jnp.float32)
        _lenS = 1024 - jax.random.randint(jax.random.fold_in(_rk, 7), (2,), 0, max(1, 1024 // 4) + 1, jnp.int32)
        _lenS2 = 77 - jax.random.randint(jax.random.fold_in(_rk, 8), (2,), 0, max(1, 77 // 4) + 1, jnp.int32)
        _ctx_1024P = jax.random.normal(jax.random.fold_in(_rk, 11), (2, 16, 256), jnp.float32)
        _ctx_1024c = jax.random.dirichlet(jax.random.fold_in(_rk, 511), 0.3 * jnp.ones((16,), jnp.float32), (2, 77))
        _ctx_1024t = jnp.einsum('bsk,bkd->bsd', _ctx_1024c, _ctx_1024P)
        _ctx_1024t = _ctx_1024t * jax.lax.rsqrt(jnp.mean(jnp.square(_ctx_1024t)) + 1e-12) * 0.953939
        ctx_1024 = -1.39393e-06 + 0.999914 * (_ctx_1024t + 0.3 * jax.random.normal(jax.random.fold_in(_rk, 611), (2, 77, 256), jnp.float32))
        return (x, ctx_1024)
    x, ctx_1024 = _rec_inputs()

    def _L0_xattn_setup():
        import jax, jax.numpy as jnp
        import numpy as np
        B, S, SE, D, H, FF, E, K = (2, 512, 512, 256, 16, 1024, 8, 2)
        HD = D // H

        def _layernorm(x, g, b):
            m = x.mean(-1, keepdims=True)
            v = ((x - m) ** 2).mean(-1, keepdims=True)
            return (x - m) / jnp.sqrt(v + 1e-05) * g + b

        def _attn(q_in, k_in, v_in, wq, bq, wk, bk, wv, bv, wo, bo, causal):
            Bq, Sq, Dm = q_in.shape
            Sk = k_in.shape[1]
            Q = (q_in @ wq + bq).reshape(Bq, Sq, H, HD)
            Kp = (k_in @ wk + bk).reshape(Bq, Sk, H, HD)
            V = (v_in @ wv + bv).reshape(Bq, Sk, H, HD)
            scores = jnp.einsum('bqhd,bkhd->bhqk', Q, Kp) / jnp.sqrt(jnp.float32(HD))
            if causal:
                mask = jnp.tril(jnp.ones((Sq, Sk), bool))
                scores = jnp.where(mask, scores, -jnp.inf)
            a = jax.nn.softmax(scores, axis=-1)
            o = jnp.einsum('bhqk,bkhd->bqhd', a, V).reshape(Bq, Sq, Dm)
            return o @ wo + bo

        def _moe(x, rw, rb, w1, b1, w2, b2):
            T = x.shape[0] * x.shape[1]
            xf = x.reshape(T, D)
            router_weights = jax.nn.softmax(xf @ rw + rb, axis=-1)
            topw, topi = jax.lax.top_k(router_weights, K)
            topw = jax.nn.softmax(topw, axis=-1)
            combine = jnp.zeros((T, E), xf.dtype).at[jnp.arange(T)[:, None], topi].add(topw)
            h = jax.nn.gelu(jnp.einsum('td,edf->etf', xf, w1) + b1[:, None, :], approximate=False)
            eo = jnp.einsum('etf,efd->etd', h, w2) + b2[:, None, :]
            out = jnp.einsum('etd,te->td', eo, combine)
            return out.reshape(x.shape)
        key = jax.random.key(seed)
        ks = jax.random.split(key, 32)
        w = lambda k, shape: jax.random.normal(k, shape, jnp.float32) * 0.02
        inp = {'x': jax.random.normal(ks[0], (B, S, D), jnp.float32), 'encoder_output': jax.random.normal(ks[1], (B, SE, D), jnp.float32), 'sa_wq': w(ks[2], (D, D)), 'sa_bq': jnp.zeros((D,), jnp.float32), 'sa_wk': w(ks[3], (D, D)), 'sa_bk': jnp.zeros((D,), jnp.float32), 'sa_wv': w(ks[4], (D, D)), 'sa_bv': jnp.zeros((D,), jnp.float32), 'sa_wo': w(ks[5], (D, D)), 'sa_bo': jnp.zeros((D,), jnp.float32), 'ca_wq': w(ks[6], (D, D)), 'ca_bq': jnp.zeros((D,), jnp.float32), 'ca_wk': w(ks[7], (D, D)), 'ca_bk': jnp.zeros((D,), jnp.float32), 'ca_wv': w(ks[8], (D, D)), 'ca_bv': jnp.zeros((D,), jnp.float32), 'ca_wo': w(ks[9], (D, D)), 'ca_bo': jnp.zeros((D,), jnp.float32), 'ln1_g': jnp.ones((D,), jnp.float32), 'ln1_b': jnp.zeros((D,), jnp.float32), 'ln2_g': jnp.ones((D,), jnp.float32), 'ln2_b': jnp.zeros((D,), jnp.float32), 'ln3_g': jnp.ones((D,), jnp.float32), 'ln3_b': jnp.zeros((D,), jnp.float32), 'router_w': w(ks[10], (D, E)), 'router_b': jnp.zeros((E,), jnp.float32), 'e_w1': w(ks[11], (E, D, FF)), 'e_b1': jnp.zeros((E, FF), jnp.float32), 'e_w2': w(ks[12], (E, FF, D)), 'e_b2': jnp.zeros((E, D), jnp.float32)}
        return inp
    _L0_xattn_all = _L0_xattn_setup()
    _L0_xattn_in = {k: v for k, v in _L0_xattn_all.items() if k in ('sa_wq', 'sa_bq', 'sa_wk', 'sa_bk', 'sa_wv', 'sa_bv', 'sa_wo', 'sa_bo', 'ca_wq', 'ca_bq', 'ca_wk', 'ca_bk', 'ca_wv', 'ca_bv', 'ca_wo', 'ca_bo', 'ln1_g', 'ln1_b', 'ln2_g', 'ln2_b', 'ln3_g', 'ln3_b', 'router_w', 'router_b', 'e_w1', 'e_b1', 'e_w2', 'e_b2')}
    del _L0_xattn_all
    return {'x': x, 'ctx_1024': ctx_1024, 'L0_xattn_sa_wq': _L0_xattn_in['sa_wq'], 'L0_xattn_sa_bq': _L0_xattn_in['sa_bq'], 'L0_xattn_sa_wk': _L0_xattn_in['sa_wk'], 'L0_xattn_sa_bk': _L0_xattn_in['sa_bk'], 'L0_xattn_sa_wv': _L0_xattn_in['sa_wv'], 'L0_xattn_sa_bv': _L0_xattn_in['sa_bv'], 'L0_xattn_sa_wo': _L0_xattn_in['sa_wo'], 'L0_xattn_sa_bo': _L0_xattn_in['sa_bo'], 'L0_xattn_ca_wq': _L0_xattn_in['ca_wq'], 'L0_xattn_ca_bq': _L0_xattn_in['ca_bq'], 'L0_xattn_ca_wk': _L0_xattn_in['ca_wk'], 'L0_xattn_ca_bk': _L0_xattn_in['ca_bk'], 'L0_xattn_ca_wv': _L0_xattn_in['ca_wv'], 'L0_xattn_ca_bv': _L0_xattn_in['ca_bv'], 'L0_xattn_ca_wo': _L0_xattn_in['ca_wo'], 'L0_xattn_ca_bo': _L0_xattn_in['ca_bo'], 'L0_xattn_ln1_g': _L0_xattn_in['ln1_g'], 'L0_xattn_ln1_b': _L0_xattn_in['ln1_b'], 'L0_xattn_ln2_g': _L0_xattn_in['ln2_g'], 'L0_xattn_ln2_b': _L0_xattn_in['ln2_b'], 'L0_xattn_ln3_g': _L0_xattn_in['ln3_g'], 'L0_xattn_ln3_b': _L0_xattn_in['ln3_b'], 'L0_xattn_router_w': _L0_xattn_in['router_w'], 'L0_xattn_router_b': _L0_xattn_in['router_b'], 'L0_xattn_e_w1': _L0_xattn_in['e_w1'], 'L0_xattn_e_b1': _L0_xattn_in['e_b1'], 'L0_xattn_e_w2': _L0_xattn_in['e_w2'], 'L0_xattn_e_b2': _L0_xattn_in['e_b2']}

def reference(x, ctx_1024, L0_xattn_sa_wq, L0_xattn_sa_bq, L0_xattn_sa_wk, L0_xattn_sa_bk, L0_xattn_sa_wv, L0_xattn_sa_bv, L0_xattn_sa_wo, L0_xattn_sa_bo, L0_xattn_ca_wq, L0_xattn_ca_bq, L0_xattn_ca_wk, L0_xattn_ca_bk, L0_xattn_ca_wv, L0_xattn_ca_bv, L0_xattn_ca_wo, L0_xattn_ca_bo, L0_xattn_ln1_g, L0_xattn_ln1_b, L0_xattn_ln2_g, L0_xattn_ln2_b, L0_xattn_ln3_g, L0_xattn_ln3_b, L0_xattn_router_w, L0_xattn_router_b, L0_xattn_e_w1, L0_xattn_e_b1, L0_xattn_e_w2, L0_xattn_e_b2):
    import jax
    import jax.numpy as jnp

    def _L0_xattn_ref(x, encoder_output, sa_wq, sa_bq, sa_wk, sa_bk, sa_wv, sa_bv, sa_wo, sa_bo, ca_wq, ca_bq, ca_wk, ca_bk, ca_wv, ca_bv, ca_wo, ca_bo, ln1_g, ln1_b, ln2_g, ln2_b, ln3_g, ln3_b, router_w, router_b, e_w1, e_b1, e_w2, e_b2):
        import jax, jax.numpy as jnp
        import numpy as np
        B, S, SE, D, H, FF, E, K = (2, 512, 512, 256, 16, 1024, 8, 2)
        HD = D // H

        def _layernorm(x, g, b):
            m = x.mean(-1, keepdims=True)
            v = ((x - m) ** 2).mean(-1, keepdims=True)
            return (x - m) / jnp.sqrt(v + 1e-05) * g + b

        def _attn(q_in, k_in, v_in, wq, bq, wk, bk, wv, bv, wo, bo, causal):
            Bq, Sq, Dm = q_in.shape
            Sk = k_in.shape[1]
            Q = (q_in @ wq + bq).reshape(Bq, Sq, H, HD)
            Kp = (k_in @ wk + bk).reshape(Bq, Sk, H, HD)
            V = (v_in @ wv + bv).reshape(Bq, Sk, H, HD)
            scores = jnp.einsum('bqhd,bkhd->bhqk', Q, Kp) / jnp.sqrt(jnp.float32(HD))
            if causal:
                mask = jnp.tril(jnp.ones((Sq, Sk), bool))
                scores = jnp.where(mask, scores, -jnp.inf)
            a = jax.nn.softmax(scores, axis=-1)
            o = jnp.einsum('bhqk,bkhd->bqhd', a, V).reshape(Bq, Sq, Dm)
            return o @ wo + bo

        def _moe(x, rw, rb, w1, b1, w2, b2):
            T = x.shape[0] * x.shape[1]
            xf = x.reshape(T, D)
            router_weights = jax.nn.softmax(xf @ rw + rb, axis=-1)
            topw, topi = jax.lax.top_k(router_weights, K)
            topw = jax.nn.softmax(topw, axis=-1)
            combine = jnp.zeros((T, E), xf.dtype).at[jnp.arange(T)[:, None], topi].add(topw)
            h = jax.nn.gelu(jnp.einsum('td,edf->etf', xf, w1) + b1[:, None, :], approximate=False)
            eo = jnp.einsum('etf,efd->etd', h, w2) + b2[:, None, :]
            out = jnp.einsum('etd,te->td', eo, combine)
            return out.reshape(x.shape)
        x = _layernorm(x + _attn(x, x, x, sa_wq, sa_bq, sa_wk, sa_bk, sa_wv, sa_bv, sa_wo, sa_bo, True), ln1_g, ln1_b)
        x = _layernorm(x + _attn(x, encoder_output, encoder_output, ca_wq, ca_bq, ca_wk, ca_bk, ca_wv, ca_bv, ca_wo, ca_bo, False), ln2_g, ln2_b)
        x = _layernorm(x + _moe(x, router_w, router_b, e_w1, e_b1, e_w2, e_b2), ln3_g, ln3_b)
        return x
    x = _L0_xattn_ref(x, ctx_1024, L0_xattn_sa_wq, L0_xattn_sa_bq, L0_xattn_sa_wk, L0_xattn_sa_bk, L0_xattn_sa_wv, L0_xattn_sa_bv, L0_xattn_sa_wo, L0_xattn_sa_bo, L0_xattn_ca_wq, L0_xattn_ca_bq, L0_xattn_ca_wk, L0_xattn_ca_bk, L0_xattn_ca_wv, L0_xattn_ca_bv, L0_xattn_ca_wo, L0_xattn_ca_bo, L0_xattn_ln1_g, L0_xattn_ln1_b, L0_xattn_ln2_g, L0_xattn_ln2_b, L0_xattn_ln3_g, L0_xattn_ln3_b, L0_xattn_router_w, L0_xattn_router_b, L0_xattn_e_w1, L0_xattn_e_b1, L0_xattn_e_w2, L0_xattn_e_b2)
    return x

_drawn_inputs = setup_inputs


def setup_inputs(seed=0):
    import zlib

    import numpy as np

    out = dict(_drawn_inputs(seed))
    spreads = {'L0_xattn_sa_bq': (0.0, 0.8),
     'L0_xattn_sa_bk': (0.0, 0.8),
     'L0_xattn_sa_bv': (0.0, 0.1),
     'L0_xattn_sa_bo': (0.0, 0.1),
     'L0_xattn_ca_bq': (0.0, 0.8),
     'L0_xattn_ca_bk': (0.0, 0.8),
     'L0_xattn_ca_bv': (0.0, 0.1),
     'L0_xattn_ca_bo': (0.0, 0.1),
     'L0_xattn_ln1_g': (1.0, 0.2),
     'L0_xattn_ln1_b': (0.0, 0.1),
     'L0_xattn_ln2_g': (1.0, 0.2),
     'L0_xattn_ln2_b': (0.0, 0.1),
     'L0_xattn_ln3_g': (1.0, 0.2),
     'L0_xattn_ln3_b': (0.0, 0.1),
     'L0_xattn_router_b': (0.0, 0.1),
     'L0_xattn_e_b1': (0.0, 0.34),
     'L0_xattn_e_b2': (0.0, 0.1)}
    factors = {'L0_xattn_sa_wq': 8.0,
     'L0_xattn_sa_wk': 8.0,
     'L0_xattn_sa_wv': 4.821,
     'L0_xattn_ca_wq': 8.0,
     'L0_xattn_ca_wk': 8.0}
    for name, (base, spread) in spreads.items():
        noise = np.random.default_rng([zlib.crc32(name.encode()), seed]).standard_normal(out[name].shape)
        drawn = base * np.exp(spread * noise) if base else spread * noise
        out[name] = jnp.asarray(drawn.astype(out[name].dtype))
    for name, factor in factors.items():
        out[name] = (out[name] * factor).astype(out[name].dtype)
    return out
```

```python
from contextlib import ExitStack

import concourse.bass as bass
from concourse import mybir

P = 128
B, S, D = 2, 1024, 256
SE = 77
H, HD = 16, 16
E, FF = 8, 1024
EPS = 1e-5
KC = D // P
FC = FF // P
T = B * S
NT = T // P
TB = S // P
HH = P // HD
QUAD = 4
QG = 512
NG = S // QG
BANK = 512
VW = 2 * HD
Q_PART = (0, 0, 1, 1, 0, 2)
K_PART = (0, 1, 0, 1, 2, 0)
NGR = len(Q_PART)
R_S = NGR * HD
R_M = R_S + 3
NEG = -1e30
NSLOT = (2 * T + E * (P - 1)) // P
NPARAM = 10
MORE = 11776


class Mark:

    def __init__(self, sem, value):
        self.sem, self.value = sem, value


class Engine:

    def __init__(self, sem):
        self.sem, self.count, self.queue, self.waited = sem, 0, [], {}

    def wait(self, *marks):
        for m in marks:
            if m is not None and self.waited.get(id(m.sem), 0) < m.value:
                self.waited[id(m.sem)] = m.value
                self.queue.append((lambda e, m=m: e.wait_ge(m.sem, m.value), None, 0))

    def do(self, call, *after):
        self.wait(*after)
        self.queue.append((call, None, 0))

    def mark(self, call, *after):
        self.wait(*after)
        self.count += 1
        self.queue.append((call, self.sem, 1))
        return Mark(self.sem, self.count)

    def dma(self, call, stream, *after):
        self.wait(*after)
        stream.count += 16
        self.queue.append((call, stream.sem, 16))
        return Mark(stream.sem, stream.count)

    def run(self, e):
        for call, sem, inc in self.queue:
            made = call(e)
            if sem is not None:
                made.then_inc(sem, inc)


class Stream:

    def __init__(self, sem):
        self.sem, self.count = sem, 0


class Ring:

    def __init__(self, buffers):
        self.buffers, self.free, self.at = buffers, [()] * len(buffers), -1

    def next(self):
        self.at = (self.at + 1) % len(self.buffers)
        free, self.free[self.at] = self.free[self.at], None
        assert free is not None, "a buffer is taken again before it was given back"
        return self.at, self.buffers[self.at], free

    def release(self, i, *marks):
        self.free[i] = marks


def interleave(main, side):
    done = 0
    for i, step in enumerate(main):
        step()
        while done < len(side) * (i + 1) // len(main):
            side[done]()
            done += 1
    for step in side[done:]:
        step()


def build(nc, x, ctx_in, par, wts, router_w, w1, b1, w2, b2, out):
    f32, bf16, i32, u32 = mybir.dt.float32, mybir.dt.bfloat16, mybir.dt.int32, mybir.dt.uint32
    ALU, ACT, AX = mybir.AluOpType, mybir.ActivationFunctionType, mybir.AxisListType
    stack = ExitStack()
    with stack:
        def sb(name, shape, dt=f32):
            return stack.enter_context(nc.sbuf_tensor(name, shape, dt))

        n_sem = [0]

        def stream(name):
            n_sem[0] += 1
            return Stream(stack.enter_context(nc.semaphore(f"dma_{name}_{n_sem[0]}")))

        PE, ACTE, DVE, POOL, SP = (Engine(stack.enter_context(nc.semaphore(f"done_{n}")))
                                   for n in ("pe", "act", "dve", "pool", "sp"))

        parts_d = nc.dram_tensor("parts_scratch", [2 * B * (H // HH), 2, 3, P, S], bf16, kind="Internal").ap()
        negm_d = nc.dram_tensor("negmax_scratch", [2 * B * (H // HH), 3, HH, S], bf16, kind="Internal").ap()
        xs_d = nc.dram_tensor("slot_in_scratch", [NSLOT * P, D], f32, kind="Internal").ap()
        ys_d = nc.dram_tensor("slot_out_scratch", [NSLOT * P, D], f32, kind="Internal").ap()

        res = sb("residual", [P, NT, D])
        param = sb("param_rows", [P, NPARAM, D])
        ident = sb("ident", [P, P])
        identb = sb("identb", [P, P], bf16)
        mask_qk = sb("mask_qk", [P, P], bf16)
        b_qk = sb("b_qk", [P, 2, 2, KC])
        rbias = sb("router_bias", [P, E])
        rw = sb("router_w", [P, KC, E])
        epsc = sb("eps", [P, 1])
        stat = sb("stat", [P, 2, 6])
        mv = sb("mean_var", [P, NT, 2])
        rstd = sb("rstd", [P, NT])
        sdev = sb("sdev", [P, NT])
        pm = sb("part_max", [P, TB, HH, 2])
        negm = sb("neg_max", [P, TB, HH])
        negp = sb("neg_max_parts", [P, TB, 3, HH], bf16)
        negr = sb("neg_max_rest", [P, TB, HH])
        rsum = sb("recip_sum", [P, 2, QUAD, QUAD])
        (A_BV, A_BO, C_BV, C_BO, G1, B1N, G2, B2N, G3, B3N) = range(NPARAM)

        W_WORDS = 2 * E * KC * FF
        arena = sb("arena", [P, W_WORDS])
        more = sb("arena_more", [P, MORE])
        at = {"arena": 0, "more": 0}

        def cut(where, words):
            a = at[where]
            at[where] += words
            whole = arena if where == "arena" else more
            assert at[where] <= whole.shape[1], (where, at[where])
            return whole[:, a:a + words]

        def cut_bf(where, n):
            return cut(where, n // 2).bitcast(bf16)

        w1_sb = arena[:, 0:W_WORDS // 2]
        w2_sb = arena[:, W_WORDS // 2:W_WORDS]
        EW = KC * FF
        ka = [cut_bf("arena", HH * S).rearrange("p (h t) -> p h t", h=HH) for _ in range(2)]
        va = [cut("arena", TB * HH * VW).rearrange("p (k h v) -> p k h v", k=TB, h=HH) for _ in range(2)]
        w_self = [cut("arena", KC * D).rearrange("p (c n) -> p c n", c=KC) for _ in range(4)]
        qa = [cut_bf("arena", HH * S).rearrange("p (h t) -> p h t", h=HH) for _ in range(2)]
        w_cross = [cut("arena", KC * D).rearrange("p (c n) -> p c n", c=KC) for _ in range(4)]
        kac = [cut_bf("arena", HH * 80).rearrange("p (h t) -> p h t", h=HH) for _ in range(2)]
        vac = [cut("arena", HH * VW).rearrange("p (h v) -> p h v", h=HH) for _ in range(2)]
        ctxT = cut("arena", B * KC * SE).rearrange("p (b c n) -> p b c n", b=B, c=KC)
        ot = [cut("arena", QG) for _ in range(2)]
        ctxn = ot[0].rearrange("p (b n) -> p b n", b=B)
        onT = [cut("arena", D).rearrange("p (c n) -> p c n", c=KC) for _ in range(2)]
        xT = cut("more", KC * T // 2).rearrange("p (c n) -> p c n", c=KC)
        pt = [cut("arena", 2 * QG).rearrange("p (j q) -> p j q", j=2) for _ in range(4)]
        onat = [cut("more", TB * D).rearrange("p (t n) -> p t n", t=TB) for _ in range(2)]
        f_sb = [cut("arena", S)]
        part_sb = [[cut_bf("more", S) for _ in range(3)] for _ in range(2)]
        mT = cut_bf("more", S)
        y_sb = [cut("more", D) for _ in range(2)]
        at["more"] = 0
        slot_x = [cut("more", D) for _ in range(3)]
        slot_xT = [cut("more", D).rearrange("p (c n) -> p c n", c=KC) for _ in range(2)]
        bias12 = [cut("more", FF + D) for _ in range(3)]
        hid = [cut("more", FF) for _ in range(2)]
        act = [cut("more", FF) for _ in range(2)]
        hidT = [cut("more", FF).rearrange("p (c n) -> p c n", c=FC) for _ in range(1)]
        slot_y = [cut("more", D) for _ in range(2)]
        gath = [cut("more", 2 * D).rearrange("p (k n) -> p k n", k=2) for _ in range(2)]

        st2 = [stack.enter_context(nc.psum_tensor(f"score_pair{i}", [P, 2, BANK], f32)) for i in range(2)]
        o_ps = stack.enter_context(nc.psum_tensor("out_acc", [P, BANK], f32))
        work = [stack.enter_context(nc.psum_tensor(f"work{i}", [P, BANK], f32))[:, :] for i in range(3)]
        banks = Ring(work)
        pairs = Ring(st2)
        o_free = [()]

        s_x = [stream("x") for _ in range(B)]
        x_in = [SP.dma(lambda e, b=b: e.dma_start(res[:, b * TB:(b + 1) * TB, :],
                                                  x[b].rearrange("(t p) n -> p t n", p=P)), s_x[b])
                for b in range(B)]
        s_w = stream("w_self")
        for i in range(4):
            w_in = ACTE.dma(lambda e, i=i: e.dma_start(w_self[i], wts[i].rearrange("(c p) n -> p c n", p=P)), s_w)
        s_bc = stream("bias_cols")
        for a in range(2):
            for i in range(2):
                bc_in = SP.dma(lambda e, a=a, i=i: e.dma_start(
                    b_qk[:, a, i, :], par[("bq", "bk")[i]][a].rearrange("(c p) -> p c", p=P),
                    allow_slow_non_contiguous=True), s_bc)
        s_pr = stream("params")
        for i, row in enumerate(par["rows"]):
            par_in = SP.dma(lambda e, i=i, row=row: e.dma_start(
                param[:, i, :], row.rearrange("(o n) -> o n", o=1).to_broadcast([P, D])), s_pr)
        par_in = SP.dma(lambda e: e.dma_start(
            rbias[:, :], par["rb"].rearrange("(o n) -> o n", o=1).to_broadcast([P, E])), s_pr)
        s_wc = stream("w_cross")
        for i in range(4):
            wc_in = ACTE.dma(lambda e, i=i: e.dma_start(w_cross[i], wts[4 + i].rearrange("(c p) n -> p c n", p=P)), s_wc)
        wc_in = ACTE.dma(lambda e: e.dma_start(rw[:, :, :], router_w.rearrange("(c p) n -> p c n", p=P)), s_wc)
        wc_in = ACTE.dma(lambda e: e.dma_start(ctxn[0:SE, :, :], ctx_in.rearrange("b s n -> s b n")), s_wc)

        c0 = DVE.mark(lambda e: e.memset(ident[:, :], 0.0))
        c1 = DVE.mark(lambda e: e.memset(mask_qk[:, :], 0.0))
        id_ok = POOL.mark(lambda e: e.affine_select(
            out=ident[:, :], in_=ident[:, :], compare_op=ALU.not_equal, fill=1.0, base=0,
            pattern=[[-1, P]], channel_multiplier=1), c0)
        mask_ok = POOL.mark(lambda e: e.affine_select(
            out=mask_qk[:, :], in_=mask_qk[:, :], compare_op=ALU.is_ge, fill=NEG, base=0,
            pattern=[[-1, P]], channel_multiplier=1), c1)
        idb_ok = DVE.mark(lambda e: e.tensor_copy(identb[:, :], ident[:, :]), id_ok)
        DVE.do(lambda e: e.memset(epsc[:, :], EPS))
        DVE.do(lambda e: e.memset(pm[:, 0:TB // 2, :, 1:2], NEG))
        for i in range(2):
            DVE.do(lambda e, i=i: e.memset(ka[i][R_S:R_M, :, :], 1.0))
            DVE.do(lambda e, i=i: e.memset(kac[i][R_S:R_M, :, 0:SE], 1.0))
            DVE.do(lambda e, i=i: e.memset(vac[i][:, :, HD:VW], 1.0))
            const_ok = DVE.mark(lambda e, i=i: e.memset(va[i][:, :, :, HD:VW], 1.0))
        POOL.do(lambda e: e.memset(y_sb[0], 0.0))
        zero_ok = POOL.mark(lambda e: e.memset(y_sb[1], 0.0))
        s_z = stream("zero")
        for j in range(NSLOT):
            zeros_in = POOL.dma(lambda e, j=j: e.dma_start(xs_d[j * P:(j + 1) * P, :], y_sb[j % 2]), s_z, zero_ok)

        x_t_free = [()]

        def transpose_tile(t, ready, dst, free, evac):
            i, bank, bfree = banks.next()
            PE.wait(ready, id_ok, *bfree)
            for c in range(KC):
                m = (PE.mark if c == KC - 1 else PE.do)(lambda e, c=c, bank=bank: e.transpose(
                    bank[:, c * P:(c + 1) * P], res[:, t, c * P:(c + 1) * P], ident[:, :]))
            src = bank[:, 0:D].rearrange("p (c n) -> p c n", c=KC)
            if evac is ACTE:
                done = ACTE.mark(lambda e: e.copy(dst, src), m, *free)
            else:
                done = DVE.mark(lambda e: e.tensor_copy(dst, src), m, *free)
            banks.release(i, done)
            return done

        def x_t_steps(b, ready, say):
            def step(t):
                say[t] = transpose_tile(b * TB + t, ready[t], xT[:, :, t * P:(t + 1) * P],
                                        x_t_free[0], ACTE if t % 2 else DVE)
            return [lambda t=t: step(t) for t in range(TB)]

        f_ring, part_ring = Ring(f_sb), Ring(part_sb)
        slot_free = {"qa": [(), ()], "ka": [(), ()], "va": [(), ()], "kac": [(), ()], "vac": [(), ()]}
        mT_free, pm_free, negp_free = [()], [()], [()]
        s_part = {}

        class Stage:
            def __init__(self, n, cross, b, hh):
                self.n, self.cross, self.b, self.hh, self.slot = n, cross, b, hh, n % 2
                self.keys = SE if cross else S
                self.ka = (kac if cross else ka)[self.slot]
                self.qa = qa[self.slot]
                self.va_ok = self.q_ok = self.k_ok = self.m_ok = ()

        def project_steps(st, which, src, n_tok, src_ok, weights, w_ok):
            box = {}

            def make(n0):
                if n0 == 0:
                    box["f"] = f_ring.next()
                fi, f, ffree = box["f"]
                w = min(BANK, n_tok - n0)
                i, bank, bfree = banks.next()
                PE.wait(w_ok, *bfree)
                for m in src_ok(n0, w):
                    PE.wait(m)
                for c in range(KC):
                    m = (PE.mark if c == KC - 1 else PE.do)(lambda e, c=c: e.matmul(
                        bank[:, 0:w], weights[:, c, st.hh * P:(st.hh + 1) * P], src(c, n0, w),
                        start=(c == 0), stop=(c == KC - 1)))
                if which == 0:
                    x_t_free[0] = x_t_free[0] + (m,)
                box["made"] = ACTE.mark(lambda e: e.activation(
                    f[:, n0:n0 + w], bank[:, 0:w], ACT.Identity,
                    bias=b_qk[:, int(st.cross), which, st.hh:st.hh + 1]), m, bc_in, *ffree)
                banks.release(i, box["made"])

            def split():
                fi, f, _ = box["f"]
                pi, part, pfree = part_ring.next()
                a, p = f[:, 0:n_tok], [q[:, 0:n_tok] for q in part]
                POOL.wait(box["made"], *pfree)
                m = POOL.mark(lambda e: e.tensor_copy(p[0], a))
                m = POOL.mark(lambda e: e.tensor_tensor(a, a, p[0], ALU.subtract), m)
                m = POOL.mark(lambda e: e.tensor_copy(p[1], a), m)
                m = POOL.mark(lambda e: e.tensor_tensor(p[2], a, p[1], ALU.subtract), m)
                f_ring.release(fi, m)
                out_s = s_part.setdefault(("out", pi), stream("parts_out"))
                for k in range(3):
                    stored = SP.dma(lambda e, k=k: e.dma_start(parts_d[st.n, which, k, :, 0:n_tok], p[k]),
                                    out_s, m)
                part_ring.release(pi, stored)
                into = (st.qa, st.ka)[which]
                key = "qa" if which == 0 else ("kac" if st.cross else "ka")
                in_s = s_part.setdefault((key, st.slot), stream(f"{key}_in"))
                for g in range(NGR):
                    loaded = SP.dma(lambda e, g=g: e.dma_start(
                        into[g * HD:(g + 1) * HD, :, 0:n_tok],
                        parts_d[st.n, which, (Q_PART, K_PART)[which][g], :, 0:n_tok]
                        .rearrange("(h d) t -> d h t", d=HD)), in_s, stored, *slot_free[key][st.slot])
                if which == 0:
                    st.q_ok = (loaded,)
                else:
                    st.k_ok = (loaded, const_ok)

            return [lambda n0=n0: make(n0) for n0 in range(0, n_tok, BANK)] + [split]

        def v_steps(st, src, src_ok, weights, w_ok, row):
            def make(k0):
                i, bank, bfree = banks.next()
                nk = 1 if st.cross else 4
                rows = SE if st.cross else P
                PE.wait(w_ok, *bfree)
                for k in range(nk):
                    for mk in src_ok((k0 + k) * P, rows):
                        PE.wait(mk)
                    for c in range(KC):
                        m = (PE.mark if k == nk - 1 and c == KC - 1 else PE.do)(lambda e, k=k, c=c: e.matmul(
                            bank[0:rows, k * P:(k + 1) * P], src(c, (k0 + k) * P, rows),
                            weights[:, c, st.hh * P:(st.hh + 1) * P], start=(c == 0), stop=(c == KC - 1)))
                if not st.cross:
                    x_t_free[0] = x_t_free[0] + (m,)
                bias = param[0:rows, row, st.hh * P:(st.hh + 1) * P].rearrange("p (h d) -> p h d", h=HH)
                key = "vac" if st.cross else "va"
                DVE.wait(m, par_in, *slot_free[key][st.slot])
                for k in range(nk):
                    to = vac[st.slot][0:rows, :, 0:HD] if st.cross else va[st.slot][:, k0 + k, :, 0:HD]
                    frm = bank[0:rows, k * P:(k + 1) * P].rearrange("p (h d) -> p h d", h=HH)
                    d = DVE.mark(lambda e, to=to, frm=frm: e.tensor_tensor(to, frm, bias, ALU.add))
                banks.release(i, d)
                st.va_ok = (d, const_ok)
            return [lambda k0=k0: make(k0) for k0 in range(0, 1 if st.cross else TB, 4)]

        def max_steps(st):
            box = {}

            def item(qb, c, w, h0, nh, diagonal):
                i, bank, bfree = banks.next()
                PE.wait(*st.q_ok, *st.k_ok, *bfree, mask_ok, idb_ok)
                for j in range(nh):
                    h = h0 + j
                    m = (PE.mark if j == nh - 1 and not diagonal else PE.do)(lambda e, h=h, j=j: e.matmul(
                        bank[:, j * w:(j + 1) * w], st.qa[0:R_S, h, qb * P:(qb + 1) * P],
                        st.ka[0:R_S, h, c * BANK:c * BANK + w], start=True, stop=not diagonal))
                    if diagonal:
                        m = (PE.mark if j == nh - 1 else PE.do)(lambda e, j=j: e.matmul(
                            bank[:, (j + 1) * w - P:(j + 1) * w], identb[:, :], mask_qk[:, :],
                            start=False, stop=True))
                src = bank[:, 0:nh * w].rearrange("p (j k) -> p j k", j=nh)
                r = DVE.mark(lambda e: e.tensor_reduce(pm[:, qb, h0:h0 + nh, c], src, AX.X, ALU.max),
                             m, *pm_free[0])
                banks.release(i, r)
                box["r"] = r

            def gather():
                flat = negm[:, :, :].rearrange("p t h -> p (t h)")
                if st.cross:
                    m = DVE.mark(lambda e: e.tensor_scalar(
                        negm[:, :, :], pm[:, :, :, 0], -1.0, None, ALU.mult), box["r"])
                else:
                    m = DVE.mark(lambda e: e.tensor_reduce(
                        negm[:, :, :], pm[:, :, :, :], AX.X, ALU.max, negate=True), box["r"])
                pm_free[0] = (m,)
                p = [negp[:, :, k, :] for k in range(3)]
                m = DVE.mark(lambda e: e.tensor_copy(p[0], negm[:, :, :]), m, *negp_free[0])
                m = DVE.mark(lambda e: e.tensor_tensor(negr[:, :, :], negm[:, :, :], p[0], ALU.subtract), m)
                m = DVE.mark(lambda e: e.tensor_copy(p[1], negr[:, :, :]), m)
                m = DVE.mark(lambda e: e.tensor_tensor(p[2], negr[:, :, :], p[1], ALU.subtract), m)
                i, bank, bfree = banks.next()
                rows = bank[0:3 * HH, :].bitcast(bf16)
                PE.wait(m, idb_ok, *bfree)
                for t in range(TB):
                    t_m = (PE.mark if t == TB - 1 else PE.do)(lambda e, t=t: e.transpose(
                        rows[:, t * P:(t + 1) * P], negp[:, t, :, :].rearrange("p k h -> p (k h)"), identb[:, :]))
                negp_free[0] = (t_m,)
                m = ACTE.mark(lambda e: e.copy(mT[0:3 * HH, :], rows), t_m, *mT_free[0])
                banks.release(i, m)
                s = s_part.setdefault(("negm", 0), stream("negm_out"))
                stored = SP.dma(lambda e: e.dma_start(
                    negm_d[st.n].rearrange("k h t -> (k h) t"), mT[0:3 * HH, :]), s, m)
                mT_free[0] = (stored,)
                s2 = s_part.setdefault(("negm_in", st.slot), stream("negm_in"))
                st.m_ok = (SP.dma(lambda e: e.dma_start(st.qa[R_S:R_M, :, :], negm_d[st.n]), s2, stored,
                                  *slot_free["qa"][st.slot]),)

            steps = []
            for qb in range(TB):
                if st.cross:
                    steps += [lambda qb=qb, h0=h0: item(qb, 0, SE, h0, HH // 2, False)
                              for h0 in range(0, HH, HH // 2)]
                    continue
                keys = (qb + 1) * P
                for c in range((keys + BANK - 1) // BANK):
                    w = min(BANK, keys - c * BANK)
                    nh = BANK // w
                    last = (c + 1) * BANK >= keys
                    steps += [lambda qb=qb, c=c, w=w, h0=h0, nh=nh, last=last: item(qb, c, w, h0, nh, last)
                              for h0 in range(0, HH, nh)]
            return steps + [gather]

        pt_ring, ot_ring = Ring(pt), Ring(ot)
        rs_ring = Ring([rsum[:, i] for i in range(2)])
        onat_ok = {}
        onat_free = [(), ()]

        def attend_steps(st):
            steps, pending, box = [], [], {}
            nkb = lambda g: 1 if st.cross else (g + 1) * (QG // P)

            def score(g, quad, kb, pair):
                rows = SE if st.cross else P
                skip = 0 if st.cross else max(0, kb * P - g * QG)
                w = QG - skip
                i, ps, free = pairs.next()
                PE.wait(*st.q_ok, *st.k_ok, *st.m_ok, *free)
                diagonal = not st.cross and kb * P >= g * QG
                for j in range(2):
                    h = quad * QUAD + pair * 2 + j
                    k0 = 0 if st.cross else kb * P
                    m = (PE.mark if j == 1 and not diagonal else PE.do)(lambda e, h=h, j=j, k0=k0: e.matmul(
                        ps[0:rows, j, 0:w], st.ka[0:R_M, h, k0:k0 + rows],
                        st.qa[0:R_M, h, g * QG + skip:(g + 1) * QG], start=True, stop=not diagonal))
                    if diagonal:
                        m = (PE.mark if j == 1 else PE.do)(lambda e, j=j: e.matmul(
                            ps[:, j, 0:P], mask_qk[:, :], identb[:, :], start=False, stop=True))
                pi, prob, pfree = pt_ring.next()
                x_ok = ACTE.mark(lambda e: e.activation(
                    prob[0:rows, :, 0:w], ps[0:rows, :, 0:w], ACT.Exp, scale=float(HD) ** -0.5), m, *pfree)
                pairs.release(i, x_ok)
                pending.append((pi, prob, x_ok, rows, skip, w))

            def weigh(g, quad, kb):
                first, last = kb == 0, kb == nkb(g) - 1
                PE.wait(*st.va_ok, *(o_free[0] if first else ()))
                for pair in range(2):
                    pi, prob, x_ok, rows, skip, w = pending.pop(0)
                    PE.wait(x_ok)
                    for j in range(2):
                        c = pair * 2 + j
                        h = quad * QUAD + c
                        v = vac[st.slot][0:rows, h, :] if st.cross else va[st.slot][:, kb, h, :]
                        m = (PE.mark if j == 1 else PE.do)(lambda e, c=c, v=v, prob=prob, rows=rows, j=j, w=w, skip=skip: e.matmul(
                            o_ps[c * VW:(c + 1) * VW, skip:QG], v, prob[0:rows, j, 0:w], start=first, stop=last))
                    pt_ring.release(pi, m)
                box["pv"] = m

            def normalise(g, quad):
                oi, o, ofree = ot_ring.next()
                if (g + quad) % 2:
                    cp = ACTE.mark(lambda e: e.copy(o, o_ps[:, :]), box["pv"], *ofree)
                else:
                    cp = DVE.mark(lambda e: e.tensor_copy(o, o_ps[:, :]), box["pv"], *ofree)
                o_free[0] = (cp,)
                box[g, quad] = (oi, o, cp)

            def divide(g, quad):
                oi, o, cp = box[g, quad]
                i, bank, bfree = banks.next()
                PE.wait(cp, *bfree)
                for q in range(QG // P):
                    m = (PE.mark if q == QG // P - 1 else PE.do)(lambda e, q=q: e.transpose(
                        bank[:, q * P:(q + 1) * P], o[:, q * P:(q + 1) * P], ident[:, :]))
                ot_ring.release(oi, m)
                view = bank[:, :].rearrange("p (q c v) -> p q c v", q=QG // P, c=QUAD)
                ri, rs_, rfree = rs_ring.next()
                r = DVE.mark(lambda e: e.reciprocal(rs_, view[:, :, :, HD]), m, *rfree)
                col = st.hh * P + quad * QUAD * HD
                DVE.wait(r, *onat_free[st.b])
                for q in range(QG // P):
                    d = DVE.mark(lambda e, q=q: e.tensor_tensor(
                        onat[st.b][:, g * (QG // P) + q, col:col + QUAD * HD].rearrange("p (c d) -> p c d", c=QUAD),
                        view[:, q, :, 0:HD],
                        rs_[:, q, :].rearrange("p (c o) -> p c o", o=1).to_broadcast([P, QUAD, HD]), ALU.mult))
                banks.release(i, d)
                rs_ring.release(ri, d)
                onat_ok[st.b] = d

            order = [(g, quad, kb) for g in range(NG) for quad in range(HH // QUAD) for kb in range(nkb(g))]
            late = []
            for n, (g, quad, kb) in enumerate(order):
                steps.append(lambda g=g, quad=quad, kb=kb: score(g, quad, kb, 0))
                steps.append(lambda g=g, quad=quad, kb=kb: score(g, quad, kb, 1))
                steps += late
                late = [lambda g=g, quad=quad, kb=kb: weigh(g, quad, kb)]
                if kb == nkb(g) - 1:
                    late += [lambda g=g, quad=quad: normalise(g, quad), lambda g=g, quad=quad: divide(g, quad)]
            steps += late

            def close():
                slot_free["qa"][st.slot] = (box["pv"],)
                for k in (("kac", "vac") if st.cross else ("ka", "va")):
                    slot_free[k][st.slot] = (box["pv"],)
            return steps + [close]

        onT_ring, y_ring = Ring(onT), Ring(y_sb)

        stat_free = [(), ()]

        def norm_stats(t, src, ready, k):
            m = DVE.mark(lambda e: e.bn_stats(stat[:, k, :], src), ready, *stat_free[k])
            m = DVE.mark(lambda e: e.bn_aggr(mv[:, t, :], stat[:, k, :]), m)
            stat_free[k] = (m,)
            return m

        def norm_scale(t0, n, ready):
            m = ACTE.mark(lambda e: e.activation(sdev[:, t0:t0 + n], mv[:, t0:t0 + n, 1], ACT.Sqrt,
                                                 bias=epsc[:, 0:1]), ready, const_ok)
            return DVE.mark(lambda e: e.reciprocal(rstd[:, t0:t0 + n], sdev[:, t0:t0 + n]), m)

        def norm_apply(t, scaled, g, b, dst=None):
            src = res[:, t, :]
            dst = src if dst is None else dst
            m = DVE.mark(lambda e: e.tensor_scalar(src, src, mv[:, t, 0:1], rstd[:, t:t + 1],
                                                   ALU.subtract, ALU.mult), scaled)
            m = POOL.mark(lambda e: e.tensor_tensor(src, src, param[:, g, :], ALU.mult), m, par_in)
            return POOL.mark(lambda e: e.tensor_tensor(dst, src, param[:, b, :], ALU.add), m)

        def project_out_steps(b, w_o, w_ok, bo, g, bn, say):
            box = {}

            def tile(t):
                tt = b * TB + t
                m_b = POOL.mark(lambda e: e.tensor_tensor(res[:, tt, :], res[:, tt, :], param[:, bo, :], ALU.add),
                                par_in, *x_t_src_free[b])
                i, bank, bfree = banks.next()
                PE.wait(onat_ok[b], *bfree)
                for c in range(KC):
                    m = (PE.mark if c == KC - 1 else PE.do)(lambda e, c=c: e.transpose(
                        bank[:, c * P:(c + 1) * P], onat[b][:, t, c * P:(c + 1) * P], ident[:, :]))
                onat_free[b] = (m,)
                oi, o, ofree = onT_ring.next()
                cp = ACTE.mark(lambda e: e.copy(o, bank[:, 0:D].rearrange("p (c n) -> p c n", c=KC)), m, *ofree)
                banks.release(i, cp)
                i, bank2, bfree = banks.next()
                PE.wait(cp, w_ok, *bfree)
                for c in range(KC):
                    m = (PE.mark if c == KC - 1 else PE.do)(lambda e, c=c: e.matmul(
                        bank2[:, 0:D], o[:, c, :], w_o[:, c, :], start=(c == 0), stop=(c == KC - 1)))
                onT_ring.release(oi, m)
                s = DVE.mark(lambda e: e.tensor_tensor(res[:, tt, :], bank2[:, 0:D], res[:, tt, :], ALU.add), m, m_b)
                banks.release(i, s)
                box["s"] = norm_stats(tt, res[:, tt, :], s, t % 2)

            def scale():
                box["r"] = norm_scale(b * TB, TB, box["s"])

            def apply(t):
                say[t] = norm_apply(b * TB + t, box["r"], g, bn)

            return ([lambda t=t: tile(t) for t in range(TB)] + [scale]
                    + [lambda t=t: apply(t) for t in range(TB)])

        x_t_src_free = {}
        xt_ok = {}

        def self_prep(st, first):
            steps = []
            if first:
                say = [None] * TB
                xt_ok[st.b] = say
                steps += x_t_steps(st.b, [x_in[st.b]] * TB, say)

                def note():
                    x_t_src_free[st.b] = tuple(say)
                    x_t_free[0] = ()
                steps.append(note)
            src = lambda c, n0, w: xT[:, c, n0:n0 + w]
            ok = lambda n0, w: xt_ok[st.b][n0 // P:(n0 + w) // P]
            steps += project_steps(st, 0, src, S, ok, w_self[0], w_in)
            steps += project_steps(st, 1, src, S, ok, w_self[1], w_in)
            steps += v_steps(st, src, ok, w_self[2], w_in, A_BV)
            return steps + max_steps(st)

        ctx_ok = []

        def ctx_steps():
            def step(b):
                i, bank, bfree = banks.next()
                PE.wait(wc_in, id_ok, *bfree)
                for c in range(KC):
                    m = (PE.mark if c == KC - 1 else PE.do)(lambda e, c=c: e.transpose(
                        bank[:, c * P:c * P + SE], ctxn[0:SE, b, c * P:(c + 1) * P], ident[0:SE, 0:SE]))
                d = DVE.mark(lambda e: e.tensor_copy(
                    ctxT[:, b, :, :], bank[:, 0:KC * P].rearrange("p (c n) -> p c n", c=KC)[:, :, 0:SE]), m)
                banks.release(i, d)
                ctx_ok.append(d)
                ot_ring.release(0, d)
            return [lambda b=b: step(b) for b in range(B)]

        def cross_prep(st, first, norm_say):
            steps = []
            csrc = lambda c, n0, w: ctxT[:, st.b, c, n0:n0 + w]
            cok = lambda n0, w: ctx_ok
            steps += project_steps(st, 1, csrc, SE, cok, w_cross[1], wc_in)
            steps += v_steps(st, csrc, cok, w_cross[2], wc_in, C_BV)
            if first:
                say = [None] * TB
                xt_ok[st.b] = say
                steps += x_t_steps(st.b, norm_say, say)

                def note():
                    x_t_src_free[st.b] = tuple(say)
                    x_t_free[0] = ()
                steps.append(note)
            src = lambda c, n0, w: xT[:, c, n0:n0 + w]
            ok = lambda n0, w: xt_ok[st.b][n0 // P:(n0 + w) // P]
            steps += project_steps(st, 0, src, S, ok, w_cross[0], wc_in)
            return steps + max_steps(st)

        stages = [Stage(n, n >= 4, (n // 2) % 2, n % 2) for n in range(8)]
        norm1 = [[None] * TB for _ in range(B)]
        norm2 = [[None] * TB for _ in range(B)]
        out1 = lambda b: project_out_steps(b, w_self[3], w_in, A_BO, G1, B1N, norm1[b])
        out2 = lambda b: project_out_steps(b, w_cross[3], wc_in, C_BO, G2, B2N, norm2[b])
        for s in self_prep(stages[0], True) + ctx_steps():
            s()
        interleave(attend_steps(stages[0]), self_prep(stages[1], False))
        interleave(attend_steps(stages[1]), self_prep(stages[2], True))
        interleave(attend_steps(stages[2]), out1(0) + self_prep(stages[3], False))
        interleave(attend_steps(stages[3]), cross_prep(stages[4], True, norm1[0]))
        self_done = Mark(PE.sem, PE.count)
        interleave(attend_steps(stages[4]), cross_prep(stages[5], False, None) + out1(1))
        self_w_done = Mark(PE.sem, PE.count)
        s_e = stream("w1_early")
        early = 2 * (HH * S // 2 + TB * HH * VW) // EW
        w1_v = w1.rearrange("e (c p) f -> p e c f", p=P)
        w2_v = w2.rearrange("e (c p) n -> p e c n", p=P)
        w1_s = w1_sb.rearrange("p (e c f) -> p e c f", e=E, c=KC)
        w2_s = w2_sb.rearrange("p (e c n) -> p e c n", e=E, c=FC)
        for ex in range(early):
            early_in = SP.dma(lambda e, ex=ex: e.dma_start(w1_s[:, ex], w1_v[:, ex]), s_e, self_w_done)
        interleave(attend_steps(stages[5]), cross_prep(stages[6], True, norm1[1]))
        interleave(attend_steps(stages[6]), out2(0) + cross_prep(stages[7], False, None))
        for s in attend_steps(stages[7]) + out2(1):
            s()

        x2_ring = onT_ring
        i_l, logit_ps, lfree = banks.next()
        tbanks = Ring([b for b in work if b is not logit_ps])
        tbanks.free = [banks.free[work.index(b)] for b in tbanks.buffers]
        for t in range(NT):
            i, bank, bfree = tbanks.next()
            PE.wait(norm2[t // TB][t % TB], *bfree)
            for c in range(KC):
                m = (PE.mark if c == KC - 1 else PE.do)(lambda e, c=c, bank=bank, t=t: e.transpose(
                    bank[:, c * P:(c + 1) * P], res[:, t, c * P:(c + 1) * P], ident[:, :]))
            xi, xt, xfree = x2_ring.next()
            cp = ACTE.mark(lambda e, xt=xt, bank=bank: e.copy(xt, bank[:, 0:D].rearrange("p (c n) -> p c n", c=KC)),
                           m, *xfree)
            tbanks.release(i, cp)
            PE.wait(cp, wc_in, *lfree)
            for c in range(KC):
                m = (PE.mark if c == KC - 1 else PE.do)(lambda e, c=c, xt=xt, t=t: e.matmul(
                    logit_ps[:, t * E:(t + 1) * E], xt[:, c, :], rw[:, c, :], start=(c == 0), stop=(c == KC - 1)))
            x2_ring.release(xi, m)
        logits_ok = m
        attention_done = m

        s_l = stream("w_late")
        for ex in range(early, E):
            late_in = SP.dma(lambda e, ex=ex: e.dma_start(w1_s[:, ex], w1_v[:, ex]), s_l, attention_done, cp)
        for ex in range(E):
            late_in = SP.dma(lambda e, ex=ex: e.dma_start(w2_s[:, ex], w2_v[:, ex]), s_l)

        NE = NT * E
        spare = [2 * D * len(gath), MORE - 2 * D * len(gath)]

        def table(n, dt=f32):
            spare[0] -= n
            a = spare[1]
            spare[1] += n
            assert spare[0] >= 0
            return more[:, a:a + n].bitcast(dt)

        lg = table(NE).rearrange("p (t e) -> p t e", t=NT)
        top = table(NE).rearrange("p (t e) -> p t e", t=NT)
        topi = table(NE, u32).rearrange("p (t e) -> p t e", t=NT)
        ex_l = table(NE).rearrange("p (t e) -> p t e", t=NT)
        oh = table(2 * NE).rearrange("p (k t e) -> p k t e", k=2, t=NT)
        tri, ones = table(P), table(P)
        topf = sb("top_index_f", [P, NT, 2])
        pr = sb("top_prob", [P, NT, 2])
        rs = sb("prob_recip", [P, NT])
        dw = sb("weight_tmp", [P, NT])
        wgt = sb("combine", [P, 2, NT])
        iota_e = sb("iota_e", [P, E])
        cnt = sb("tile_counts", [P, NT + 1, E])
        rank = sb("rank", [P, NT, E])
        tmp = sb("rank_tmp", [P, NT, E])
        ntot = sb("n_expert", [P, E])
        ntile = sb("tiles_expert", [P, E], i32)
        ntile_f = sb("tiles_expert_f", [P, E])
        tinc = sb("tiles_upto", [P, E])
        base = sb("slot_base", [P, E])
        posf = sb("slot_f", [P, 2, NT])
        pos = sb("slot", [P, 2, NT], i32)
        iota_j = sb("iota_j", [1, NSLOT])
        cmp_j = sb("cmp_j", [1, NSLOT, E])
        ejf = sb("tile_expert_f", [1, NSLOT])
        ej = sb("tile_expert", [1, NSLOT], i32)

        io1 = POOL.mark(lambda e: e.iota(iota_e[:, :], [[1, E]], base=0, channel_multiplier=0,
                                         allow_small_or_imprecise_dtypes=True))
        io2 = POOL.mark(lambda e: e.iota(iota_j[:, :], [[1, NSLOT]], base=0, channel_multiplier=0,
                                         allow_small_or_imprecise_dtypes=True))
        one_ok = POOL.mark(lambda e: e.memset(ones[:, :], 1.0))
        tri_ok = POOL.mark(lambda e: e.affine_select(
            out=tri[:, :], in_=ones[:, :], compare_op=ALU.is_gt, fill=0.0, base=0,
            pattern=[[1, P]], channel_multiplier=-1), one_ok)

        def bc(ap, shape):
            return ap.to_broadcast(shape)

        m = DVE.mark(lambda e: e.tensor_tensor(
            lg[:, :, :], logit_ps[:, 0:NE].rearrange("p (t e) -> p t e", t=NT),
            bc(rbias[:, :].rearrange("p (o e) -> p o e", o=1), [P, NT, E]), ALU.add), logits_ok, par_in)
        lg_ok = m
        for t in range(NT):
            m = DVE.mark(lambda e, t=t: e.max(top[:, t, :], lg[:, t, :]), lg_ok)
        for t in range(NT):
            m2 = DVE.mark(lambda e, t=t: e.max_index(topi[:, t, :], top[:, t, :], lg[:, t, :]), m)
        m = DVE.mark(lambda e: e.tensor_tensor(lg[:, :, :], lg[:, :, :], bc(top[:, :, 0:1], [P, NT, E]),
                                               ALU.subtract), m2)
        m = DVE.mark(lambda e: e.tensor_tensor(pr[:, :, :], top[:, :, 0:2], bc(top[:, :, 0:1], [P, NT, 2]),
                                               ALU.subtract), m)
        xm = ACTE.mark(lambda e: e.activation(ex_l[:, :, :], lg[:, :, :], ACT.Exp), m)
        xm = ACTE.mark(lambda e: e.activation(pr[:, :, :], pr[:, :, :], ACT.Exp))
        m = DVE.mark(lambda e: e.tensor_reduce(rs[:, :], ex_l[:, :, :], AX.X, ALU.add), xm)
        m = DVE.mark(lambda e: e.reciprocal(rs[:, :], rs[:, :]), m)
        m = DVE.mark(lambda e: e.tensor_tensor(
            pr[:, :, :], pr[:, :, :], bc(rs[:, :].rearrange("p (t o) -> p t o", o=1), [P, NT, 2]), ALU.mult), m)
        m = DVE.mark(lambda e: e.tensor_tensor(dw[:, :], pr[:, :, 1], pr[:, :, 0], ALU.subtract), m)
        xm = ACTE.mark(lambda e: e.activation(wgt[:, 1, :], dw[:, :], ACT.Exp), m)
        m = DVE.mark(lambda e: e.tensor_scalar(dw[:, :], wgt[:, 1, :], 1.0, None, ALU.add), xm)
        m = DVE.mark(lambda e: e.reciprocal(wgt[:, 0, :], dw[:, :]), m)
        wgt_ok = DVE.mark(lambda e: e.tensor_tensor(wgt[:, 1, :], wgt[:, 1, :], wgt[:, 0, :], ALU.mult), m)
        m = DVE.mark(lambda e: e.tensor_copy(topf[:, :, :], topi[:, :, 0:2]), m2)
        for k in range(2):
            mo = DVE.mark(lambda e, k=k: e.tensor_tensor(
                oh[:, k, :, :], bc(iota_e[:, :].rearrange("p (o e) -> p o e", o=1), [P, NT, E]),
                bc(topf[:, :, k:k + 1], [P, NT, E]), ALU.is_equal), m, io1)
        both = DVE.mark(lambda e: e.tensor_tensor(tmp[:, :, :], oh[:, 0, :, :], oh[:, 1, :, :], ALU.add), mo)
        m = DVE.mark(lambda e: e.memset(cnt[:, 0, :], 0.0))
        for t in range(NT):
            m = DVE.mark(lambda e, t=t: e.tensor_tensor(cnt[:, t + 1, :], cnt[:, t, :], tmp[:, t, :], ALU.add),
                         m, both)
        i, rbank, rfree = tbanks.next()
        PE.wait(m, tri_ok, *rfree)
        PE.do(lambda e: e.matmul(rbank[:, 0:NE], tri[:, :], tmp[:, :, :].rearrange("p t e -> p (t e)"),
                                 start=True, stop=False))
        PE.do(lambda e: e.matmul(rbank[:, 0:NE], ones[:, :],
                                 cnt[:, 0:NT, :].rearrange("p t e -> p (t e)"), start=False, stop=True))
        pm_m = PE.mark(lambda e: e.matmul(rbank[:, NE:NE + E], ones[:, :], cnt[:, NT, :], start=True, stop=True))
        m = DVE.mark(lambda e: e.tensor_copy(rank[:, :, :], rbank[:, 0:NE].rearrange("p (t e) -> p t e", t=NT)), pm_m)
        m = DVE.mark(lambda e: e.tensor_scalar(ntot[:, :], rbank[:, NE:NE + E], float(P - 1), None, ALU.add), m)
        rank_read = m
        m = DVE.mark(lambda e: e.tensor_copy(ntile[:, :], ntot[:, :]), m)
        m = DVE.mark(lambda e: e.tensor_scalar(ntile[:, :], ntile[:, :], 7, None, ALU.arith_shift_right), m)
        m = DVE.mark(lambda e: e.tensor_copy(ntile_f[:, :], ntile[:, :]), m)
        m = DVE.mark(lambda e: e.tensor_copy(tinc[:, 0:1], ntile_f[:, 0:1]), m)
        for ex in range(1, E):
            m = DVE.mark(lambda e, ex=ex: e.tensor_tensor(tinc[:, ex:ex + 1], tinc[:, ex - 1:ex],
                                                          ntile_f[:, ex:ex + 1], ALU.add), m)
        tinc_ok = m
        m = DVE.mark(lambda e: e.tensor_tensor(base[:, :], tinc[:, :], ntile_f[:, :], ALU.subtract), m)
        m = DVE.mark(lambda e: e.tensor_scalar(base[:, :], base[:, :], float(P), None, ALU.mult), m)
        m = DVE.mark(lambda e: e.tensor_tensor(rank[:, :, :], rank[:, :, :],
                                               bc(base[:, :].rearrange("p (o e) -> p o e", o=1), [P, NT, E]),
                                               ALU.add), m)
        for k in range(2):
            m = DVE.mark(lambda e, k=k: e.tensor_tensor(tmp[:, :, :], oh[:, k, :, :], rank[:, :, :], ALU.mult), m, pm_m)
            m = DVE.mark(lambda e, k=k: e.tensor_reduce(posf[:, k, :], tmp[:, :, :], AX.X, ALU.add), m)
        pos_ok = DVE.mark(lambda e: e.tensor_copy(pos[:, :, :], posf[:, :, :]), m)
        m = DVE.mark(lambda e: e.tensor_tensor(
            cmp_j[:, :, :], bc(iota_j[:, :].rearrange("p (j o) -> p j o", o=1), [1, NSLOT, E]),
            bc(tinc[0:1, :].rearrange("p (o e) -> p o e", o=1), [1, NSLOT, E]), ALU.is_ge), tinc_ok, io2, pos_ok)
        m = DVE.mark(lambda e: e.tensor_reduce(ejf[:, :], cmp_j[:, :, :], AX.X, ALU.add), m)
        m = DVE.mark(lambda e: e.tensor_scalar(ejf[:, :], ejf[:, :], float(E - 1), None, ALU.min), m)
        ej_ok = DVE.mark(lambda e: e.tensor_copy(ej[:, :], ejf[:, :]), m)

        s_sc = stream("scatter")
        for t in range(NT):
            for k in range(2):
                scattered = POOL.dma(lambda e, t=t, k=k: e.indirect_dma_start(
                    xs_d, bass.IndirectOffsetOnAxis(ap=pos[:, k, t:t + 1], axis=0), res[:, t, :], None),
                    s_sc, pos_ok, zeros_in, norm2[t // TB][t % TB])

        mbanks = Ring(work + [st2[1][:, 0, :], st2[1][:, 1, :], o_ps[:, :]])
        mbanks.free = [(rank_read, logits_ok, lg_ok)] * 3 + [pairs.free[0] + pairs.free[1]] * 2 + [o_free[0]]
        y_free_bank = st2[0]
        hid_ring, act_ring, hidT_ring = Ring(hid), Ring(act), Ring(hidT)
        sx_ring, sxT_ring, b12_ring, sy_ring = Ring(slot_x), Ring(slot_xT), Ring(bias12), Ring(slot_y)
        ybanks = Ring([st2[0][:, 0, :], st2[0][:, 1, :]])
        ybanks.free = [pairs.free[0] + pairs.free[1]] * 2
        s_sx = [stream("slot_x") for _ in slot_x]
        s_b12 = [stream("bias") for _ in bias12]
        s_sy = [stream("slot_y") for _ in slot_y]
        more_free = (attention_done, cp, norm2[0][-1], norm2[1][-1], zeros_in)
        tiles = [dict() for _ in range(NSLOT)]

        def load(j):
            t = tiles[j]
            t["xi"], t["x"], free = sx_ring.next()
            t["x_in"] = SP.dma(lambda e: e.dma_start(t["x"], xs_d[j * P:(j + 1) * P, :]), s_sx[t["xi"]],
                               scattered, *more_free, *free)
            t["bi"], t["b"], free = b12_ring.next()
            SP.wait(ej_ok, *free)

            def biases(e, which):
                if which == 0:
                    t["ex"] = e.value_load(ej[0:1, j:j + 1], min_val=0, max_val=E - 1)
                    return e.dma_start(t["b"][:, 0:FF], b1[bass.ds(t["ex"], 1), :].to_broadcast([P, FF]))
                return e.dma_start(t["b"][:, FF:FF + D], b2[bass.ds(t["ex"], 1), :].to_broadcast([P, D]))
            SP.dma(lambda e: biases(e, 0), s_b12[t["bi"]])
            t["b_in"] = SP.dma(lambda e: biases(e, 1), s_b12[t["bi"]])

        def turn(j):
            t = tiles[j]
            i, bank, bfree = mbanks.next()
            PE.wait(t["x_in"], *bfree)
            for c in range(KC):
                m = (PE.mark if c == KC - 1 else PE.do)(lambda e, c=c: e.transpose(
                    bank[:, c * P:(c + 1) * P], t["x"][:, c * P:(c + 1) * P], ident[:, :]))
            sx_ring.release(t["xi"], m)
            t["xTi"], t["xT"], free = sxT_ring.next()
            t["xT_ok"] = ACTE.mark(lambda e: e.copy(
                t["xT"], bank[:, 0:D].rearrange("p (c n) -> p c n", c=KC)), m, *free)
            mbanks.release(i, t["xT_ok"])

        def up(j):
            t = tiles[j]
            PE.wait(t["xT_ok"], ej_ok, early_in, late_in)
            hi, hd, hfree = hid_ring.next()

            def first(e):
                t["ex_pe"] = e.value_load(ej[0:1, j:j + 1], min_val=0, max_val=E - 1)
            for n in range(FF // BANK):
                i, bank, bfree = mbanks.next()
                PE.wait(*bfree)
                for c in range(KC):
                    def mm(e, n=n, c=c, bank=bank):
                        if n == 0 and c == 0:
                            first(e)
                        return e.matmul(bank, t["xT"][:, c, :],
                                        w1_sb[:, bass.ds(t["ex_pe"] * EW + (c * FF + n * BANK), BANK)],
                                        start=(c == 0), stop=(c == KC - 1))
                    m = (PE.mark if c == KC - 1 else PE.do)(mm)
                d = DVE.mark(lambda e, n=n, bank=bank: e.tensor_tensor(
                    hd[:, n * BANK:(n + 1) * BANK], bank, t["b"][:, n * BANK:(n + 1) * BANK], ALU.add),
                    m, t["b_in"], *hfree)
                mbanks.release(i, d)
            sxT_ring.release(t["xTi"], m)
            ai, t["act"], afree = act_ring.next()
            t["ai"] = ai
            t["act_ok"] = ACTE.mark(lambda e: e.activation(t["act"], hd, ACT.Gelu), d, *afree)
            hid_ring.release(hi, t["act_ok"])

        def down(j):
            t = tiles[j]
            ti, hT, tfree = hidT_ring.next()
            PE.wait(t["act_ok"])
            for half in range(2):
                i, bank, bfree = mbanks.next()
                PE.wait(*bfree)
                for q in range(4):
                    c = half * 4 + q
                    m = (PE.mark if q == 3 else PE.do)(lambda e, q=q, c=c, bank=bank: e.transpose(
                        bank[:, q * P:(q + 1) * P], t["act"][:, c * P:(c + 1) * P], ident[:, :]))
                src = bank.rearrange("p (c n) -> p c n", c=4)
                dst = hT[:, half * 4:half * 4 + 4, :]
                if half == 0:
                    a = ACTE.mark(lambda e, src=src, dst=dst: e.copy(dst, src), m, *tfree)
                else:
                    a = DVE.mark(lambda e, src=src, dst=dst: e.tensor_copy(dst, src), m, *tfree)
                mbanks.release(i, a)
                t["h", half] = a
            act_ring.release(t["ai"], m)
            i, bank, bfree = ybanks.next()
            PE.wait(*bfree)
            for c in range(FC):
                PE.wait(t["h", c // 4])
                m = (PE.mark if c == FC - 1 else PE.do)(lambda e, c=c: e.matmul(
                    bank[:, 0:D], hT[:, c, :], w2_sb[:, bass.ds(t["ex_pe"] * EW + c * D, D)],
                    start=(c == 0), stop=(c == FC - 1)))
            hidT_ring.release(ti, m)
            yi, y, yfree = sy_ring.next()
            d = DVE.mark(lambda e: e.tensor_tensor(y, bank[:, 0:D], t["b"][:, FF:FF + D], ALU.add), m, *yfree)
            ybanks.release(i, d)
            b12_ring.release(t["bi"], d)
            t["stored"] = ACTE.dma(lambda e: e.dma_start(ys_d[j * P:(j + 1) * P, :], y), s_sy[yi], d)
            sy_ring.release(yi, t["stored"])

        DVE.wait(*more_free)
        ACTE.wait(*more_free)
        load(0)
        turn(0)
        load(1)
        for j in range(NSLOT):
            if j + 1 < NSLOT:
                turn(j + 1)
            up(j)
            if j >= 1:
                down(j - 1)
            if j + 2 < NSLOT:
                load(j + 2)
        down(NSLOT - 1)

        g_ring = Ring(gath)
        g_ring.free = [(pos_ok, wgt_ok, rank_read)] * 2
        s_g = [stream("gather") for _ in gath]
        s_out = stream("out")
        stored = [tiles[NSLOT - 1]["stored"], tiles[NSLOT - 2]["stored"]]
        for t in range(NT):
            gi, gt, gfree = g_ring.next()
            for k in range(2):
                got = POOL.dma(lambda e, t=t, k=k, gt=gt: e.indirect_dma_start(
                    gt[:, k, :], None, ys_d, bass.IndirectOffsetOnAxis(ap=pos[:, k, t:t + 1], axis=0)),
                    s_g[gi], *stored, *gfree)
            DVE.wait(got, wgt_ok, scattered)
            m = DVE.mark(lambda e, t=t, gt=gt: e.scalar_tensor_tensor(
                res[:, t, :], gt[:, 0, :], wgt[:, 0, t:t + 1], res[:, t, :], ALU.mult, ALU.add))
            m = DVE.mark(lambda e, t=t, gt=gt: e.scalar_tensor_tensor(
                res[:, t, :], gt[:, 1, :], wgt[:, 1, t:t + 1], res[:, t, :], ALU.mult, ALU.add), m)
            g_ring.release(gi, m)
            m = norm_stats(t, res[:, t, :], m, t % 2)
        scaled = norm_scale(0, NT, m)
        for t in range(NT):
            m = norm_apply(t, scaled, G3, B3N)
            done = SP.dma(lambda e, t=t: e.dma_start(
                out[t // TB, (t % TB) * P:(t % TB + 1) * P, :], res[:, t, :]), s_out, m)
        SP.wait(done)

        block = stack.enter_context(nc.Block())

        @block.tensor
        def _(e):
            PE.run(e)

        @block.scalar
        def _(e):
            ACTE.run(e)

        @block.vector
        def _(e):
            DVE.run(e)

        @block.gpsimd
        def _(e):
            POOL.run(e)

        @block.sync
        def _(e):
            SP.run(e)


def kernel(**inputs):
    import numpy as np
    import concourse.bacc as bacc
    from concourse.bass_utils import run_bass_kernel_spmd

    nc = bacc.Bacc("TRN2", target_bir_lowering=False, num_devices=1)
    arrays, ap = {}, {}
    for name, value in inputs.items():
        a = np.ascontiguousarray(value)
        arrays[f"in_{name}"] = a
        ap[name.removeprefix("L0_xattn_")] = nc.dram_tensor(
            f"in_{name}", a.shape, mybir.dt.from_np(a.dtype), kind="ExternalInput").ap()
    out = nc.dram_tensor("out_0", (B, S, D), mybir.dt.float32, kind="ExternalOutput").ap()
    par = {
        "bq": (ap["sa_bq"], ap["ca_bq"]), "bk": (ap["sa_bk"], ap["ca_bk"]), "rb": ap["router_b"],
        "rows": [ap[n] for n in ("sa_bv", "sa_bo", "ca_bv", "ca_bo", "ln1_g", "ln1_b",
                                 "ln2_g", "ln2_b", "ln3_g", "ln3_b")],
    }
    wts = [ap[f"{a}_w{w}"] for a in ("sa", "ca") for w in "qkvo"]
    build(nc, ap["x"], ap["ctx_1024"], par, wts, ap["router_w"], ap["e_w1"], ap["e_b1"],
          ap["e_w2"], ap["e_b2"], out)
    r = run_bass_kernel_spmd(nc, [arrays], core_ids=[0])
    return r.results[0]["out_0"]
```

```python
from contextlib import ExitStack

import numpy as np

import concourse.bass as bass
from concourse import mybir

P = 128
B, S, D = 2, 1024, 256
SE = 77
H, HD = 16, 16
E, FF = 8, 1024
EPS = 1e-5
KC = D // P
FC = FF // P
T = B * S
NT = T // P
TB = S // P
HH = P // HD
QUAD = 4
QG = 512
NG = S // QG
BANK = 512
VW = 2 * HD
Q_PART = (0, 0, 1, 1, 0, 2)
K_PART = (0, 1, 0, 1, 2, 0)
NGR = len(Q_PART)
R_S = NGR * HD
R_M = R_S + 3
TWO_ONES = float(np.array([0x3F803F80], np.uint32).view(np.float32)[0])
NEG = -1e30
NSLOT = (2 * T + E * (P - 1)) // P
NPARAM = 10
MORE = 11776


class Mark:

    def __init__(self, sem, value):
        self.sem, self.value = sem, value


class Engine:

    def __init__(self, sem):
        self.sem, self.count, self.queue, self.waited = sem, 0, [], {}

    def wait(self, *marks):
        for m in marks:
            if m is not None and self.waited.get(id(m.sem), 0) < m.value:
                self.waited[id(m.sem)] = m.value
                self.queue.append((lambda e, m=m: e.wait_ge(m.sem, m.value), None, 0))

    def do(self, call, *after):
        self.wait(*after)
        self.queue.append((call, None, 0))

    def mark(self, call, *after):
        self.wait(*after)
        self.count += 1
        self.queue.append((call, self.sem, 1))
        return Mark(self.sem, self.count)

    def dma(self, call, stream, *after):
        self.wait(*after)
        stream.count += 16
        self.queue.append((call, stream.sem, 16))
        return Mark(stream.sem, stream.count)

    def run(self, e):
        for call, sem, inc in self.queue:
            made = call(e)
            if sem is not None:
                made.then_inc(sem, inc)


class Stream:

    def __init__(self, sem):
        self.sem, self.count = sem, 0


class Ring:

    def __init__(self, buffers):
        self.buffers, self.free, self.at = buffers, [()] * len(buffers), -1

    def next(self):
        self.at = (self.at + 1) % len(self.buffers)
        free, self.free[self.at] = self.free[self.at], None
        assert free is not None, "a buffer is taken again before it was given back"
        return self.at, self.buffers[self.at], free

    def release(self, i, *marks):
        self.free[i] = marks


def interleave(main, side, end=0.9):
    done = 0
    for i, step in enumerate(main):
        step()
        while done < min(len(side), len(side) * (i + 1) // (end * len(main))):
            side[done]()
            done += 1
    for step in side[done:]:
        step()


def build(nc, x, ctx_in, par, wts, router_w, w1, b1, w2, b2, out):
    f32, bf16, i32, u32 = mybir.dt.float32, mybir.dt.bfloat16, mybir.dt.int32, mybir.dt.uint32
    ALU, ACT, AX = mybir.AluOpType, mybir.ActivationFunctionType, mybir.AxisListType
    stack = ExitStack()
    with stack:
        def sb(name, shape, dt=f32):
            return stack.enter_context(nc.sbuf_tensor(name, shape, dt))

        n_sem = [0]

        def stream(name):
            n_sem[0] += 1
            return Stream(stack.enter_context(nc.semaphore(f"dma_{name}_{n_sem[0]}")))

        PE, ACTE, DVE, POOL, SP = (Engine(stack.enter_context(nc.semaphore(f"done_{n}")))
                                   for n in ("pe", "act", "dve", "pool", "sp"))

        parts_d = nc.dram_tensor("parts_scratch", [2 * B * (H // HH), 2, 3, P, S], bf16, kind="Internal").ap()
        negm_d = nc.dram_tensor("negmax_scratch", [2 * B * (H // HH), 3, HH, S], bf16, kind="Internal").ap()
        tokens_d = nc.dram_tensor("tokens_scratch", [T, D], f32, kind="Internal").ap()
        sums_d = nc.dram_tensor("sums_scratch", [T + P, D], f32, kind="Internal").ap()

        res = sb("residual", [P, NT, D])
        param = sb("param_rows", [P, NPARAM, D])
        ident = sb("ident", [P, P])
        identb = sb("identb", [P, P], bf16)
        mask_qk = sb("mask_qk", [P, P], bf16)
        b_qk = sb("b_qk", [P, 2, 2, KC])
        rbias = sb("router_bias", [P, E])
        rw = sb("router_w", [P, KC, E])
        epsc = sb("eps", [P, 1])
        stat = sb("stat", [P, 2, 6])
        mv = sb("mean_var", [P, NT, 2])
        rstd = sb("rstd", [P, NT])
        sdev = sb("sdev", [P, NT])
        pm = sb("part_max", [P, TB, HH, 2])
        negm = sb("neg_max", [P, TB, HH])
        negp = sb("neg_max_parts", [P, TB, 3, HH], bf16)
        negr = sb("neg_max_rest", [P, TB, HH])
        rsum = sb("recip_sum", [P, 2, QUAD, QUAD])
        (A_BV, A_BO, C_BV, C_BO, G1, B1N, G2, B2N, G3, B3N) = range(NPARAM)

        W_WORDS = 2 * E * KC * FF
        arena = sb("arena", [P, W_WORDS])
        more = sb("arena_more", [P, MORE])
        at = {"arena": 0, "more": 0}

        def cut(where, words):
            a = at[where]
            at[where] += words
            whole = arena if where == "arena" else more
            assert at[where] <= whole.shape[1], (where, at[where])
            return whole[:, a:a + words]

        def cut_bf(where, n):
            return cut(where, n // 2).bitcast(bf16)

        w1_sb = arena[:, 0:W_WORDS // 2]
        w2_sb = arena[:, W_WORDS // 2:W_WORDS]
        EW = KC * FF
        ka = [cut_bf("arena", HH * S).rearrange("p (h t) -> p h t", h=HH) for _ in range(2)]
        va = [cut("arena", TB * HH * VW).rearrange("p (k h v) -> p k h v", k=TB, h=HH) for _ in range(2)]
        w_self = [cut("arena", KC * D).rearrange("p (c n) -> p c n", c=KC) for _ in range(4)]
        qa = [cut_bf("arena", HH * S).rearrange("p (h t) -> p h t", h=HH) for _ in range(2)]
        pt = [cut("arena", 2 * QG).rearrange("p (j q) -> p j q", j=2) for _ in range(4)]
        f_sb = [cut("arena", S)]
        kac = [cut_bf("arena", HH * 80).rearrange("p (h t) -> p h t", h=HH) for _ in range(2)]
        vac = [cut("arena", HH * VW).rearrange("p (h v) -> p h v", h=HH) for _ in range(2)]
        ctxT = cut("arena", B * KC * SE).rearrange("p (b c n) -> p b c n", b=B, c=KC)
        w_cross = [cut("arena", KC * D).rearrange("p (c n) -> p c n", c=KC) for _ in range(3)]
        assert at["arena"] <= W_WORDS - EW
        at["arena"] = W_WORDS - EW
        w_cross.append(cut("arena", KC * D).rearrange("p (c n) -> p c n", c=KC))
        ot = [cut("arena", QG) for _ in range(2)]
        ctxn = ot[0].rearrange("p (b n) -> p b n", b=B)
        onT = [cut("arena", D).rearrange("p (c n) -> p c n", c=KC) for _ in range(2)]
        xT = cut("more", KC * T // 2).rearrange("p (c n) -> p c n", c=KC)
        onat = [cut("more", TB * D).rearrange("p (t n) -> p t n", t=TB) for _ in range(2)]
        part_sb = [[cut_bf("more", S) for _ in range(3)] for _ in range(2)]
        mT = cut_bf("more", S)
        zeros = cut("more", D)
        at["more"] = 0
        slot_x = [cut("more", D) for _ in range(3)]
        slot_xT = [cut("more", D).rearrange("p (c n) -> p c n", c=KC) for _ in range(2)]
        bias12 = [cut("more", FF + D) for _ in range(3)]
        hid = [cut("more", FF) for _ in range(2)]
        act = [cut("more", FF) for _ in range(2)]
        hidT = [cut("more", FF).rearrange("p (c n) -> p c n", c=FC) for _ in range(1)]
        slot_y = [cut("more", D) for _ in range(2)]

        st2 = [stack.enter_context(nc.psum_tensor(f"score_pair{i}", [P, 2, BANK], f32)) for i in range(2)]
        o_ps = stack.enter_context(nc.psum_tensor("out_acc", [P, BANK], f32))
        work = [stack.enter_context(nc.psum_tensor(f"work{i}", [P, BANK], f32))[:, :] for i in range(3)]
        banks = Ring(work)
        pairs = Ring(st2)
        o_free = [()]

        s_x = [stream("x") for _ in range(B)]
        x_in = [SP.dma(lambda e, b=b: e.dma_start(res[:, b * TB:(b + 1) * TB, :],
                                                  x[b].rearrange("(t p) n -> p t n", p=P)), s_x[b])
                for b in range(B)]
        s_w = stream("w_self")
        for i in range(4):
            w_in = ACTE.dma(lambda e, i=i: e.dma_start(w_self[i], wts[i].rearrange("(c p) n -> p c n", p=P)), s_w)
        s_bc = stream("bias_cols")
        for a in range(2):
            for i in range(2):
                bc_in = SP.dma(lambda e, a=a, i=i: e.dma_start(
                    b_qk[:, a, i, :], par[("bq", "bk")[i]][a].rearrange("(c p) -> p c", p=P),
                    allow_slow_non_contiguous=True), s_bc)
        s_pr = stream("params")
        for i, row in enumerate(par["rows"]):
            par_in = SP.dma(lambda e, i=i, row=row: e.dma_start(
                param[:, i, :], row.rearrange("(o n) -> o n", o=1).to_broadcast([P, D])), s_pr)
        par_in = SP.dma(lambda e: e.dma_start(
            rbias[:, :], par["rb"].rearrange("(o n) -> o n", o=1).to_broadcast([P, E])), s_pr)
        s_wc = stream("w_cross")
        for i in range(4):
            wc_in = ACTE.dma(lambda e, i=i: e.dma_start(w_cross[i], wts[4 + i].rearrange("(c p) n -> p c n", p=P)), s_wc)
        wc_in = ACTE.dma(lambda e: e.dma_start(rw[:, :, :], router_w.rearrange("(c p) n -> p c n", p=P)), s_wc)
        wc_in = ACTE.dma(lambda e: e.dma_start(ctxn[0:SE, :, :], ctx_in.rearrange("b s n -> s b n")), s_wc)

        c0 = DVE.mark(lambda e: e.memset(ident[:, :], 0.0))
        c1 = DVE.mark(lambda e: e.memset(mask_qk[:, :], 0.0))
        id_ok = POOL.mark(lambda e: e.affine_select(
            out=ident[:, :], in_=ident[:, :], compare_op=ALU.not_equal, fill=1.0, base=0,
            pattern=[[-1, P]], channel_multiplier=1), c0)
        mask_ok = POOL.mark(lambda e: e.affine_select(
            out=mask_qk[:, :], in_=mask_qk[:, :], compare_op=ALU.is_ge, fill=NEG, base=0,
            pattern=[[-1, P]], channel_multiplier=1), c1)
        idb_ok = DVE.mark(lambda e: e.tensor_copy(identb[:, :], ident[:, :]), id_ok)
        DVE.do(lambda e: e.memset(epsc[:, :], EPS))
        DVE.do(lambda e: e.memset(pm[:, 0:TB // 2, :, 1:2], NEG))
        for i in range(2):
            mask_done = POOL.mark(lambda e, i=i: e.memset(kac[i][R_S:R_M, :, 0:SE], 1.0),
                                  mask_ok if i == 0 else ones_ok)
            ones_ok = POOL.mark(lambda e, i=i: e.memset(
                ka[i][R_S:R_M, :, :].rearrange("p h t -> p (h t)").bitcast(f32), TWO_ONES), mask_done)
            DVE.do(lambda e, i=i: e.memset(vac[i][:, :, HD:VW], 1.0))
            const_ok = DVE.mark(lambda e, i=i: e.memset(va[i][:, :, :, HD:VW], 1.0))
        zero_ok = POOL.mark(lambda e: e.memset(zeros, 0.0), ones_ok)
        POOL.wait(zero_ok)
        s_z = stream("zero")
        zeros_in = SP.dma(lambda e: e.dma_start(sums_d[T:T + P, :], zeros), s_z, zero_ok)

        x_t_free = [()]

        def transpose_tile(t, ready, dst, free, evac):
            i, bank, bfree = banks.next()
            PE.wait(ready, id_ok, *bfree)
            for c in range(KC):
                m = (PE.mark if c == KC - 1 else PE.do)(lambda e, c=c, bank=bank: e.transpose(
                    bank[:, c * P:(c + 1) * P], res[:, t, c * P:(c + 1) * P], ident[:, :]))
            src = bank[:, 0:D].rearrange("p (c n) -> p c n", c=KC)
            if evac is ACTE:
                done = ACTE.mark(lambda e: e.copy(dst, src), m, *free)
            else:
                done = DVE.mark(lambda e: e.tensor_copy(dst, src), m, *free)
            banks.release(i, done)
            return done

        def x_t_steps(b, ready, say):
            def step(t):
                say[t] = transpose_tile(b * TB + t, ready[t], xT[:, :, t * P:(t + 1) * P],
                                        x_t_free[0], ACTE if t % 2 else DVE)
            return [lambda t=t: step(t) for t in range(TB)]

        f_ring, part_ring = Ring(f_sb), Ring(part_sb)
        slot_free = {"qa": [(), ()], "ka": [(), ()], "va": [(), ()], "kac": [(), ()], "vac": [(), ()]}
        mT_free, pm_free, negp_free = [(), ()], [(), ()], [(), ()]
        s_part = {}

        class Stage:
            def __init__(self, n, cross, b, hh):
                self.n, self.cross, self.b, self.hh, self.slot = n, cross, b, hh, n % 2
                self.keys = SE if cross else S
                self.ka = (kac if cross else ka)[self.slot]
                self.qa = qa[self.slot]
                self.loads = []
                self.va_ok = self.q_ok = self.k_ok = ()
                self.m_ok = [(), ()]

        def project_steps(st, which, src, n_tok, src_ok, weights, w_ok):
            box = {}

            def make(n0):
                if n0 == 0:
                    box["f"] = f_ring.next()
                fi, f, ffree = box["f"]
                w = min(BANK, n_tok - n0)
                i, bank, bfree = banks.next()
                PE.wait(w_ok, *bfree)
                for m in src_ok(n0, w):
                    PE.wait(m)
                for c in range(KC):
                    m = (PE.mark if c == KC - 1 else PE.do)(lambda e, c=c: e.matmul(
                        bank[:, 0:w], weights[:, c, st.hh * P:(st.hh + 1) * P], src(c, n0, w),
                        start=(c == 0), stop=(c == KC - 1)))
                if which == 0:
                    x_t_free[0] = x_t_free[0] + (m,)
                if n0 == 0:
                    box["p"] = part_ring.next()
                part, pfree = box["p"][1:]
                bias = b_qk[:, int(st.cross), which, st.hh:st.hh + 1]
                ACTE.do(lambda e: e.activation(part[0][:, n0:n0 + w], bank[:, 0:w], ACT.Identity, bias=bias),
                        m, bc_in, *pfree)
                box["made"] = ACTE.mark(lambda e: e.activation(
                    f[:, n0:n0 + w], bank[:, 0:w], ACT.Identity, bias=bias), *ffree)
                banks.release(i, box["made"])

            def split():
                fi, f, _ = box["f"]
                pi, part, pfree = box["p"]
                a, p = f[:, 0:n_tok], [q[:, 0:n_tok] for q in part]
                m = POOL.mark(lambda e: e.tensor_tensor(a, a, p[0], ALU.subtract), box["made"])
                m = ACTE.mark(lambda e: e.copy(p[1], a), m)
                m = POOL.mark(lambda e: e.tensor_tensor(p[2], a, p[1], ALU.subtract), m)
                f_ring.release(fi, m)
                out_s = s_part.setdefault(("out", pi), stream("parts_out"))
                for k in range(3):
                    stored = SP.dma(lambda e, k=k: e.dma_start(parts_d[st.n, which, k, :, 0:n_tok], p[k]),
                                    out_s, m)
                part_ring.release(pi, stored)
                box["stored"] = stored

            def load():
                into = (st.qa, st.ka)[which]
                key = "qa" if which == 0 else ("kac" if st.cross else "ka")
                in_s = s_part.setdefault((key, st.slot), stream(f"{key}_in"))
                for g in range(NGR):
                    loaded = SP.dma(lambda e, g=g: e.dma_start(
                        into[g * HD:(g + 1) * HD, :, 0:n_tok],
                        parts_d[st.n, which, (Q_PART, K_PART)[which][g], :, 0:n_tok]
                        .rearrange("(h d) t -> d h t", d=HD)), in_s, box["stored"], *slot_free[key][st.slot])
                if which == 0:
                    st.q_ok = (loaded,)
                else:
                    st.k_ok = (loaded, ones_ok)

            st.loads.append(load)
            return [lambda n0=n0: make(n0) for n0 in range(0, n_tok, BANK)] + [split]

        def v_steps(st, src, src_ok, weights, w_ok, row):
            def make(k0):
                i, bank, bfree = banks.next()
                nk = 1 if st.cross else 4
                rows = SE if st.cross else P
                PE.wait(w_ok, *bfree)
                for k in range(nk):
                    for mk in src_ok((k0 + k) * P, rows):
                        PE.wait(mk)
                    for c in range(KC):
                        m = (PE.mark if k == nk - 1 and c == KC - 1 else PE.do)(lambda e, k=k, c=c: e.matmul(
                            bank[0:rows, k * P:(k + 1) * P], src(c, (k0 + k) * P, rows),
                            weights[:, c, st.hh * P:(st.hh + 1) * P], start=(c == 0), stop=(c == KC - 1)))
                if not st.cross:
                    x_t_free[0] = x_t_free[0] + (m,)
                bias = param[0:rows, row, st.hh * P:(st.hh + 1) * P].rearrange("p (h d) -> p h d", h=HH)
                key = "vac" if st.cross else "va"
                DVE.wait(m, par_in, *slot_free[key][st.slot])
                for k in range(nk):
                    to = vac[st.slot][0:rows, :, 0:HD] if st.cross else va[st.slot][:, k0 + k, :, 0:HD]
                    frm = bank[0:rows, k * P:(k + 1) * P].rearrange("p (h d) -> p h d", h=HH)
                    d = DVE.mark(lambda e, to=to, frm=frm: e.tensor_tensor(to, frm, bias, ALU.add))
                banks.release(i, d)
                st.va_ok = (d, const_ok)
            return [lambda k0=k0: make(k0) for k0 in range(0, 1 if st.cross else TB, 4)]

        def max_steps(st):
            box = {}

            def item(qb, c, w, h0, nh, diagonal):
                i, bank, bfree = banks.next()
                PE.wait(*st.q_ok, *st.k_ok, *bfree, mask_ok, idb_ok)
                for j in range(nh):
                    h = h0 + j
                    m = (PE.mark if j == nh - 1 and not diagonal else PE.do)(lambda e, h=h, j=j: e.matmul(
                        bank[:, j * w:(j + 1) * w], st.qa[0:R_S, h, qb * P:(qb + 1) * P],
                        st.ka[0:R_S, h, c * BANK:c * BANK + w], start=True, stop=not diagonal))
                    if diagonal:
                        m = (PE.mark if j == nh - 1 else PE.do)(lambda e, j=j: e.matmul(
                            bank[:, (j + 1) * w - P:(j + 1) * w], identb[:, :], mask_qk[:, :],
                            start=False, stop=True))
                src = bank[:, 0:nh * w].rearrange("p (j k) -> p j k", j=nh)
                r = DVE.mark(lambda e: e.tensor_reduce(pm[:, qb, h0:h0 + nh, c], src, AX.X, ALU.max),
                             m, *pm_free[qb * P // QG])
                banks.release(i, r)
                box["r"] = r

            def gather(g):
                tl = slice(g * TB // NG, (g + 1) * TB // NG)
                if st.cross:
                    m = DVE.mark(lambda e: e.tensor_scalar(
                        negm[:, tl, :], pm[:, tl, :, 0], -1.0, None, ALU.mult), box["r"])
                else:
                    m = DVE.mark(lambda e: e.tensor_reduce(
                        negm[:, tl, :], pm[:, tl, :, :], AX.X, ALU.max, negate=True), box["r"])
                pm_free[g] = (m,)
                p = [negp[:, tl, k, :] for k in range(3)]
                m = DVE.mark(lambda e: e.tensor_copy(p[0], negm[:, tl, :]), m, *negp_free[g])
                m = DVE.mark(lambda e: e.tensor_tensor(negr[:, tl, :], negm[:, tl, :], p[0], ALU.subtract), m)
                m = DVE.mark(lambda e: e.tensor_copy(p[1], negr[:, tl, :]), m)
                m = DVE.mark(lambda e: e.tensor_tensor(p[2], negr[:, tl, :], p[1], ALU.subtract), m)
                box["neg"] = m

            def lay(g):
                i, bank, bfree = banks.next()
                rows = bank[0:3 * HH, 0:QG // 2].bitcast(bf16)
                PE.wait(box["neg"], idb_ok, *bfree)
                for t in range(QG // P):
                    m = (PE.mark if t == QG // P - 1 else PE.do)(lambda e, t=t: e.transpose(
                        rows[:, t * P:(t + 1) * P],
                        negp[:, g * (QG // P) + t, :, :].rearrange("p k h -> p (k h)"), identb[:, :]))
                negp_free[g] = (m,)
                cols = slice(g * QG, (g + 1) * QG)
                m = ACTE.mark(lambda e: e.copy(mT[0:3 * HH, cols], rows), m, *mT_free[g])
                banks.release(i, m)
                s = s_part.setdefault(("negm", g), stream("negm_out"))
                stored = SP.dma(lambda e: e.dma_start(
                    negm_d[st.n].rearrange("k h t -> (k h) t")[:, cols], mT[0:3 * HH, cols]), s, m)
                mT_free[g] = (stored,)
                s2 = s_part.setdefault(("negm_in", st.slot, g), stream("negm_in"))
                st.m_ok[g] = (SP.dma(lambda e: e.dma_start(st.qa[R_S:R_M, :, cols], negm_d[st.n][:, :, cols]),
                                     s2, stored, *slot_free["qa"][st.slot]),)

            steps = []
            for qb in range(TB):
                if qb == TB // NG:
                    steps.append(lambda: gather(0))
                    st.second_max_at = len(steps) + 4
                if st.cross:
                    steps += [lambda qb=qb, h0=h0: item(qb, 0, SE, h0, HH // 2, False)
                              for h0 in range(0, HH, HH // 2)]
                    continue
                keys = (qb + 1) * P
                for c in range((keys + BANK - 1) // BANK):
                    w = min(BANK, keys - c * BANK)
                    nh = BANK // w
                    last = (c + 1) * BANK >= keys
                    steps += [lambda qb=qb, c=c, w=w, h0=h0, nh=nh, last=last: item(qb, c, w, h0, nh, last)
                              for h0 in range(0, HH, nh)]
            steps.insert(st.second_max_at - 1, lambda: lay(0))
            return steps + [lambda: gather(1), lambda: lay(1)]

        pt_ring, ot_ring = Ring(pt), Ring(ot)
        rs_ring = Ring([rsum[:, i] for i in range(2)])
        onat_ok = {}
        pt_done = [None]
        onat_free = [(), ()]

        def attend_steps(st):
            steps, pending, box = [], [], {}
            nkb = lambda g: 1 if st.cross else (g + 1) * (QG // P)

            def score(g, quad, kb, pair):
                rows = SE if st.cross else P
                skip = 0 if st.cross else max(0, kb * P - g * QG)
                w = QG - skip
                i, ps, free = pairs.next()
                PE.wait(*st.q_ok, *st.k_ok, *st.m_ok[g], *free)
                diagonal = not st.cross and kb * P >= g * QG
                for j in range(2):
                    h = quad * QUAD + pair * 2 + j
                    k0 = 0 if st.cross else kb * P
                    m = (PE.mark if j == 1 and not diagonal else PE.do)(lambda e, h=h, j=j, k0=k0: e.matmul(
                        ps[0:rows, j, 0:w], st.ka[0:R_M, h, k0:k0 + rows],
                        st.qa[0:R_M, h, g * QG + skip:(g + 1) * QG], start=True, stop=not diagonal))
                    if diagonal:
                        m = (PE.mark if j == 1 else PE.do)(lambda e, j=j: e.matmul(
                            ps[:, j, 0:P], mask_qk[:, :], identb[:, :], start=False, stop=True))
                pi, prob, pfree = pt_ring.next()
                x_ok = ACTE.mark(lambda e: e.activation(
                    prob[0:rows, :, 0:w], ps[0:rows, :, 0:w], ACT.Exp, scale=float(HD) ** -0.5), m, *pfree)
                pairs.release(i, x_ok)
                pt_done[0] = x_ok
                pending.append((pi, prob, x_ok, rows, skip, w))

            def weigh(g, quad, kb):
                first, last = kb == 0, kb == nkb(g) - 1
                PE.wait(*st.va_ok, *(o_free[0] if first else ()))
                for pair in range(2):
                    pi, prob, x_ok, rows, skip, w = pending.pop(0)
                    PE.wait(x_ok)
                    for j in range(2):
                        c = pair * 2 + j
                        h = quad * QUAD + c
                        v = vac[st.slot][0:rows, h, :] if st.cross else va[st.slot][:, kb, h, :]
                        m = (PE.mark if j == 1 else PE.do)(lambda e, c=c, v=v, prob=prob, rows=rows, j=j, w=w, skip=skip: e.matmul(
                            o_ps[c * VW:(c + 1) * VW, skip:QG], v, prob[0:rows, j, 0:w], start=first, stop=last))
                    pt_ring.release(pi, m)
                box["pv"] = m

            def normalise(g, quad):
                oi, o, ofree = ot_ring.next()
                if (g + quad) % 2:
                    cp = ACTE.mark(lambda e: e.copy(o, o_ps[:, :]), box["pv"], *ofree)
                else:
                    cp = DVE.mark(lambda e: e.tensor_copy(o, o_ps[:, :]), box["pv"], *ofree)
                o_free[0] = (cp,)
                box[g, quad] = (oi, o, cp)

            def divide(g, quad):
                oi, o, cp = box[g, quad]
                i, bank, bfree = banks.next()
                PE.wait(cp, *bfree)
                for q in range(QG // P):
                    m = (PE.mark if q == QG // P - 1 else PE.do)(lambda e, q=q: e.transpose(
                        bank[:, q * P:(q + 1) * P], o[:, q * P:(q + 1) * P], ident[:, :]))
                ot_ring.release(oi, m)
                view = bank[:, :].rearrange("p (q c v) -> p q c v", q=QG // P, c=QUAD)
                ri, rs_, rfree = rs_ring.next()
                r = DVE.mark(lambda e: e.reciprocal(rs_, view[:, :, :, HD]), m, *rfree)
                col = st.hh * P + quad * QUAD * HD
                DVE.wait(r, *onat_free[st.b])
                for q in range(QG // P):
                    d = DVE.mark(lambda e, q=q: e.tensor_tensor(
                        onat[st.b][:, g * (QG // P) + q, col:col + QUAD * HD].rearrange("p (c d) -> p c d", c=QUAD),
                        view[:, q, :, 0:HD],
                        rs_[:, q, :].rearrange("p (c o) -> p c o", o=1).to_broadcast([P, QUAD, HD]), ALU.mult))
                banks.release(i, d)
                rs_ring.release(ri, d)
                onat_ok[st.b] = d

            order = [(g, quad, kb) for g in range(NG) for quad in range(HH // QUAD) for kb in range(nkb(g))]
            late, divisions = [], []
            for g, quad, kb in order:
                if (g, quad, kb) == (1, 0, 0):
                    st.second_group_at = len(steps)
                steps.append(lambda g=g, quad=quad, kb=kb: score(g, quad, kb, 0))
                steps.append(lambda g=g, quad=quad, kb=kb: score(g, quad, kb, 1))
                steps += divisions + late
                late, divisions = [lambda g=g, quad=quad, kb=kb: weigh(g, quad, kb)], late[1:] and [
                    lambda gq=ended: divide(*gq)]
                if kb == nkb(g) - 1:
                    ended = (g, quad)
                    late.append(lambda g=g, quad=quad: normalise(g, quad))
            steps += divisions + late + [lambda: divide(*ended)]

            def close():
                slot_free["qa"][st.slot] = (box["pv"],)
                for k in (("kac", "vac") if st.cross else ("ka", "va")):
                    slot_free[k][st.slot] = (box["pv"],)
            return steps + [close]

        onT_ring = Ring(onT)

        stat_free = [(), ()]

        def norm_stats(t, src, ready, k):
            m = DVE.mark(lambda e: e.bn_stats(stat[:, k, :], src), ready, *stat_free[k])
            m = DVE.mark(lambda e: e.bn_aggr(mv[:, t, :], stat[:, k, :]), m)
            stat_free[k] = (m,)
            return m

        def norm_scale(t0, n, ready):
            m = ACTE.mark(lambda e: e.activation(sdev[:, t0:t0 + n], mv[:, t0:t0 + n, 1], ACT.Sqrt,
                                                 bias=epsc[:, 0:1]), ready, const_ok)
            return DVE.mark(lambda e: e.reciprocal(rstd[:, t0:t0 + n], sdev[:, t0:t0 + n]), m)

        def norm_apply(t, scaled, g, b, dst=None):
            src = res[:, t, :]
            dst = src if dst is None else dst
            m = DVE.mark(lambda e: e.scalar_tensor_tensor(
                src, src, mv[:, t, 0:1], param[:, g, :], ALU.subtract, ALU.mult), scaled, par_in)
            return DVE.mark(lambda e: e.scalar_tensor_tensor(
                dst, src, rstd[:, t:t + 1], param[:, b, :], ALU.mult, ALU.add), m)

        def project_out_steps(b, w_o, w_ok, bo, g, bn, say):
            box = {}

            def turn(t):
                i, bank, bfree = banks.next()
                PE.wait(onat_ok[b], *bfree)
                for c in range(KC):
                    m = (PE.mark if c == KC - 1 else PE.do)(lambda e, c=c: e.transpose(
                        bank[:, c * P:(c + 1) * P], onat[b][:, t, c * P:(c + 1) * P], ident[:, :]))
                onat_free[b] = (m,)
                oi, o, ofree = onT_ring.next()
                cp = ACTE.mark(lambda e: e.copy(o, bank[:, 0:D].rearrange("p (c n) -> p c n", c=KC)), m, *ofree)
                banks.release(i, cp)
                box[t] = (oi, o, cp)

            def tile(t):
                tt = b * TB + t
                m_b = POOL.mark(lambda e: e.tensor_tensor(res[:, tt, :], res[:, tt, :], param[:, bo, :], ALU.add),
                                par_in, *x_t_src_free[b])
                oi, o, cp = box[t]
                i, bank2, bfree = banks.next()
                PE.wait(cp, w_ok, *bfree)
                for c in range(KC):
                    m = (PE.mark if c == KC - 1 else PE.do)(lambda e, c=c: e.matmul(
                        bank2[:, 0:D], o[:, c, :], w_o[:, c, :], start=(c == 0), stop=(c == KC - 1)))
                onT_ring.release(oi, m)
                s = DVE.mark(lambda e: e.tensor_tensor(res[:, tt, :], bank2[:, 0:D], res[:, tt, :], ALU.add), m, m_b)
                banks.release(i, s)
                box["s"] = norm_stats(tt, res[:, tt, :], s, t % 2)

            def scale():
                box["r"] = norm_scale(b * TB, TB, box["s"])

            def apply(t):
                say[t] = norm_apply(b * TB + t, box["r"], g, bn)

            tiles = [lambda: turn(0)]
            for t in range(TB):
                if t + 1 < TB:
                    tiles.append(lambda t=t: turn(t + 1))
                tiles.append(lambda t=t: tile(t))
            return (tiles + [scale]
                    + [lambda t=t: apply(t) for t in range(TB)])

        x_t_src_free = {}
        xt_ok = {}

        def turn_steps(b, ready):
            say = [None] * TB
            xt_ok[b] = say

            def note():
                x_t_src_free[b] = tuple(say)
                x_t_free[0] = ()
            return x_t_steps(b, ready, say) + [note]

        def x_src(st):
            return (lambda c, n0, w: xT[:, c, n0:n0 + w],
                    lambda n0, w: xt_ok[st.b][n0 // P:(n0 + w) // P])

        def ctx_src(st):
            return lambda c, n0, w: ctxT[:, st.b, c, n0:n0 + w], lambda n0, w: ctx_ok

        def qk_steps(st):
            src, ok = x_src(st)
            w, w_ok = (w_cross, wc_in) if st.cross else (w_self, w_in)
            ksrc, kok = ctx_src(st) if st.cross else (src, ok)
            return (project_steps(st, 1, ksrc, st.keys, kok, w[1], w_ok)
                    + project_steps(st, 0, src, S, ok, w[0], w_ok))

        def vl_steps(st):
            src, ok = ctx_src(st) if st.cross else x_src(st)
            w, w_ok, row = (w_cross, wc_in, C_BV) if st.cross else (w_self, w_in, A_BV)
            return [lambda: [load() for load in st.loads]] + v_steps(st, src, ok, w[2], w_ok, row)

        ctx_ok = []

        def ctx_steps():
            def step(b):
                i, bank, bfree = banks.next()
                PE.wait(wc_in, id_ok, *bfree)
                for c in range(KC):
                    m = (PE.mark if c == KC - 1 else PE.do)(lambda e, c=c: e.transpose(
                        bank[:, c * P:c * P + SE], ctxn[0:SE, b, c * P:(c + 1) * P], ident[0:SE, 0:SE]))
                d = DVE.mark(lambda e: e.tensor_copy(
                    ctxT[:, b, :, :], bank[:, 0:KC * P].rearrange("p (c n) -> p c n", c=KC)[:, :, 0:SE]), m)
                banks.release(i, d)
                ctx_ok.append(d)
                ot_ring.release(0, d)
            return [lambda b=b: step(b) for b in range(B)]

        stages = [Stage(n, n >= 4, (n // 2) % 2, n % 2) for n in range(8)]
        norm1 = [[None] * TB for _ in range(B)]
        norm2 = [[None] * TB for _ in range(B)]
        out1 = lambda b: project_out_steps(b, w_self[3], w_in, A_BO, G1, B1N, norm1[b])
        s_tok = stream("tokens")
        tokens_in = []

        def keep(b):
            for to in (tokens_d, sums_d):
                tokens_in[:] = [SP.dma(lambda e, to=to: e.dma_start(
                    to[b * S:(b + 1) * S, :].rearrange("(t p) n -> p t n", p=P),
                    res[:, b * TB:(b + 1) * TB, :]), s_tok, norm2[b][TB - 1])]

        out2 = lambda b: project_out_steps(b, w_cross[3], wc_in, C_BO, G2, B2N, norm2[b]) + [lambda: keep(b)]
        w1_v = w1.rearrange("e (c p) f -> p e c f", p=P)
        w2_v = w2.rearrange("e (c p) n -> p e c n", p=P)
        w1_s = w1_sb.rearrange("p (e c f) -> p e c f", e=E, c=KC)
        w2_s = w2_sb.rearrange("p (e c n) -> p e c n", e=E, c=FC)

        NE = NT * E
        spare = [0]

        def table(n, dt=f32):
            words = n // 2 if dt is bf16 else n
            a = spare[0]
            spare[0] += words
            assert spare[0] <= MORE
            return more[:, a:a + words].bitcast(dt)

        NK = 2 * NT
        KINDS = 6
        spare[0] = 10240
        lg = table(NE).rearrange("p (t e) -> p t e", t=NT)
        top = table(NE).rearrange("p (t e) -> p t e", t=NT)
        topi = table(NE, u32).rearrange("p (t e) -> p t e", t=NT)
        ex_l = table(NE).rearrange("p (t e) -> p t e", t=NT)
        oh = table(2 * NE).rearrange("p (k t e) -> p k t e", k=2, t=NT)
        tri, ones = table(P), table(P)
        cmp_j = table(NSLOT * E)[0:1, :].rearrange("p (j e) -> p j e", j=NSLOT)
        spare[0] = 0
        hot_s = table(NK * P, bf16).rearrange("p (n s) -> p n s", n=NK)
        hot_j = table(NK * NSLOT).rearrange("p (n j) -> p n j", n=NK)
        val_j = table(NK * KINDS * NSLOT, bf16).rearrange("p (n k j) -> p n k j", n=NK, k=KINDS)
        iota_s = table(P)
        iota_jj = table(NSLOT)
        inv = table(KINDS * NSLOT).rearrange("p (k j) -> p k j", k=KINDS)
        assert spare[0] <= 10240
        pr = sb("top_prob", [P, NT, 2])
        topf = sb("top_index_f", [P, NT, 2])
        logits = []

        def router_steps(b):
            box = {}

            def turn(t):
                i, bank, bfree = banks.next()
                PE.wait(norm2[b][t], *bfree)
                for c in range(KC):
                    m = (PE.mark if c == KC - 1 else PE.do)(lambda e, c=c: e.transpose(
                        bank[:, c * P:(c + 1) * P], res[:, b * TB + t, c * P:(c + 1) * P], ident[:, :]))
                xi, xt, xfree = onT_ring.next()
                cp = ACTE.mark(lambda e: e.copy(xt, bank[:, 0:D].rearrange("p (c n) -> p c n", c=KC)), m, *xfree)
                banks.release(i, cp)
                box[t] = (xi, xt, cp)

            def multiply(t):
                xi, xt, cp = box[t]
                i, bank, bfree = banks.next()
                PE.wait(cp, wc_in, *bfree)
                for c in range(KC):
                    m = (PE.mark if c == KC - 1 else PE.do)(lambda e, c=c: e.matmul(
                        bank[:, 0:E], xt[:, c, :], rw[:, c, :], start=(c == 0), stop=(c == KC - 1)))
                onT_ring.release(xi, m)
                tt = b * TB + t
                m = DVE.mark(lambda e: e.tensor_tensor(lg[:, tt, :], bank[:, 0:E], rbias[:, :], ALU.add), m, par_in)
                banks.release(i, m)
                m = DVE.mark(lambda e: e.max(top[:, tt, :], lg[:, tt, :]), m)
                logits[:] = [DVE.mark(lambda e: e.max_index(topi[:, tt, :], top[:, tt, :], lg[:, tt, :]), m)]

            steps = [lambda: turn(0)]
            for t in range(TB):
                if t + 1 < TB:
                    steps.append(lambda t=t: turn(t + 1))
                steps.append(lambda t=t: multiply(t))
            return steps

        first_max = max_steps(stages[0])
        cut_at = stages[0].second_max_at
        for s in (turn_steps(0, [x_in[0]] * TB) + qk_steps(stages[0]) + vl_steps(stages[0])
                  + qk_steps(stages[1]) + ctx_steps() + first_max[:cut_at]):
            s()
        first = attend_steps(stages[0])
        at_g1 = stages[0].second_group_at
        interleave(first[:at_g1], first_max[cut_at:], 1.0)
        interleave(first[at_g1:], vl_steps(stages[1]) + turn_steps(1, [x_in[1]] * TB)
                   + qk_steps(stages[2]) + max_steps(stages[1]))
        interleave(attend_steps(stages[1]), vl_steps(stages[2]) + qk_steps(stages[3]) + max_steps(stages[2]))
        interleave(attend_steps(stages[2]), vl_steps(stages[3]) + out1(0) + turn_steps(0, norm1[0])
                   + qk_steps(stages[4]) + max_steps(stages[3]))
        interleave(attend_steps(stages[3]), vl_steps(stages[4]) + qk_steps(stages[5]) + max_steps(stages[4]))
        interleave(attend_steps(stages[4]), vl_steps(stages[5]) + out1(1) + max_steps(stages[5])
                   + turn_steps(1, norm1[1]) + qk_steps(stages[6]))
        self_done = Mark(PE.sem, PE.count)
        s_e = stream("w1_early")
        early = 2 * (HH * S // 2 + TB * HH * VW) // EW + 1
        got_early = []

        def early_load(ex):
            got_early[:] = [SP.dma(lambda e: e.dma_start(w1_s[:, ex], w1_v[:, ex]), s_e, self_done)]

        def spread(steps, loads):
            n = max(1, len(steps) // (len(loads) + 1))
            return [x for k, step in enumerate(steps)
                    for x in ([step] + ([loads.pop(0)] if loads and k % n == n - 1 else []))] + loads

        loads = [lambda ex=ex: early_load(ex) for ex in range(early)]
        interleave(attend_steps(stages[5]), spread(
            vl_steps(stages[6]) + qk_steps(stages[7]) + max_steps(stages[6]), loads[:early // 2]))
        interleave(attend_steps(stages[6]), spread(
            vl_steps(stages[7]) + max_steps(stages[7]) + out2(0), loads[early // 2:]))
        interleave(attend_steps(stages[7]), router_steps(0), 1.0)
        early_in = got_early[0]
        attend_done = (Mark(PE.sem, PE.count), pt_done[0])
        s_l = stream("w_late")
        for ex in range(early, E):
            late_in = SP.dma(lambda e, ex=ex: e.dma_start(w1_s[:, ex], w1_v[:, ex]), s_l, *attend_done)
        for ex in range(E - 1):
            late_in = SP.dma(lambda e, ex=ex: e.dma_start(w2_s[:, ex], w2_v[:, ex]), s_l, *attend_done)
        for s in out2(1) + router_steps(1):
            s()
        attention_done = Mark(PE.sem, PE.count)
        cp = Mark(ACTE.sem, ACTE.count)
        last_kept = Mark(DVE.sem, DVE.count)


        s_last = stream("w_last")
        last_in = SP.dma(lambda e: e.dma_start(w2_s[:, E - 1], w2_v[:, E - 1]), s_last, attention_done, cp)

        rs = sb("prob_recip", [P, NT])
        dw = sb("weight_tmp", [P, NT])
        wgt = sb("combine", [P, 2, NT])
        iota_e = sb("iota_e", [P, E])
        cnt = sb("tile_counts", [P, NT + 1, E])
        rank = sb("rank", [P, NT, E])
        tmp = sb("rank_tmp", [P, NT, E])
        ntot = sb("n_expert", [P, E])
        ntile = sb("tiles_expert", [P, E], i32)
        ntile_f = sb("tiles_expert_f", [P, E])
        tinc = sb("tiles_upto", [P, E])
        base = sb("slot_base", [P, E])
        posf = sb("slot_f", [P, 2, NT])
        pos = sb("slot", [P, 2, NT], i32)
        pos_p = sb("slot_parts", [P, 2, NK], i32)
        pos_pf = sb("slot_parts_f", [P, 2, NK])
        kinds = sb("kinds", [P, 5, NK], bf16)
        ids = sb("token_ids", [P, NSLOT])
        dummy = sb("dummy_ids", [P, NSLOT])
        rows_in = sb("gather_rows", [P, NSLOT], i32)
        rows_out = sb("scatter_rows", [P, NSLOT], i32)
        w_slot = sb("slot_weight", [P, NSLOT])
        w_rest = sb("weight_rest", [P, NK])
        slot_no = sb("slot_no", [P, 1])
        iota_j = sb("iota_j", [1, NSLOT])
        ejf = sb("tile_expert_f", [1, NSLOT])
        ej = sb("tile_expert", [1, NSLOT], i32)

        def numbers(dst, pattern, base=0, by_partition=0, *after):
            return POOL.mark(lambda e: e.iota(dst, pattern, base=base, channel_multiplier=by_partition,
                                              allow_small_or_imprecise_dtypes=True), *after)

        router_free = (attention_done, cp, norm2[1][-1], last_kept)
        io1 = numbers(iota_e[:, :], [[1, E]])
        io2 = numbers(iota_j[:, :], [[1, NSLOT]])
        numbers(slot_no[:, :], [[0, 1]], T, 1)
        numbers(kinds[:, 0, :], [[0, 2], [1, NT]])
        numbers(kinds[:, 1, :], [[0, NK]], 0, 1)
        numbers(iota_s, [[1, P]], 0, 0, *router_free)
        io3 = numbers(iota_jj, [[1, NSLOT]])
        one_ok = POOL.mark(lambda e: e.memset(ones[:, :], 1.0))
        tri_ok = POOL.mark(lambda e: e.affine_select(
            out=tri[:, :], in_=ones[:, :], compare_op=ALU.is_gt, fill=0.0, base=0,
            pattern=[[1, P]], channel_multiplier=-1), one_ok)

        def bc(ap, shape):
            return ap.to_broadcast(shape)

        m = m2 = logits[0]
        m = DVE.mark(lambda e: e.tensor_tensor(lg[:, :, :], lg[:, :, :], bc(top[:, :, 0:1], [P, NT, E]),
                                               ALU.subtract), m2)
        m = DVE.mark(lambda e: e.tensor_tensor(pr[:, :, :], top[:, :, 0:2], bc(top[:, :, 0:1], [P, NT, 2]),
                                               ALU.subtract), m)
        xm = ACTE.mark(lambda e: e.activation(ex_l[:, :, :], lg[:, :, :], ACT.Exp), m)
        xm = ACTE.mark(lambda e: e.activation(pr[:, :, :], pr[:, :, :], ACT.Exp))
        m = DVE.mark(lambda e: e.tensor_reduce(rs[:, :], ex_l[:, :, :], AX.X, ALU.add), xm)
        m = DVE.mark(lambda e: e.reciprocal(rs[:, :], rs[:, :]), m)
        m = DVE.mark(lambda e: e.tensor_tensor(
            pr[:, :, :], pr[:, :, :], bc(rs[:, :].rearrange("p (t o) -> p t o", o=1), [P, NT, 2]), ALU.mult), m)
        m = DVE.mark(lambda e: e.tensor_tensor(dw[:, :], pr[:, :, 1], pr[:, :, 0], ALU.subtract), m)
        xm = ACTE.mark(lambda e: e.activation(wgt[:, 1, :], dw[:, :], ACT.Exp), m)
        m = DVE.mark(lambda e: e.tensor_scalar(dw[:, :], wgt[:, 1, :], 1.0, None, ALU.add), xm)
        m = DVE.mark(lambda e: e.reciprocal(wgt[:, 0, :], dw[:, :]), m)
        wgt_ok = DVE.mark(lambda e: e.tensor_tensor(wgt[:, 1, :], wgt[:, 1, :], wgt[:, 0, :], ALU.mult), m)
        m = DVE.mark(lambda e: e.tensor_copy(topf[:, :, :], topi[:, :, 0:2]), m2)
        for k in range(2):
            mo = DVE.mark(lambda e, k=k: e.tensor_tensor(
                oh[:, k, :, :], bc(iota_e[:, :].rearrange("p (o e) -> p o e", o=1), [P, NT, E]),
                bc(topf[:, :, k:k + 1], [P, NT, E]), ALU.is_equal), m, io1)
        both = DVE.mark(lambda e: e.tensor_tensor(tmp[:, :, :], oh[:, 0, :, :], oh[:, 1, :, :], ALU.add), mo)
        m = DVE.mark(lambda e: e.memset(cnt[:, 0, :], 0.0))
        for t in range(NT):
            m = DVE.mark(lambda e, t=t: e.tensor_tensor(cnt[:, t + 1, :], cnt[:, t, :], tmp[:, t, :], ALU.add),
                         m, both)
        ri_, rbank, rfree = banks.next()
        PE.wait(m, tri_ok, *rfree)
        PE.do(lambda e: e.matmul(rbank[:, 0:NE], tri[:, :], tmp[:, :, :].rearrange("p t e -> p (t e)"),
                                 start=True, stop=False))
        PE.do(lambda e: e.matmul(rbank[:, 0:NE], ones[:, :],
                                 cnt[:, 0:NT, :].rearrange("p t e -> p (t e)"), start=False, stop=True))
        pm_m = PE.mark(lambda e: e.matmul(rbank[:, NE:NE + E], ones[:, :], cnt[:, NT, :], start=True, stop=True))
        m = DVE.mark(lambda e: e.tensor_copy(rank[:, :, :], rbank[:, 0:NE].rearrange("p (t e) -> p t e", t=NT)), pm_m)
        m = DVE.mark(lambda e: e.tensor_scalar(ntot[:, :], rbank[:, NE:NE + E], float(P - 1), None, ALU.add), m)
        rank_read = m
        m = DVE.mark(lambda e: e.tensor_copy(ntile[:, :], ntot[:, :]), m)
        m = DVE.mark(lambda e: e.tensor_scalar(ntile[:, :], ntile[:, :], 7, None, ALU.arith_shift_right), m)
        m = DVE.mark(lambda e: e.tensor_copy(ntile_f[:, :], ntile[:, :]), m)
        m = DVE.mark(lambda e: e.tensor_copy(tinc[:, 0:1], ntile_f[:, 0:1]), m)
        for ex in range(1, E):
            m = DVE.mark(lambda e, ex=ex: e.tensor_tensor(tinc[:, ex:ex + 1], tinc[:, ex - 1:ex],
                                                          ntile_f[:, ex:ex + 1], ALU.add), m)
        tinc_ok = m
        m = DVE.mark(lambda e: e.tensor_tensor(base[:, :], tinc[:, :], ntile_f[:, :], ALU.subtract), m)
        m = DVE.mark(lambda e: e.tensor_scalar(base[:, :], base[:, :], float(P), None, ALU.mult), m)
        m = DVE.mark(lambda e: e.tensor_tensor(rank[:, :, :], rank[:, :, :],
                                               bc(base[:, :].rearrange("p (o e) -> p o e", o=1), [P, NT, E]),
                                               ALU.add), m)
        for k in range(2):
            m = DVE.mark(lambda e, k=k: e.tensor_tensor(tmp[:, :, :], oh[:, k, :, :], rank[:, :, :], ALU.mult), m, pm_m)
            m = DVE.mark(lambda e, k=k: e.tensor_reduce(posf[:, k, :], tmp[:, :, :], AX.X, ALU.add), m)
        pos_ok = DVE.mark(lambda e: e.tensor_copy(pos[:, :, :], posf[:, :, :]), m)
        m = DVE.mark(lambda e: e.tensor_tensor(
            cmp_j[:, :, :], bc(iota_j[:, :].rearrange("p (j o) -> p j o", o=1), [1, NSLOT, E]),
            bc(tinc[0:1, :].rearrange("p (o e) -> p o e", o=1), [1, NSLOT, E]), ALU.is_ge), tinc_ok, io2, pos_ok)
        m = DVE.mark(lambda e: e.tensor_reduce(ejf[:, :], cmp_j[:, :, :], AX.X, ALU.add), m)
        m = DVE.mark(lambda e: e.tensor_scalar(ejf[:, :], ejf[:, :], float(E - 1), None, ALU.min), m)
        ej_ok = DVE.mark(lambda e: e.tensor_copy(ej[:, :], ejf[:, :]), m)

        m = DVE.mark(lambda e: e.tensor_scalar(
            pos_p[:, 0, :], pos[:, :, :].rearrange("p k t -> p (k t)"), P - 1, None, ALU.bitwise_and), pos_ok)
        m = DVE.mark(lambda e: e.tensor_scalar(
            pos_p[:, 1, :], pos[:, :, :].rearrange("p k t -> p (k t)"), 7, None, ALU.arith_shift_right), m)
        m = DVE.mark(lambda e: e.tensor_copy(pos_pf[:, :, :], pos_p[:, :, :]), m)
        hs = DVE.mark(lambda e: e.tensor_tensor(
            hot_s, bc(iota_s.rearrange("p (o s) -> p o s", o=1), [P, NK, P]),
            bc(pos_pf[:, 0, :].rearrange("p (n o) -> p n o", o=1), [P, NK, P]), ALU.is_equal), m, io3, *router_free)
        hj = DVE.mark(lambda e: e.tensor_tensor(
            hot_j, bc(iota_jj.rearrange("p (o j) -> p o j", o=1), [P, NK, NSLOT]),
            bc(pos_pf[:, 1, :].rearrange("p (n o) -> p n o", o=1), [P, NK, NSLOT]), ALU.is_equal), m, io3)
        wflat = wgt[:, :, :].rearrange("p k t -> p (k t)")
        m = DVE.mark(lambda e: e.tensor_copy(kinds[:, 2, :], wflat), wgt_ok)
        m = DVE.mark(lambda e: e.tensor_tensor(w_rest[:, :], wflat, kinds[:, 2, :], ALU.subtract), m)
        m = DVE.mark(lambda e: e.tensor_copy(kinds[:, 3, :], w_rest[:, :]), m)
        m = DVE.mark(lambda e: e.tensor_tensor(kinds[:, 4, :], w_rest[:, :], kinds[:, 3, :], ALU.subtract), m)
        for k in range(5):
            on = POOL if k in (1, 3) else DVE
            vals = on.mark(lambda e, k=k: e.tensor_tensor(
                val_j[:, :, k, :], hot_j, bc(kinds[:, k, :].rearrange("p (n o) -> p n o", o=1), [P, NK, NSLOT]),
                ALU.mult), m, hj, io3)
            if on is POOL:
                vals_pool = vals
        vals_last = ACTE.mark(lambda e: e.copy(val_j[:, :, 5, :], hot_j), hj)
        i, ibank, ifree = banks.next()
        PE.wait(vals, vals_pool, vals_last, hs, *ifree)
        for n in range(NK):
            m = (PE.mark if n == NK - 1 else PE.do)(lambda e, n=n: e.matmul(
                ibank[:, 0:KINDS * NSLOT], hot_s[:, n, :], val_j[:, n, :, :].rearrange("p k j -> p (k j)"),
                start=(n == 0), stop=(n == NK - 1)))
        inv_m = DVE.mark(lambda e: e.tensor_copy(inv, ibank[:, 0:KINDS * NSLOT].rearrange("p (k j) -> p k j", k=KINDS)), m)
        m = DVE.mark(lambda e: e.scalar_tensor_tensor(ids[:, :], inv[:, 0, :], float(P), inv[:, 1, :],
                                                      ALU.mult, ALU.add), inv_m)
        rows_ok = DVE.mark(lambda e: e.tensor_copy(rows_in[:, :], ids[:, :]), m)
        m2 = DVE.mark(lambda e: e.tensor_scalar(dummy[:, :], inv[:, 5, :], -1.0, 1.0, ALU.mult, ALU.add), inv_m)
        m2 = DVE.mark(lambda e: e.scalar_tensor_tensor(ids[:, :], dummy[:, :], slot_no[:, 0:1], ids[:, :],
                                                       ALU.mult, ALU.add), m2, rows_ok, io3)
        m2 = DVE.mark(lambda e: e.tensor_copy(rows_out[:, :], ids[:, :]), m2)
        m2 = DVE.mark(lambda e: e.tensor_tensor(w_slot[:, :], inv[:, 2, :], inv[:, 3, :], ALU.add), m2)
        slots_ok = DVE.mark(lambda e: e.tensor_tensor(w_slot[:, :], w_slot[:, :], inv[:, 4, :], ALU.add), m2)

        mbanks = Ring(work + [st2[1][:, 0, :], st2[1][:, 1, :], o_ps[:, :]])
        mbanks.free = [(rank_read, inv_m)] * 3 + [pairs.free[0] + pairs.free[1]] * 2 + [o_free[0]]
        y_free_bank = st2[0]
        hid_ring, act_ring, hidT_ring = Ring(hid), Ring(act), Ring(hidT)
        sx_ring, sxT_ring, b12_ring, sy_ring = Ring(slot_x), Ring(slot_xT), Ring(bias12), Ring(slot_y)
        ybanks = Ring([st2[0][:, 0, :], st2[0][:, 1, :]])
        ybanks.free = [pairs.free[0] + pairs.free[1]] * 2
        s_sx = [stream("slot_x") for _ in slot_x]
        s_b12 = [stream("bias") for _ in bias12]
        s_sy = [stream("slot_y") for _ in slot_y]
        more_free = (attention_done, cp, norm2[0][-1], norm2[1][-1], zeros_in, slots_ok, vals_last, vals_pool)
        tiles = [dict() for _ in range(NSLOT)]

        def load(j):
            t = tiles[j]
            t["xi"], t["x"], free = sx_ring.next()
            t["x_in"] = POOL.dma(lambda e: e.indirect_dma_start(
                t["x"], None, tokens_d, bass.IndirectOffsetOnAxis(ap=rows_in[:, j:j + 1], axis=0)),
                s_sx[t["xi"]], rows_ok, *tokens_in, *more_free, *free)
            t["bi"], t["b"], free = b12_ring.next()
            SP.wait(ej_ok, *more_free, *free)

            def biases(e, which):
                if which == 0:
                    t["ex"] = e.value_load(ej[0:1, j:j + 1], min_val=0, max_val=E - 1)
                    return e.dma_start(t["b"][:, 0:FF], b1[bass.ds(t["ex"], 1), :].to_broadcast([P, FF]))
                return e.dma_start(t["b"][:, FF:FF + D], b2[bass.ds(t["ex"], 1), :].to_broadcast([P, D]))
            SP.dma(lambda e: biases(e, 0), s_b12[t["bi"]])
            t["b_in"] = SP.dma(lambda e: biases(e, 1), s_b12[t["bi"]])

        def turn(j):
            t = tiles[j]
            i, bank, bfree = mbanks.next()
            PE.wait(t["x_in"], *bfree)
            for c in range(KC):
                m = (PE.mark if c == KC - 1 else PE.do)(lambda e, c=c: e.transpose(
                    bank[:, c * P:(c + 1) * P], t["x"][:, c * P:(c + 1) * P], ident[:, :]))
            sx_ring.release(t["xi"], m)
            t["xTi"], t["xT"], free = sxT_ring.next()
            t["xT_ok"] = ACTE.mark(lambda e: e.copy(
                t["xT"], bank[:, 0:D].rearrange("p (c n) -> p c n", c=KC)), m, *free)
            mbanks.release(i, t["xT_ok"])

        def up(j):
            t = tiles[j]
            PE.wait(t["xT_ok"], ej_ok, early_in, late_in, last_in)
            hi, hd, hfree = hid_ring.next()

            def first(e):
                t["ex_pe"] = e.value_load(ej[0:1, j:j + 1], min_val=0, max_val=E - 1)
            for n in range(FF // BANK):
                i, bank, bfree = mbanks.next()
                PE.wait(*bfree)
                for c in range(KC):
                    def mm(e, n=n, c=c, bank=bank):
                        if n == 0 and c == 0:
                            first(e)
                        return e.matmul(bank, t["xT"][:, c, :],
                                        w1_sb[:, bass.ds(t["ex_pe"] * EW + (c * FF + n * BANK), BANK)],
                                        start=(c == 0), stop=(c == KC - 1))
                    m = (PE.mark if c == KC - 1 else PE.do)(mm)
                d = DVE.mark(lambda e, n=n, bank=bank: e.tensor_tensor(
                    hd[:, n * BANK:(n + 1) * BANK], bank, t["b"][:, n * BANK:(n + 1) * BANK], ALU.add),
                    m, t["b_in"], *hfree)
                mbanks.release(i, d)
            sxT_ring.release(t["xTi"], m)
            ai, t["act"], afree = act_ring.next()
            t["ai"] = ai
            t["act_ok"] = ACTE.mark(lambda e: e.activation(t["act"], hd, ACT.Gelu), d, *afree)
            hid_ring.release(hi, t["act_ok"])

        def turn_hidden(j):
            t = tiles[j]
            t["hTi"], t["hT"], tfree = hidT_ring.next()
            hT = t["hT"]
            PE.wait(t["act_ok"])
            for half in range(2):
                i, bank, bfree = mbanks.next()
                PE.wait(*bfree)
                for q in range(4):
                    c = half * 4 + q
                    m = (PE.mark if q == 3 else PE.do)(lambda e, q=q, c=c, bank=bank: e.transpose(
                        bank[:, q * P:(q + 1) * P], t["act"][:, c * P:(c + 1) * P], ident[:, :]))
                src = bank.rearrange("p (c n) -> p c n", c=4)
                dst = hT[:, half * 4:half * 4 + 4, :]
                if half == 0:
                    a = ACTE.mark(lambda e, src=src, dst=dst: e.copy(dst, src), m, *tfree)
                else:
                    a = DVE.mark(lambda e, src=src, dst=dst: e.tensor_copy(dst, src), m, *tfree)
                mbanks.release(i, a)
                t["h", half] = a
            act_ring.release(t["ai"], m)

        def down(j):
            t = tiles[j]
            hT = t["hT"]
            i, bank, bfree = ybanks.next()
            PE.wait(*bfree)
            for c in range(FC):
                PE.wait(t["h", c // 4])
                m = (PE.mark if c == FC - 1 else PE.do)(lambda e, c=c: e.matmul(
                    bank[:, 0:D], hT[:, c, :], w2_sb[:, bass.ds(t["ex_pe"] * EW + c * D, D)],
                    start=(c == 0), stop=(c == FC - 1)))
            hidT_ring.release(t["hTi"], m)
            yi, y, yfree = sy_ring.next()
            d = DVE.mark(lambda e: e.tensor_tensor(y, bank[:, 0:D], t["b"][:, FF:FF + D], ALU.add), m, *yfree)
            ybanks.release(i, d)
            b12_ring.release(t["bi"], d)
            t["y"], t["yi"] = y, yi
            t["y_ok"] = DVE.mark(lambda e: e.tensor_scalar(y, y, w_slot[:, j:j + 1], None, ALU.mult), d)

        def add_up(j):
            t = tiles[j]
            t["added"] = POOL.dma(lambda e: e.indirect_dma_start(
                sums_d, bass.IndirectOffsetOnAxis(ap=rows_out[:, j:j + 1], axis=0), t["y"], None,
                compute_op=ALU.add), s_sy[t["yi"]], t["y_ok"], slots_ok,
                *([tiles[j - 1]["added"]] if j else [*tokens_in, zeros_in]))
            sy_ring.release(t["yi"], t["added"])

        DVE.wait(*more_free)
        ACTE.wait(*more_free)
        load(0)
        turn(0)
        load(1)
        for j in range(NSLOT):
            if j + 1 < NSLOT:
                turn(j + 1)
            if j >= 1:
                turn_hidden(j - 1)
            up(j)
            if j >= 1:
                down(j - 1)
            if j + 2 < NSLOT:
                load(j + 2)
            if j >= 1:
                add_up(j - 1)
        turn_hidden(NSLOT - 1)
        down(NSLOT - 1)
        add_up(NSLOT - 1)

        PIECE = 4
        s_out = stream("out")
        s_back = [stream("sums") for _ in range(NT // PIECE)]
        rows = lambda ap, t: ap[t * P:(t + PIECE) * P, :].rearrange("(t p) n -> p t n", p=P)
        back = [SP.dma(lambda e, n=n: e.dma_start(res[:, n * PIECE:(n + 1) * PIECE, :], rows(sums_d, n * PIECE)),
                       s_back[n], tiles[NSLOT - 1]["added"]) for n in range(NT // PIECE)]
        flat_out = out.rearrange("b s n -> (b s) n")
        last = []

        def finish(n):
            for t in range(n * PIECE, (n + 1) * PIECE):
                m = norm_apply(t, last[n], G3, B3N)
            last[n] = SP.dma(lambda e: e.dma_start(rows(flat_out, n * PIECE),
                                                   res[:, n * PIECE:(n + 1) * PIECE, :]), s_out, m)

        for n in range(NT // PIECE):
            for t in range(n * PIECE, (n + 1) * PIECE):
                m = norm_stats(t, res[:, t, :], back[n], t % 2)
            last.append(norm_scale(n * PIECE, PIECE, m))
            if n:
                finish(n - 1)
        finish(NT // PIECE - 1)
        SP.wait(last[-1])

        block = stack.enter_context(nc.Block())

        @block.tensor
        def _(e):
            PE.run(e)

        @block.scalar
        def _(e):
            ACTE.run(e)

        @block.vector
        def _(e):
            DVE.run(e)

        @block.gpsimd
        def _(e):
            POOL.run(e)

        @block.sync
        def _(e):
            SP.run(e)


def kernel(**inputs):
    import concourse.bacc as bacc
    from concourse.bass_utils import run_bass_kernel_spmd

    nc = bacc.Bacc("TRN2", target_bir_lowering=False, num_devices=1)
    arrays, ap = {}, {}
    for name, value in inputs.items():
        a = np.ascontiguousarray(value)
        arrays[f"in_{name}"] = a
        ap[name.removeprefix("L0_xattn_")] = nc.dram_tensor(
            f"in_{name}", a.shape, mybir.dt.from_np(a.dtype), kind="ExternalInput").ap()
    out = nc.dram_tensor("out_0", (B, S, D), mybir.dt.float32, kind="ExternalOutput").ap()
    par = {
        "bq": (ap["sa_bq"], ap["ca_bq"]), "bk": (ap["sa_bk"], ap["ca_bk"]), "rb": ap["router_b"],
        "rows": [ap[n] for n in ("sa_bv", "sa_bo", "ca_bv", "ca_bo", "ln1_g", "ln1_b",
                                 "ln2_g", "ln2_b", "ln3_g", "ln3_b")],
    }
    wts = [ap[f"{a}_w{w}"] for a in ("sa", "ca") for w in "qkvo"]
    build(nc, ap["x"], ap["ctx_1024"], par, wts, ap["router_w"], ap["e_w1"], ap["e_b1"],
          ap["e_w2"], ap["e_b2"], out)
    r = run_bass_kernel_spmd(nc, [arrays], core_ids=[0])
    return r.results[0]["out_0"]
```

```python
from contextlib import ExitStack, contextmanager

import numpy as np

import concourse.bass as bass
from concourse import mybir

P = 128
B, S, D = 2, 1024, 256
SE = 77
H, HD = 16, 16
E, FF = 8, 1024
EPS = 1e-5
KC = D // P
FC = FF // P
T = B * S
NT = T // P
TB = S // P
HH = P // HD
QUAD = 4
QG = 512
NG = S // QG
BANK = 512
VW = 2 * HD
Q_PART = (0, 0, 1, 1, 0, 2)
K_PART = (0, 1, 0, 1, 2, 0)
NGR = len(Q_PART)
R_S = NGR * HD
R_M = R_S + 3
TWO_ONES = float(np.array([0x3F803F80], np.uint32).view(np.float32)[0])
NEG = -1e30
NSLOT = (2 * T + E * (P - 1)) // P
NSURE = 2 * T // P
NPARAM = 10
MORE = 11776


class Mark:

    def __init__(self, sem, value, maybe=False):
        self.sem, self.value, self.maybe = sem, value, maybe


class Engine:

    def __init__(self, sem):
        self.sem, self.count, self.queue, self.waited = sem, 0, [], {}

    def wait(self, *marks):
        for m in marks:
            if m is not None and self.waited.get(id(m.sem), 0) < m.value:
                self.waited[id(m.sem)] = m.value
                self.queue.append((m, None, 0))

    def do(self, call, *after):
        self.wait(*after)
        self.queue.append((call, None, 0))

    def mark(self, call, *after):
        self.wait(*after)
        self.count += 1
        self.queue.append((call, self.sem, 1))
        return Mark(self.sem, self.count)

    def dma(self, call, stream, *after):
        self.wait(*after)
        stream.count += 16
        self.queue.append((call, stream.sem, 16))
        return Mark(stream.sem, stream.count, stream.maybe)

    @contextmanager
    def only_if(self, test):
        outer, self.queue, before = self.queue, [], self.count
        yield
        group, self.queue = self.queue, outer

        def either(e):
            with e.If(test(self, e)):
                self.emit(e, group)
            with e.Else():
                if before:
                    e.wait_ge(self.sem, before)
                for call, sem, inc in group:
                    if isinstance(call, Mark):
                        if not call.maybe:
                            e.wait_ge(call.sem, call.value)
                    elif sem is self.sem:
                        e.sem_inc(sem, inc)
        if group:
            outer.append((either, None, 0))

    def emit(self, e, queue):
        for call, sem, inc in queue:
            if isinstance(call, Mark):
                e.wait_ge(call.sem, call.value)
                continue
            made = call(e)
            if sem is not None:
                made.then_inc(sem, inc)

    def run(self, e):
        self.emit(e, self.queue)


class Stream:

    def __init__(self, sem, maybe=False):
        self.sem, self.count, self.maybe = sem, 0, maybe


class Ring:

    def __init__(self, buffers):
        self.buffers, self.free, self.at = buffers, [()] * len(buffers), -1

    def next(self):
        self.at = (self.at + 1) % len(self.buffers)
        free, self.free[self.at] = self.free[self.at], None
        assert free is not None, "a buffer is taken again before it was given back"
        return self.at, self.buffers[self.at], free

    def release(self, i, *marks):
        self.free[i] = marks


def interleave(main, side, end=0.9):
    done = 0
    for i, step in enumerate(main):
        step()
        while done < min(len(side), len(side) * (i + 1) // (end * len(main))):
            side[done]()
            done += 1
    for step in side[done:]:
        step()


def mix(a, b):
    both = sorted([((i + 0.5) / len(a), 0, i) for i in range(len(a))]
                  + [((i + 0.5) / len(b), 1, i) for i in range(len(b))])
    return [(a, b)[which][i] for _, which, i in both]


def build(nc, x, ctx_in, par, wts, router_w, w1, b1, w2, b2, out):
    f32, bf16, i32, u32 = mybir.dt.float32, mybir.dt.bfloat16, mybir.dt.int32, mybir.dt.uint32
    ALU, ACT, AX = mybir.AluOpType, mybir.ActivationFunctionType, mybir.AxisListType
    stack = ExitStack()
    with stack:
        def sb(name, shape, dt=f32):
            return stack.enter_context(nc.sbuf_tensor(name, shape, dt))

        n_sem = [0]

        def stream(name, maybe=False):
            n_sem[0] += 1
            return Stream(stack.enter_context(nc.semaphore(f"dma_{name}_{n_sem[0]}")), maybe)

        PE, ACTE, DVE, POOL, SP = (Engine(stack.enter_context(nc.semaphore(f"done_{n}")))
                                   for n in ("pe", "act", "dve", "pool", "sp"))

        parts_d = nc.dram_tensor("parts_scratch", [2 * B * (H // HH), 2, 3, P, S], bf16, kind="Internal").ap()
        negm_d = nc.dram_tensor("negmax_scratch", [2 * B * (H // HH), 3, HH, S], bf16, kind="Internal").ap()
        tokens_d = nc.dram_tensor("tokens_scratch", [T, D], f32, kind="Internal").ap()
        sums_d = nc.dram_tensor("sums_scratch", [T + P, D], f32, kind="Internal").ap()

        res = sb("residual", [P, NT, D])
        param = sb("param_rows", [P, NPARAM, D])
        ident = sb("ident", [P, P])
        identb = sb("identb", [P, P], bf16)
        mask_qk = sb("mask_qk", [P, P], bf16)
        b1_rows = sb("expert_b1_rows", [E * FC, P])
        b1_col = sb("expert_b1_cols", [P, E * FC])
        b_qk = sb("b_qk", [P, 2, 2, KC])
        rbias = sb("router_bias", [P, E])
        rw = sb("router_w", [P, KC, E])
        epsc = sb("eps", [P, 1])
        stat = sb("stat", [P, 2, 6])
        mv = sb("mean_var", [P, NT, 2])
        rstd = sb("rstd", [P, NT])
        sdev = sb("sdev", [P, NT])
        shift = sb("minus_mean_scaled", [P, NT])
        pm = sb("part_max", [P, TB, HH, 2])
        negm = sb("neg_max", [P, TB, HH])
        negp = sb("neg_max_parts", [P, TB, 3, HH], bf16)
        negr = sb("neg_max_rest", [P, TB, HH])
        rsum = sb("recip_sum", [P, 2, QUAD, QUAD])
        (A_BV, A_BO, C_BV, C_BO, G1, B1N, G2, B2N, G3, B3N) = range(NPARAM)

        W_WORDS = 2 * E * KC * FF
        arena = sb("arena", [P, W_WORDS])
        more = sb("arena_more", [P, MORE])
        at = {"arena": 0, "more": 0}

        def cut(where, words):
            a = at[where]
            at[where] += words
            whole = arena if where == "arena" else more
            assert at[where] <= whole.shape[1], (where, at[where])
            return whole[:, a:a + words]

        def cut_bf(where, n):
            return cut(where, n // 2).bitcast(bf16)

        w1_sb = arena[:, 0:W_WORDS // 2]
        w2_sb = arena[:, W_WORDS // 2:W_WORDS]
        EW = KC * FF
        ka = [cut_bf("arena", HH * S).rearrange("p (h t) -> p h t", h=HH) for _ in range(2)]
        va = [cut("arena", TB * HH * VW).rearrange("p (k h v) -> p k h v", k=TB, h=HH) for _ in range(2)]
        w_self = [cut("arena", KC * D).rearrange("p (c n) -> p c n", c=KC) for _ in range(4)]
        qa = [cut_bf("arena", HH * S).rearrange("p (h t) -> p h t", h=HH) for _ in range(2)]
        pt = [cut("arena", 2 * QG).rearrange("p (j q) -> p j q", j=2) for _ in range(4)]
        f_sb = [cut("arena", S)]
        kac = [cut_bf("arena", HH * 80).rearrange("p (h t) -> p h t", h=HH) for _ in range(2)]
        vac = [cut("arena", HH * VW).rearrange("p (h v) -> p h v", h=HH) for _ in range(2)]
        ctxT = cut("arena", B * KC * SE).rearrange("p (b c n) -> p b c n", b=B, c=KC)
        w_cross = [cut("arena", KC * D).rearrange("p (c n) -> p c n", c=KC) for _ in range(3)]
        assert at["arena"] <= W_WORDS - EW
        at["arena"] = W_WORDS - EW
        w_cross.append(cut("arena", KC * D).rearrange("p (c n) -> p c n", c=KC))
        ot = [cut("arena", QG) for _ in range(2)]
        ctxn = ot[0].rearrange("p (b n) -> p b n", b=B)
        onT = [cut("arena", D).rearrange("p (c n) -> p c n", c=KC) for _ in range(2)]
        xT = cut("more", KC * T // 2).rearrange("p (c n) -> p c n", c=KC)
        onat = [cut("more", TB * D).rearrange("p (t n) -> p t n", t=TB) for _ in range(2)]
        part_sb = [[cut_bf("more", S) for _ in range(3)] for _ in range(2)]
        mT = cut_bf("more", S)
        zeros = cut("more", D)
        at["more"] = 0
        hid = [cut("more", FF).rearrange("p (c n) -> p c n", c=FC) for _ in range(2)]
        act = [cut("more", FF).rearrange("p (c n) -> p c n", c=FC) for _ in range(2)]
        slot_y = [cut("more", D) for _ in range(2)]
        w1_now = [cut("more", KC * FF).rearrange("p (c f) -> p c f", c=KC)]
        low = at["more"]
        w1_now.insert(0, cut("more", KC * FF).rearrange("p (c f) -> p c f", c=KC))
        slot_x = [cut("more", D) for _ in range(3)]
        slot_xT = [cut("more", D).rearrange("p (c n) -> p c n", c=KC) for _ in range(2)]

        st2 = [stack.enter_context(nc.psum_tensor(f"score_pair{i}", [P, 2, BANK], f32)) for i in range(2)]
        o_ps = stack.enter_context(nc.psum_tensor("out_acc", [P, BANK], f32))
        work = [stack.enter_context(nc.psum_tensor(f"work{i}", [P, BANK], f32))[:, :] for i in range(3)]
        banks = Ring(work)
        pairs = Ring(st2)
        o_free = [()]

        s_x = [stream("x") for _ in range(B)]
        x_in = [SP.dma(lambda e, b=b: e.dma_start(res[:, b * TB:(b + 1) * TB, :],
                                                  x[b].rearrange("(t p) n -> p t n", p=P)), s_x[b])
                for b in range(B)]
        s_w = stream("w_self")
        for i in range(4):
            w_in = ACTE.dma(lambda e, i=i: e.dma_start(w_self[i], wts[i].rearrange("(c p) n -> p c n", p=P)), s_w)
        s_bc = stream("bias_cols")
        for a in range(2):
            for i in range(2):
                bc_in = SP.dma(lambda e, a=a, i=i: e.dma_start(
                    b_qk[:, a, i, :], par[("bq", "bk")[i]][a].rearrange("(c p) -> p c", p=P),
                    allow_slow_non_contiguous=True), s_bc)
        s_pr = stream("params")
        for i, row in enumerate(par["rows"]):
            par_in = SP.dma(lambda e, i=i, row=row: e.dma_start(
                param[:, i, :], row.rearrange("(o n) -> o n", o=1).to_broadcast([P, D])), s_pr)
        par_in = SP.dma(lambda e: e.dma_start(
            rbias[:, :], par["rb"].rearrange("(o n) -> o n", o=1).to_broadcast([P, E])), s_pr)
        s_b1 = stream("expert_b1")
        b1_in = SP.dma(lambda e: e.dma_start(b1_rows[:, :], b1.rearrange("e (c p) -> (e c) p", p=P)), s_b1)
        s_wc = stream("w_cross")
        for i in range(4):
            wc_in = ACTE.dma(lambda e, i=i: e.dma_start(w_cross[i], wts[4 + i].rearrange("(c p) n -> p c n", p=P)), s_wc)
        wc_in = ACTE.dma(lambda e: e.dma_start(rw[:, :, :], router_w.rearrange("(c p) n -> p c n", p=P)), s_wc)
        wc_in = ACTE.dma(lambda e: e.dma_start(ctxn[0:SE, :, :], ctx_in.rearrange("b s n -> s b n")), s_wc)

        c0 = DVE.mark(lambda e: e.memset(ident[:, :], 0.0))
        c1 = DVE.mark(lambda e: e.memset(mask_qk[:, :], 0.0))
        id_ok = POOL.mark(lambda e: e.affine_select(
            out=ident[:, :], in_=ident[:, :], compare_op=ALU.not_equal, fill=1.0, base=0,
            pattern=[[-1, P]], channel_multiplier=1), c0)
        mask_ok = POOL.mark(lambda e: e.affine_select(
            out=mask_qk[:, :], in_=mask_qk[:, :], compare_op=ALU.is_ge, fill=NEG, base=0,
            pattern=[[-1, P]], channel_multiplier=1), c1)
        idb_ok = DVE.mark(lambda e: e.tensor_copy(identb[:, :], ident[:, :]), id_ok)
        DVE.do(lambda e: e.memset(epsc[:, :], EPS))
        DVE.do(lambda e: e.memset(pm[:, 0:TB // 2, :, 1:2], NEG))
        for i in range(2):
            mask_done = POOL.mark(lambda e, i=i: e.memset(kac[i][R_S:R_M, :, 0:SE], 1.0),
                                  mask_ok if i == 0 else ones_ok)
            ones_ok = POOL.mark(lambda e, i=i: e.memset(
                ka[i][R_S:R_M, :, :].rearrange("p h t -> p (h t)").bitcast(f32), TWO_ONES), mask_done)
            DVE.do(lambda e, i=i: e.memset(vac[i][:, :, HD:VW], 1.0))
            const_ok = DVE.mark(lambda e, i=i: e.memset(va[i][:, :, :, HD:VW], 1.0))
        zero_ok = POOL.mark(lambda e: e.memset(zeros, 0.0), ones_ok)
        s_z = stream("zero")
        zeros_in = SP.dma(lambda e: e.dma_start(sums_d[T:T + P, :], zeros), s_z, zero_ok)

        x_t_free = [()]

        def transpose_tile(t, ready, dst, free, evac):
            i, bank, bfree = banks.next()
            PE.wait(ready, id_ok, *bfree)
            for c in range(KC):
                m = (PE.mark if c == KC - 1 else PE.do)(lambda e, c=c, bank=bank: e.transpose(
                    bank[:, c * P:(c + 1) * P], res[:, t, c * P:(c + 1) * P], ident[:, :]))
            src = bank[:, 0:D].rearrange("p (c n) -> p c n", c=KC)
            if evac is ACTE:
                done = ACTE.mark(lambda e: e.copy(dst, src), m, *free)
            else:
                done = DVE.mark(lambda e: e.tensor_copy(dst, src), m, *free)
            banks.release(i, done)
            return done

        def x_t_steps(b, ready, say):
            def step(t):
                say[t] = transpose_tile(b * TB + t, ready[t], xT[:, :, t * P:(t + 1) * P],
                                        x_t_free[0], ACTE if t % 2 else DVE)
            return [lambda t=t: step(t) for t in range(TB)]

        f_ring, part_ring = Ring(f_sb), Ring(part_sb)
        slot_free = {"qa": [(), ()], "ka": [(), ()], "va": [(), ()], "kac": [(), ()], "vac": [(), ()]}
        mT_free, pm_free, negp_free = [(), ()], [(), ()], [(), ()]
        s_part = {}

        class Stage:
            def __init__(self, n, cross, b, hh):
                self.n, self.cross, self.b, self.hh, self.slot = n, cross, b, hh, n % 2
                self.keys = SE if cross else S
                self.ka = (kac if cross else ka)[self.slot]
                self.qa = qa[self.slot]
                self.loads = []
                self.va_ok, self.q_ok, self.k_ok = (), [(), ()], [(), ()]
                self.m_ok = [(), ()]

        def project_steps(st, which, src, n_tok, src_ok, weights, w_ok):
            box = {}

            def make(n0):
                if n0 == 0:
                    box["f"] = f_ring.next()
                fi, f, ffree = box["f"]
                w = min(BANK, n_tok - n0)
                i, bank, bfree = banks.next()
                PE.wait(w_ok, *bfree)
                for m in src_ok(n0, w):
                    PE.wait(m)
                for c in range(KC):
                    m = (PE.mark if c == KC - 1 else PE.do)(lambda e, c=c: e.matmul(
                        bank[:, 0:w], weights[:, c, st.hh * P:(st.hh + 1) * P], src(c, n0, w),
                        start=(c == 0), stop=(c == KC - 1)))
                if which == 0:
                    x_t_free[0] = x_t_free[0] + (m,)
                if n0 == 0:
                    box["p"] = part_ring.next()
                part, pfree = box["p"][1:]
                bias = b_qk[:, int(st.cross), which, st.hh:st.hh + 1]
                ACTE.do(lambda e: e.activation(part[0][:, n0:n0 + w], bank[:, 0:w], ACT.Identity, bias=bias),
                        m, bc_in, *pfree)
                box["made"] = ACTE.mark(lambda e: e.activation(
                    f[:, n0:n0 + w], bank[:, 0:w], ACT.Identity, bias=bias), *ffree)
                banks.release(i, box["made"])

            def split():
                fi, f, _ = box["f"]
                pi, part, pfree = box["p"]
                a, p = f[:, 0:n_tok], [q[:, 0:n_tok] for q in part]
                m = POOL.mark(lambda e: e.tensor_tensor(a, a, p[0], ALU.subtract), box["made"])
                m = ACTE.mark(lambda e: e.copy(p[1], a), m)
                m = POOL.mark(lambda e: e.tensor_tensor(p[2], a, p[1], ALU.subtract), m)
                f_ring.release(fi, m)
                out_s = s_part.setdefault(("out", pi), stream("parts_out"))
                for k in range(3):
                    stored = SP.dma(lambda e, k=k: e.dma_start(parts_d[st.n, which, k, :, 0:n_tok], p[k]),
                                    out_s, m)
                part_ring.release(pi, stored)
                box["stored"] = stored

            def load(half):
                t0, t1 = half * QG, min((half + 1) * QG, n_tok)
                into = (st.qa, st.ka)[which]
                key = "qa" if which == 0 else ("kac" if st.cross else "ka")
                in_s = s_part.setdefault((key, st.slot, half), stream(f"{key}_in"))
                for g in range(NGR if t0 < t1 else 0):
                    loaded = SP.dma(lambda e, g=g: e.dma_start(
                        into[g * HD:(g + 1) * HD, :, t0:t1],
                        parts_d[st.n, which, (Q_PART, K_PART)[which][g], :, t0:t1]
                        .rearrange("(h d) t -> d h t", d=HD)), in_s, box["stored"], *slot_free[key][st.slot])
                    if which == 0:
                        st.q_ok[half] = (loaded,)
                    else:
                        st.k_ok[half] = (loaded, ones_ok)

            st.loads.append(load)
            return [lambda n0=n0: make(n0) for n0 in range(0, n_tok, BANK)] + [split]

        def v_steps(st, src, src_ok, weights, w_ok, row):
            def make(k0):
                i, bank, bfree = banks.next()
                nk = 1 if st.cross else 4
                rows = SE if st.cross else P
                PE.wait(w_ok, *bfree)
                for k in range(nk):
                    for mk in src_ok((k0 + k) * P, rows):
                        PE.wait(mk)
                    for c in range(KC):
                        m = (PE.mark if k == nk - 1 and c == KC - 1 else PE.do)(lambda e, k=k, c=c: e.matmul(
                            bank[0:rows, k * P:(k + 1) * P], src(c, (k0 + k) * P, rows),
                            weights[:, c, st.hh * P:(st.hh + 1) * P], start=(c == 0), stop=(c == KC - 1)))
                if not st.cross:
                    x_t_free[0] = x_t_free[0] + (m,)
                bias = param[0:rows, row, st.hh * P:(st.hh + 1) * P].rearrange("p (h d) -> p h d", h=HH)
                key = "vac" if st.cross else "va"
                DVE.wait(m, par_in, *slot_free[key][st.slot])
                for k in range(nk):
                    to = vac[st.slot][0:rows, :, 0:HD] if st.cross else va[st.slot][:, k0 + k, :, 0:HD]
                    frm = bank[0:rows, k * P:(k + 1) * P].rearrange("p (h d) -> p h d", h=HH)
                    d = DVE.mark(lambda e, to=to, frm=frm: e.tensor_tensor(to, frm, bias, ALU.add))
                banks.release(i, d)
                st.va_ok = (d, const_ok)
            return [lambda k0=k0: make(k0) for k0 in range(0, 1 if st.cross else TB, 4)]

        def max_steps(st):
            box = {}

            def item(qb, c, w, h0, nh, diagonal):
                i, bank, bfree = banks.next()
                PE.wait(*st.q_ok[qb * P // QG], *st.k_ok[c], *bfree, mask_ok, idb_ok)
                for j in range(nh):
                    h = h0 + j
                    m = (PE.mark if j == nh - 1 and not diagonal else PE.do)(lambda e, h=h, j=j: e.matmul(
                        bank[:, j * w:(j + 1) * w], st.qa[0:R_S, h, qb * P:(qb + 1) * P],
                        st.ka[0:R_S, h, c * BANK:c * BANK + w], start=True, stop=not diagonal))
                    if diagonal:
                        m = (PE.mark if j == nh - 1 else PE.do)(lambda e, j=j: e.matmul(
                            bank[:, (j + 1) * w - P:(j + 1) * w], identb[:, :], mask_qk[:, :],
                            start=False, stop=True))
                src = bank[:, 0:nh * w].rearrange("p (j k) -> p j k", j=nh)
                r = DVE.mark(lambda e: e.tensor_reduce(pm[:, qb, h0:h0 + nh, c], src, AX.X, ALU.max),
                             m, *pm_free[qb * P // QG])
                banks.release(i, r)
                box["r"] = r

            def gather(g):
                tl = slice(g * TB // NG, (g + 1) * TB // NG)
                if st.cross:
                    m = DVE.mark(lambda e: e.tensor_scalar(
                        negm[:, tl, :], pm[:, tl, :, 0], -1.0, None, ALU.mult), box["r"])
                else:
                    m = DVE.mark(lambda e: e.tensor_reduce(
                        negm[:, tl, :], pm[:, tl, :, :], AX.X, ALU.max, negate=True), box["r"])
                pm_free[g] = (m,)
                p = [negp[:, tl, k, :] for k in range(3)]
                m = DVE.mark(lambda e: e.tensor_copy(p[0], negm[:, tl, :]), m, *negp_free[g])
                m = DVE.mark(lambda e: e.tensor_tensor(negr[:, tl, :], negm[:, tl, :], p[0], ALU.subtract), m)
                m = DVE.mark(lambda e: e.tensor_copy(p[1], negr[:, tl, :]), m)
                m = DVE.mark(lambda e: e.tensor_tensor(p[2], negr[:, tl, :], p[1], ALU.subtract), m)
                box["neg"] = m

            def lay(g):
                i, bank, bfree = banks.next()
                rows = bank[0:3 * HH, 0:QG // 2].bitcast(bf16)
                PE.wait(box["neg"], idb_ok, *bfree)
                for t in range(QG // P):
                    m = (PE.mark if t == QG // P - 1 else PE.do)(lambda e, t=t: e.transpose(
                        rows[:, t * P:(t + 1) * P],
                        negp[:, g * (QG // P) + t, :, :].rearrange("p k h -> p (k h)"), identb[:, :]))
                negp_free[g] = (m,)
                cols = slice(g * QG, (g + 1) * QG)
                m = ACTE.mark(lambda e: e.copy(mT[0:3 * HH, cols], rows), m, *mT_free[g])
                banks.release(i, m)
                s = s_part.setdefault(("negm", g), stream("negm_out"))
                stored = SP.dma(lambda e: e.dma_start(
                    negm_d[st.n].rearrange("k h t -> (k h) t")[:, cols], mT[0:3 * HH, cols]), s, m)
                mT_free[g] = (stored,)
                s2 = s_part.setdefault(("negm_in", st.slot, g), stream("negm_in"))
                st.m_ok[g] = (SP.dma(lambda e: e.dma_start(st.qa[R_S:R_M, :, cols], negm_d[st.n][:, :, cols]),
                                     s2, stored, *slot_free["qa"][st.slot]),)

            steps = []
            for qb in range(TB):
                if qb == TB // NG:
                    steps.append(lambda: gather(0))
                    st.second_max_at = len(steps) + 4
                if st.cross:
                    steps += [lambda qb=qb, h0=h0: item(qb, 0, SE, h0, HH // 2, False)
                              for h0 in range(0, HH, HH // 2)]
                    continue
                keys = (qb + 1) * P
                for c in range((keys + BANK - 1) // BANK):
                    w = min(BANK, keys - c * BANK)
                    nh = BANK // w
                    last = (c + 1) * BANK >= keys
                    steps += [lambda qb=qb, c=c, w=w, h0=h0, nh=nh, last=last: item(qb, c, w, h0, nh, last)
                              for h0 in range(0, HH, nh)]
            steps.insert(st.second_max_at - 1, lambda: lay(0))
            return steps + [lambda: gather(1), lambda: lay(1)]

        pt_ring, ot_ring = Ring(pt), Ring(ot)
        rs_ring = Ring([rsum[:, i] for i in range(2)])
        onat_ok = {}
        pt_done = [None]
        onat_free = [(), ()]

        def attend_steps(st):
            steps, pending, box = [], [], {}
            nkb = lambda g: 1 if st.cross else (g + 1) * (QG // P)

            def score(g, quad, kb, pair):
                rows = SE if st.cross else P
                skip = 0 if st.cross else max(0, kb * P - g * QG)
                w = QG - skip
                i, ps, free = pairs.next()
                PE.wait(*st.q_ok[g], *st.k_ok[kb * P // QG], *st.m_ok[g], *free)
                diagonal = not st.cross and kb * P >= g * QG
                for j in range(2):
                    h = quad * QUAD + pair * 2 + j
                    k0 = 0 if st.cross else kb * P
                    m = (PE.mark if j == 1 and not diagonal else PE.do)(lambda e, h=h, j=j, k0=k0: e.matmul(
                        ps[0:rows, j, 0:w], st.ka[0:R_M, h, k0:k0 + rows],
                        st.qa[0:R_M, h, g * QG + skip:(g + 1) * QG], start=True, stop=not diagonal))
                    if diagonal:
                        m = (PE.mark if j == 1 else PE.do)(lambda e, j=j: e.matmul(
                            ps[:, j, 0:P], mask_qk[:, :], identb[:, :], start=False, stop=True))
                pi, prob, pfree = pt_ring.next()
                x_ok = ACTE.mark(lambda e: e.activation(
                    prob[0:rows, :, 0:w], ps[0:rows, :, 0:w], ACT.Exp, scale=float(HD) ** -0.5), m, *pfree)
                pairs.release(i, x_ok)
                pt_done[0] = x_ok
                pending.append((pi, prob, x_ok, rows, skip, w))

            def weigh(g, quad, kb):
                first, last = kb == 0, kb == nkb(g) - 1
                PE.wait(*st.va_ok, *(o_free[0] if first else ()))
                for pair in range(2):
                    pi, prob, x_ok, rows, skip, w = pending.pop(0)
                    PE.wait(x_ok)
                    for j in range(2):
                        c = pair * 2 + j
                        h = quad * QUAD + c
                        v = vac[st.slot][0:rows, h, :] if st.cross else va[st.slot][:, kb, h, :]
                        m = (PE.mark if j == 1 else PE.do)(lambda e, c=c, v=v, prob=prob, rows=rows, j=j, w=w, skip=skip: e.matmul(
                            o_ps[c * VW:(c + 1) * VW, skip:QG], v, prob[0:rows, j, 0:w], start=first, stop=last))
                    pt_ring.release(pi, m)
                box["pv"] = m

            def normalise(g, quad):
                oi, o, ofree = ot_ring.next()
                if (g + quad) % 2:
                    cp = ACTE.mark(lambda e: e.copy(o, o_ps[:, :]), box["pv"], *ofree)
                else:
                    cp = DVE.mark(lambda e: e.tensor_copy(o, o_ps[:, :]), box["pv"], *ofree)
                o_free[0] = (cp,)
                box[g, quad] = (oi, o, cp)

            def divide(g, quad):
                oi, o, cp = box[g, quad]
                i, bank, bfree = banks.next()
                PE.wait(cp, *bfree)
                for q in range(QG // P):
                    m = (PE.mark if q == QG // P - 1 else PE.do)(lambda e, q=q: e.transpose(
                        bank[:, q * P:(q + 1) * P], o[:, q * P:(q + 1) * P], ident[:, :]))
                ot_ring.release(oi, m)
                view = bank[:, :].rearrange("p (q c v) -> p q c v", q=QG // P, c=QUAD)
                ri, rs_, rfree = rs_ring.next()
                r = DVE.mark(lambda e: e.reciprocal(rs_, view[:, :, :, HD]), m, *rfree)
                col = st.hh * P + quad * QUAD * HD
                DVE.wait(r, *onat_free[st.b])
                for q in range(QG // P):
                    d = DVE.mark(lambda e, q=q: e.tensor_tensor(
                        onat[st.b][:, g * (QG // P) + q, col:col + QUAD * HD].rearrange("p (c d) -> p c d", c=QUAD),
                        view[:, q, :, 0:HD],
                        rs_[:, q, :].rearrange("p (c o) -> p c o", o=1).to_broadcast([P, QUAD, HD]), ALU.mult))
                banks.release(i, d)
                rs_ring.release(ri, d)
                onat_ok[st.b] = d

            order = [(g, quad, kb) for g in range(NG) for quad in range(HH // QUAD) for kb in range(nkb(g))]
            late, divisions = [], []
            for g, quad, kb in order:
                if (g, quad, kb) == (1, 0, 0):
                    st.second_group_at = len(steps)
                steps.append(lambda g=g, quad=quad, kb=kb: score(g, quad, kb, 0))
                steps.append(lambda g=g, quad=quad, kb=kb: score(g, quad, kb, 1))
                steps += divisions + late
                late, divisions = [lambda g=g, quad=quad, kb=kb: weigh(g, quad, kb)], late[1:] and [
                    lambda gq=ended: divide(*gq)]
                if kb == nkb(g) - 1:
                    ended = (g, quad)
                    late.append(lambda g=g, quad=quad: normalise(g, quad))
            steps += divisions + late + [lambda: divide(*ended)]

            def close():
                slot_free["qa"][st.slot] = (box["pv"],)
                for k in (("kac", "vac") if st.cross else ("ka", "va")):
                    slot_free[k][st.slot] = (box["pv"],)
            return steps + [close]

        onT_ring = Ring(onT)

        stat_free = [(), ()]

        def norm_stats(t, src, ready, k):
            m = DVE.mark(lambda e: e.bn_stats(stat[:, k, :], src), ready, *stat_free[k])
            m = DVE.mark(lambda e: e.bn_aggr(mv[:, t, :], stat[:, k, :]), m)
            stat_free[k] = (m,)
            return m

        def norm_scale(t0, n, ready):
            tiles = slice(t0, t0 + n)
            m = ACTE.mark(lambda e: e.activation(sdev[:, tiles], mv[:, tiles, 1], ACT.Sqrt,
                                                 bias=epsc[:, 0:1]), ready, const_ok)
            m = DVE.mark(lambda e: e.reciprocal(rstd[:, tiles], sdev[:, tiles]), m)
            return DVE.mark(lambda e: e.scalar_tensor_tensor(
                shift[:, tiles], mv[:, tiles, 0], -1.0, rstd[:, tiles], ALU.mult, ALU.mult), m)

        def norm_apply(t, scaled, g, b, alone=False):
            src = res[:, t, :]
            if alone:
                m = DVE.mark(lambda e: e.scalar_tensor_tensor(
                    src, src, mv[:, t, 0:1], param[:, g, :], ALU.subtract, ALU.mult), scaled, par_in)
                return DVE.mark(lambda e: e.scalar_tensor_tensor(
                    src, src, rstd[:, t:t + 1], param[:, b, :], ALU.mult, ALU.add), m)
            m = ACTE.mark(lambda e: e.activation(src, src, ACT.Identity, scale=rstd[:, t:t + 1],
                                                 bias=shift[:, t:t + 1]), scaled)
            m = DVE.mark(lambda e: e.tensor_tensor(src, src, param[:, g, :], ALU.mult), m, par_in)
            return POOL.mark(lambda e: e.tensor_tensor(src, src, param[:, b, :], ALU.add), m, par_in)

        def project_out_steps(b, w_o, w_ok, bo, g, bn, say):
            box = {}

            def turn(t):
                i, bank, bfree = banks.next()
                PE.wait(onat_ok[b], *bfree)
                for c in range(KC):
                    m = (PE.mark if c == KC - 1 else PE.do)(lambda e, c=c: e.transpose(
                        bank[:, c * P:(c + 1) * P], onat[b][:, t, c * P:(c + 1) * P], ident[:, :]))
                onat_free[b] = (m,)
                oi, o, ofree = onT_ring.next()
                cp = ACTE.mark(lambda e: e.copy(o, bank[:, 0:D].rearrange("p (c n) -> p c n", c=KC)), m, *ofree)
                banks.release(i, cp)
                box[t] = (oi, o, cp)

            def tile(t):
                tt = b * TB + t
                m_b = POOL.mark(lambda e: e.tensor_tensor(res[:, tt, :], res[:, tt, :], param[:, bo, :], ALU.add),
                                par_in, *x_t_src_free[b])
                oi, o, cp = box[t]
                i, bank2, bfree = banks.next()
                PE.wait(cp, w_ok, *bfree)
                for c in range(KC):
                    m = (PE.mark if c == KC - 1 else PE.do)(lambda e, c=c: e.matmul(
                        bank2[:, 0:D], o[:, c, :], w_o[:, c, :], start=(c == 0), stop=(c == KC - 1)))
                onT_ring.release(oi, m)
                s = DVE.mark(lambda e: e.tensor_tensor(res[:, tt, :], bank2[:, 0:D], res[:, tt, :], ALU.add), m, m_b)
                banks.release(i, s)
                box["s"] = norm_stats(tt, res[:, tt, :], s, t % 2)

            def scale():
                box["r"] = norm_scale(b * TB, TB, box["s"])

            def apply(t):
                say[t] = norm_apply(b * TB + t, box["r"], g, bn, alone=say is norm2[B - 1])

            tiles = [lambda: turn(0)]
            for t in range(TB):
                if t + 1 < TB:
                    tiles.append(lambda t=t: turn(t + 1))
                tiles.append(lambda t=t: tile(t))
            return (tiles + [scale]
                    + [lambda t=t: apply(t) for t in range(TB)])

        x_t_src_free = {}
        xt_ok = {}

        def turn_steps(b, ready):
            say = [None] * TB
            xt_ok[b] = say

            def note():
                x_t_src_free[b] = tuple(say)
                x_t_free[0] = ()
            return x_t_steps(b, ready, say) + [note]

        def x_src(st):
            return (lambda c, n0, w: xT[:, c, n0:n0 + w],
                    lambda n0, w: xt_ok[st.b][n0 // P:(n0 + w) // P])

        def ctx_src(st):
            return lambda c, n0, w: ctxT[:, st.b, c, n0:n0 + w], lambda n0, w: ctx_ok

        def qk_steps(st):
            src, ok = x_src(st)
            w, w_ok = (w_cross, wc_in) if st.cross else (w_self, w_in)
            ksrc, kok = ctx_src(st) if st.cross else (src, ok)
            return (project_steps(st, 1, ksrc, st.keys, kok, w[1], w_ok)
                    + project_steps(st, 0, src, S, ok, w[0], w_ok))

        def vl_steps(st):
            src, ok = ctx_src(st) if st.cross else x_src(st)
            w, w_ok, row = (w_cross, wc_in, C_BV) if st.cross else (w_self, w_in, A_BV)
            return ([lambda: [load(half) for half in range(2) for load in st.loads]]
                    + v_steps(st, src, ok, w[2], w_ok, row))

        ctx_ok = []

        def ctx_steps():
            def step(b):
                i, bank, bfree = banks.next()
                PE.wait(wc_in, id_ok, *bfree)
                for c in range(KC):
                    m = (PE.mark if c == KC - 1 else PE.do)(lambda e, c=c: e.transpose(
                        bank[:, c * P:c * P + SE], ctxn[0:SE, b, c * P:(c + 1) * P], ident[0:SE, 0:SE]))
                d = DVE.mark(lambda e: e.tensor_copy(
                    ctxT[:, b, :, :], bank[:, 0:KC * P].rearrange("p (c n) -> p c n", c=KC)[:, :, 0:SE]), m)
                banks.release(i, d)
                ctx_ok.append(d)
                ot_ring.release(0, d)
            return [lambda b=b: step(b) for b in range(B)]

        stages = [Stage(n, n >= 4, (n // 2) % 2, n % 2) for n in range(8)]
        norm1 = [[None] * TB for _ in range(B)]
        norm2 = [[None] * TB for _ in range(B)]
        out1 = lambda b: project_out_steps(b, w_self[3], w_in, A_BO, G1, B1N, norm1[b])
        s_tok = stream("tokens")
        tokens_in = []

        def keep(b):
            for to in (tokens_d, sums_d):
                tokens_in[:] = [SP.dma(lambda e, to=to: e.dma_start(
                    to[b * S:(b + 1) * S, :].rearrange("(t p) n -> p t n", p=P),
                    res[:, b * TB:(b + 1) * TB, :]), s_tok, norm2[b][TB - 1])]

        out2 = lambda b: project_out_steps(b, w_cross[3], wc_in, C_BO, G2, B2N, norm2[b]) + [lambda: keep(b)]
        w1_v = w1.rearrange("e (c p) f -> p e c f", p=P)
        w2_v = w2.rearrange("e (c p) n -> p e c n", p=P)
        w1_s = w1_sb.rearrange("p (e c f) -> p e c f", e=E, c=KC)
        w2_s = w2_sb.rearrange("p (e c n) -> p e c n", e=E, c=FC)

        NE = NT * E
        spare = [0]

        def table(n, dt=f32):
            words = n // 2 if dt is bf16 else n
            a = spare[0]
            spare[0] += words
            assert spare[0] <= MORE
            return more[:, a:a + words].bitcast(dt)

        NK = 2 * NT
        KINDS = 3
        spare[0] = 10240
        lg = table(NE).rearrange("p (t e) -> p t e", t=NT)
        top = table(NE).rearrange("p (t e) -> p t e", t=NT)
        topi = table(NE, u32).rearrange("p (t e) -> p t e", t=NT)
        ex_l = table(NE).rearrange("p (t e) -> p t e", t=NT)
        oh = table(2 * NE).rearrange("p (k t e) -> p k t e", k=2, t=NT)
        tri, ones = table(P), table(P)
        ejf = table(NSLOT)[0:1, :]
        iota_s = table(P)
        cmp_j = table(NSLOT * E)
        of_choice = cmp_j[:, 0:2 * NE].rearrange("p (k t e) -> p k t e", k=2, t=NT)
        cmp_j = cmp_j[0:1, :].rearrange("p (j e) -> p j e", j=NSLOT)
        spare[0] = 0
        hot_s = table(NK * P, bf16).rearrange("p (k t s) -> p k t s", k=2, t=NT)
        assert spare[0] <= KC * T // 2
        weight_j = table(NK * KINDS * NSLOT, bf16).rearrange("p (n k j) -> p n k j", n=NK, k=KINDS)
        row_j = table(NK * KINDS * NSLOT, bf16).rearrange("p (n k j) -> p n k j", n=NK, k=KINDS)
        iota_jj = table(NSLOT)
        inv_row = table(KINDS * NSLOT).rearrange("p (k j) -> p k j", k=KINDS)
        inv_w = table(KINDS * NSLOT).rearrange("p (k j) -> p k j", k=KINDS)
        assert spare[0] <= low
        pr = sb("top_prob", [P, NT, 2])
        topf = sb("top_index_f", [P, NT, 2])
        logits = []

        def router_steps(b):
            box = {}
            together = b == B - 1

            def turn(t):
                i, bank, bfree = banks.next()
                PE.wait(norm2[b][t], *bfree)
                for c in range(KC):
                    m = (PE.mark if c == KC - 1 else PE.do)(lambda e, c=c: e.transpose(
                        bank[:, c * P:(c + 1) * P], res[:, b * TB + t, c * P:(c + 1) * P], ident[:, :]))
                xi, xt, xfree = onT_ring.next()
                cp = ACTE.mark(lambda e: e.copy(xt, bank[:, 0:D].rearrange("p (c n) -> p c n", c=KC)), m, *xfree)
                banks.release(i, cp)
                box[t] = (xi, xt, cp)

            def multiply(t):
                xi, xt, cp = box[t]
                if together:
                    i, bank, bfree = None, o_ps[:, t * E:(t + 1) * E], o_free[0]
                else:
                    i, bank, bfree = banks.next()
                PE.wait(cp, wc_in, *bfree)
                for c in range(KC):
                    m = (PE.mark if c == KC - 1 else PE.do)(lambda e, c=c: e.matmul(
                        bank[:, 0:E], xt[:, c, :], rw[:, c, :], start=(c == 0), stop=(c == KC - 1)))
                onT_ring.release(xi, m)
                tt = b * TB + t
                if together:
                    box["m"] = m
                    return
                m = DVE.mark(lambda e: e.tensor_tensor(lg[:, tt, :], bank[:, 0:E], rbias[:, :], ALU.add), m, par_in)
                banks.release(i, m)
                m = DVE.mark(lambda e: e.max(top[:, tt, :], lg[:, tt, :]), m)
                logits[:] = [DVE.mark(lambda e: e.max_index(topi[:, tt, :], top[:, tt, :], lg[:, tt, :]), m)]

            steps = [lambda: turn(0)]
            for t in range(TB):
                if t + 1 < TB:
                    steps.append(lambda t=t: turn(t + 1))
                steps.append(lambda t=t: multiply(t))

            def choose_all():
                tiles = slice(b * TB, (b + 1) * TB)
                m = DVE.mark(lambda e: e.tensor_tensor(
                    lg[:, tiles, :], o_ps[:, 0:TB * E].rearrange("p (t e) -> p t e", t=TB),
                    rbias[:, :].rearrange("p (o e) -> p o e", o=1).to_broadcast([P, TB, E]), ALU.add),
                    box["m"], par_in)
                o_free[0] = (m,)
                for tt in range(b * TB, (b + 1) * TB):
                    mt = DVE.mark(lambda e, tt=tt: e.max(top[:, tt, :], lg[:, tt, :]), m)
                DVE.wait(mt)
                for tt in range(b * TB, (b + 1) * TB):
                    mi = DVE.mark(lambda e, tt=tt: e.max_index(topi[:, tt, :], top[:, tt, :], lg[:, tt, :]))
                logits[:] = [mi]
            return steps + [choose_all] * together

        rs = sb("prob_recip", [P, NT])
        dw = sb("weight_tmp", [P, NT])
        wgt = sb("combine", [P, 2, NT])
        iota_e = sb("iota_e", [P, E])
        cnt = sb("tile_counts", [P, NT + 1, E])
        both = sb("both_choices", [P, NT, E])
        ntile = sb("tiles_expert", [P, E], i32)
        ntile_f = sb("tiles_expert_f", [P, E])
        tinc = sb("tiles_upto", [P, E])
        base = sb("first_tile", [P, E])
        ranks = sb("rank", [P, 2, NT])
        rank_i = sb("rank_int", [P, 2, NT], i32)
        rank_p = sb("rank_parts", [P, 2, 2, NT], i32)
        rank_f = sb("rank_parts_f", [P, 2, 2, NT])
        tile_f = sb("token_tile", [P, NK])
        kinds = sb("kinds", [P, 4, NK], bf16)
        ids = sb("token_ids", [P, NSLOT])
        dummy = sb("dummy_ids", [P, NSLOT])
        rows_in = sb("gather_rows", [P, NSLOT], i32)
        rows_out = sb("scatter_rows", [P, NSLOT], i32)
        w_slot = sb("slot_weight", [P, NSLOT])
        w_rest = tile_f
        slot_no = sb("slot_no", [P, 1])
        place = sb("place", [P, 1])
        iota_j = sb("iota_j", [1, NSLOT])
        ej = sb("tile_expert", [1, NSLOT], i32)
        n_used = sb("tiles_used", [1, 1], i32)

        def bc(ap, shape):
            return ap.to_broadcast(shape)

        def numbers(dst, pattern, base=0, by_partition=0, *after):
            return POOL.mark(lambda e: e.iota(dst, pattern, base=base, channel_multiplier=by_partition,
                                              allow_small_or_imprecise_dtypes=True), *after)

        numbers(iota_e[:, :], [[1, E]])
        numbers(iota_j[:, :], [[1, NSLOT]])
        numbers(iota_s, [[1, P]])
        numbers(slot_no[:, :], [[0, 1]], T, 1)
        numbers(place[:, :], [[0, 1]], 0, 1)
        numbers(kinds[:, 0, :], [[0, 2], [1, NT]])
        one_ok = POOL.mark(lambda e: e.memset(ones[:, :], 1.0))
        place_ok = tri_ok = POOL.mark(lambda e: e.affine_select(
            out=tri[:, :], in_=ones[:, :], compare_op=ALU.is_gt, fill=0.0, base=0,
            pattern=[[1, P]], channel_multiplier=-1), one_ok)
        counted = []

        totals = {}

        def count(b):
            t0, t1 = b * TB, (b + 1) * TB
            xT_read = Mark(PE.sem, PE.count)
            yield
            m = DVE.mark(lambda e: e.tensor_copy(topf[:, t0:t1, :], topi[:, t0:t1, 0:2]), logits[0])
            for k in range(2):
                mo = DVE.mark(lambda e, k=k: e.tensor_tensor(
                    oh[:, k, t0:t1, :], bc(iota_e[:, :].rearrange("p (o e) -> p o e", o=1), [P, TB, E]),
                    bc(topf[:, t0:t1, k:k + 1], [P, TB, E]), ALU.is_equal), m, place_ok)
            m = DVE.mark(lambda e: e.tensor_tensor(both[:, t0:t1, :], oh[:, 0, t0:t1, :], oh[:, 1, t0:t1, :],
                                                   ALU.add), mo)
            if b == 0:
                m = DVE.mark(lambda e: e.memset(cnt[:, 0, :], 0.0), m)
            for t in range(t0, t1):
                m = DVE.mark(lambda e, t=t: e.tensor_tensor(cnt[:, t + 1, :], cnt[:, t, :], both[:, t, :], ALU.add), m)
            yield
            i, bank, free = banks.next()
            PE.wait(m, tri_ok, *free)
            flat = lambda ap: ap.rearrange("p t e -> p (t e)")
            PE.do(lambda e: e.matmul(bank[:, 0:TB * E], tri[:, :], flat(both[:, t0:t1, :]), start=True, stop=False))
            m = PE.mark(lambda e: e.matmul(bank[:, 0:TB * E], ones[:, :], flat(cnt[:, t0:t1, :]),
                                           start=False, stop=True))
            if b == B - 1:
                totals["m"] = m = PE.mark(lambda e: e.matmul(bank[:, BANK // 2:BANK // 2 + E], ones[:, :],
                                                            cnt[:, NT, :], start=True, stop=True))
                totals["n"] = bank[:, BANK // 2:BANK // 2 + E]
                softmax_start()
            before = bank[:, 0:TB * E].rearrange("p (t e) -> p t e", t=TB)
            for k in range(2):
                mk = DVE.mark(lambda e, k=k: e.tensor_tensor(of_choice[:, k, t0:t1, :], oh[:, k, t0:t1, :], before,
                                                             ALU.mult), m)
                mr = DVE.mark(lambda e, k=k: e.tensor_reduce(ranks[:, k, t0:t1], of_choice[:, k, t0:t1, :],
                                                             AX.X, ALU.add), mk)
            banks.release(i, mk)
            yield
            m = DVE.mark(lambda e: e.tensor_copy(rank_i[:, :, t0:t1], ranks[:, :, t0:t1]), mr)
            for part, (op, by) in enumerate(((ALU.bitwise_and, P - 1), (ALU.arith_shift_right, 7))):
                mp = DVE.mark(lambda e, part=part, op=op, by=by: e.tensor_scalar(
                    rank_p[:, part, :, t0:t1], rank_i[:, :, t0:t1], by, None, op), m)
                mf = DVE.mark(lambda e, part=part: e.tensor_copy(rank_f[:, part, :, t0:t1],
                                                                 rank_p[:, part, :, t0:t1]), mp)
            for k in range(2):
                yield
                h = DVE.mark(lambda e, k=k: e.tensor_tensor(
                    hot_s[:, k, t0:t1, :], bc(iota_s.rearrange("p (o s) -> p o s", o=1), [P, TB, P]),
                    bc(rank_f[:, 0, k, t0:t1].rearrange("p (t o) -> p t o", o=1), [P, TB, P]), ALU.is_equal),
                    mf, xT_read)
            counted[:] = [h]

        def count_steps(b):
            counting = count(b)
            return [lambda: next(counting, None)] * 6

        soft = []

        def softmax_start():
            m = DVE.mark(lambda e: e.tensor_tensor(pr[:, :, :], top[:, :, 0:2], bc(top[:, :, 0:1], [P, NT, 2]),
                                                   ALU.subtract), logits[0])
            m = DVE.mark(lambda e: e.tensor_tensor(lg[:, :, :], lg[:, :, :], bc(top[:, :, 0:1], [P, NT, E]),
                                                   ALU.subtract), m)
            ACTE.do(lambda e: e.activation(ex_l[:, :, :], lg[:, :, :], ACT.Exp), m)
            soft.append(ACTE.mark(lambda e: e.activation(pr[:, :, :], pr[:, :, :], ACT.Exp)))

        first_max = max_steps(stages[0])
        cut_at = stages[0].second_max_at
        for s in (turn_steps(0, [x_in[0]] * TB) + qk_steps(stages[0]) + vl_steps(stages[0])
                  + qk_steps(stages[1]) + ctx_steps() + first_max[:cut_at]):
            s()
        first = attend_steps(stages[0])
        at_g1 = stages[0].second_group_at
        interleave(first[:at_g1], first_max[cut_at:], 1.0)
        interleave(first[at_g1:], vl_steps(stages[1]) + mix(
            turn_steps(1, [x_in[1]] * TB) + qk_steps(stages[2]), max_steps(stages[1])))
        interleave(attend_steps(stages[1]), vl_steps(stages[2]) + mix(
            qk_steps(stages[3]), max_steps(stages[2])))
        interleave(attend_steps(stages[2]), vl_steps(stages[3]) + mix(
            out1(0) + turn_steps(0, norm1[0]) + qk_steps(stages[4]), max_steps(stages[3])))
        interleave(attend_steps(stages[3]), vl_steps(stages[4]) + mix(
            qk_steps(stages[5]), max_steps(stages[4])))
        interleave(attend_steps(stages[4]), vl_steps(stages[5]) + out1(1) + mix(
            turn_steps(1, norm1[1]) + qk_steps(stages[6]), max_steps(stages[5])))
        self_done = Mark(PE.sem, PE.count)
        s_e = stream("w1_early")
        early = 2 * (HH * S // 2 + TB * HH * VW) // EW + 1
        got_early = []

        def early_load(ex):
            got_early[:] = [SP.dma(lambda e: e.dma_start(w1_s[:, ex], w1_v[:, ex]), s_e, self_done)]

        def spread(steps, loads):
            n = max(1, len(steps) // (len(loads) + 1))
            return [x for k, step in enumerate(steps)
                    for x in ([step] + ([loads.pop(0)] if loads and k % n == n - 1 else []))] + loads

        loads = [lambda ex=ex: early_load(ex) for ex in range(early)]
        interleave(attend_steps(stages[5]), spread(
            vl_steps(stages[6]) + qk_steps(stages[7]) + max_steps(stages[6]), loads[:early // 2]))
        interleave(attend_steps(stages[6]), spread(
            vl_steps(stages[7]) + out2(0) + max_steps(stages[7]), loads[early // 2:]))
        interleave(attend_steps(stages[7]), router_steps(0), 1.0)
        early_in = got_early[0]
        attend_done = (Mark(PE.sem, PE.count), pt_done[0])
        s_l = stream("w_late")
        for ex in range(early, E):
            late_in = SP.dma(lambda e, ex=ex: e.dma_start(w1_s[:, ex], w1_v[:, ex]), s_l, *attend_done)
        for ex in range(E - 1):
            late_in = SP.dma(lambda e, ex=ex: e.dma_start(w2_s[:, ex], w2_v[:, ex]), s_l, *attend_done)
        last_out, last_router = out2(1), router_steps(1)
        tiles_end = 2 * TB + 1
        last = mix(last_out[:tiles_end], count_steps(0))
        for t in range(TB):
            last += [last_out[tiles_end + t]] + (last_router[2 * t - 1:2 * t + 1] if t else last_router[:1])
        for s in last + last_router[2 * TB - 1:] + last_out[tiles_end + TB:]:
            s()
        attention_done = Mark(PE.sem, PE.count)
        out_done = Mark(ACTE.sem, ACTE.count)
        last_kept = Mark(DVE.sem, DVE.count)


        s_last = stream("w_last")
        last_in = SP.dma(lambda e: e.dma_start(w2_s[:, E - 1], w2_v[:, E - 1]), s_last, attention_done, out_done)
        router_free = (attention_done, out_done, norm2[1][-1], last_kept)
        j_ok = numbers(iota_jj, [[1, NSLOT]], 0, 0, *router_free)

        for s in count_steps(1):
            s()
        m = DVE.mark(lambda e: e.tensor_scalar(ntile[:, :], totals["n"], float(P - 1), None, ALU.add), totals["m"])
        totals_read = m
        m = DVE.mark(lambda e: e.tensor_scalar(ntile[:, :], ntile[:, :], 7, None, ALU.arith_shift_right), m)
        m = DVE.mark(lambda e: e.tensor_copy(ntile_f[:, :], ntile[:, :]), m)
        m = DVE.mark(lambda e: e.tensor_copy(tinc[:, 0:1], ntile_f[:, 0:1]), m)
        for ex in range(1, E):
            m = DVE.mark(lambda e, ex=ex: e.tensor_tensor(tinc[:, ex:ex + 1], tinc[:, ex - 1:ex],
                                                          ntile_f[:, ex:ex + 1], ALU.add), m)
        tinc_ok = m
        m = DVE.mark(lambda e: e.tensor_tensor(base[:, :], tinc[:, :], ntile_f[:, :], ALU.subtract), m)
        m = DVE.mark(lambda e: e.tensor_tensor(
            of_choice.rearrange("p k t e -> p (k t) e"), oh.rearrange("p k t e -> p (k t) e"),
            bc(base[:, :].rearrange("p (o e) -> p o e", o=1), [P, NK, E]), ALU.mult), m, *counted)
        m = DVE.mark(lambda e: e.tensor_reduce(tile_f[:, :], of_choice.rearrange("p k t e -> p (k t) e"),
                                               AX.X, ALU.add), m)
        m = DVE.mark(lambda e: e.tensor_tensor(
            tile_f[:, :], tile_f[:, :], rank_f[:, 1].rearrange("p k t -> p (k t)"), ALU.add), m)

        by_n = lambda ap: bc(ap.rearrange("p (n o) -> p n o", o=1), [P, NK, NSLOT])
        hj = DVE.mark(lambda e: e.tensor_tensor(
            row_j[:, :, 0, :], bc(iota_jj.rearrange("p (o j) -> p o j", o=1), [P, NK, NSLOT]),
            by_n(tile_f[:, :]), ALU.is_equal), m, j_ok)
        v1 = DVE.mark(lambda e: e.tensor_scalar(row_j[:, :, 2, :], row_j[:, :, 0, :], place[:, 0:1], None, ALU.mult),
                      hj, place_ok)
        v2 = DVE.mark(lambda e: e.tensor_tensor(row_j[:, :, 1, :], row_j[:, :, 0, :], by_n(kinds[:, 0, :]), ALU.mult),
                      v1)

        def invert(values, ring, *ready):
            i, bank, free = ring.next()
            PE.wait(*ready, *free)
            for n in range(NK):
                m = (PE.mark if n == NK - 1 else PE.do)(lambda e, n=n: e.matmul(
                    bank[:, 0:KINDS * NSLOT], hot_s[:, n // NT, n % NT, :],
                    values[:, n, :, :].rearrange("p k j -> p (k j)"), start=(n == 0), stop=(n == NK - 1)))
            return i, bank[:, 0:KINDS * NSLOT].rearrange("p (k j) -> p k j", k=KINDS), m
        i, found, row_m = invert(row_j, banks, v2, *counted)
        m = DVE.mark(lambda e: e.tensor_reduce(rs[:, :], ex_l[:, :, :], AX.X, ALU.add), soft[0])
        m = DVE.mark(lambda e: e.reciprocal(rs[:, :], rs[:, :]), m)
        m = DVE.mark(lambda e: e.tensor_tensor(
            pr[:, :, :], pr[:, :, :], bc(rs[:, :].rearrange("p (t o) -> p t o", o=1), [P, NT, 2]), ALU.mult), m)
        m = DVE.mark(lambda e: e.tensor_tensor(dw[:, :], pr[:, :, 1], pr[:, :, 0], ALU.subtract), m)
        xm = ACTE.mark(lambda e: e.activation(wgt[:, 1, :], dw[:, :], ACT.Exp), m)
        m = DVE.mark(lambda e: e.tensor_tensor(
            cmp_j[:, :, :], bc(iota_j[:, :].rearrange("p (j o) -> p j o", o=1), [1, NSLOT, E]),
            bc(tinc[0:1, :].rearrange("p (o e) -> p o e", o=1), [1, NSLOT, E]), ALU.is_ge), tinc_ok, place_ok, m)
        m = DVE.mark(lambda e: e.tensor_reduce(ejf[:, :], cmp_j[:, :, :], AX.X, ALU.add), m)
        m = DVE.mark(lambda e: e.tensor_scalar(ejf[:, :], ejf[:, :], float(E - 1), None, ALU.min), m)
        DVE.do(lambda e: e.tensor_copy(n_used[:, :], tinc[0:1, E - 1:E]))
        ej_ok = DVE.mark(lambda e: e.tensor_copy(ej[:, :], ejf[:, :]), m)
        m = DVE.mark(lambda e: e.tensor_copy(inv_row, found), row_m)
        banks.release(i, m)
        inv_ok = m
        m = DVE.mark(lambda e: e.scalar_tensor_tensor(ids[:, :], inv_row[:, 1, :], float(P), inv_row[:, 2, :],
                                                      ALU.mult, ALU.add), m)
        rows_ok = DVE.mark(lambda e: e.tensor_copy(rows_in[:, :], ids[:, :]), m)
        m = DVE.mark(lambda e: e.tensor_scalar(dw[:, :], wgt[:, 1, :], 1.0, None, ALU.add), xm)
        m = DVE.mark(lambda e: e.reciprocal(wgt[:, 0, :], dw[:, :]), m)
        m = DVE.mark(lambda e: e.tensor_tensor(wgt[:, 1, :], wgt[:, 1, :], wgt[:, 0, :], ALU.mult), m)
        wflat = wgt[:, :, :].rearrange("p k t -> p (k t)")
        m = DVE.mark(lambda e: e.tensor_copy(kinds[:, 1, :], wflat), m)
        m = DVE.mark(lambda e: e.tensor_tensor(w_rest[:, :], wflat, kinds[:, 1, :], ALU.subtract), m)
        m = DVE.mark(lambda e: e.tensor_copy(kinds[:, 2, :], w_rest[:, :]), m)
        m = DVE.mark(lambda e: e.tensor_tensor(kinds[:, 3, :], w_rest[:, :], kinds[:, 2, :], ALU.subtract), m)
        kinds_ok = m

        def place_weights(engine, k):
            return engine.mark(lambda e: e.tensor_tensor(
                weight_j[:, :, k, :], row_j[:, :, 0, :], by_n(kinds[:, 1 + k, :]), ALU.mult), kinds_ok, hj)
        place_weights(DVE, 0)
        weights_dve = place_weights(DVE, 1)
        m = DVE.mark(lambda e: e.tensor_scalar(dummy[:, :], inv_row[:, 0, :], -1.0, 1.0, ALU.mult, ALU.add), inv_ok)
        m = DVE.mark(lambda e: e.scalar_tensor_tensor(ids[:, :], dummy[:, :], slot_no[:, 0:1], ids[:, :],
                                                      ALU.mult, ALU.add), m, rows_ok, place_ok)
        out_rows_ok = DVE.mark(lambda e: e.tensor_copy(rows_out[:, :], ids[:, :]), m)

        i, bank, bfree = banks.next()
        b1_m = PE.mark(lambda e: e.transpose(bank[:, 0:E * FC], b1_rows[:, :], ident[0:E * FC, 0:E * FC]),
                       b1_in, *bfree)
        b1_ok = DVE.mark(lambda e: e.tensor_copy(b1_col[:, :], bank[:, 0:E * FC]), b1_m)
        banks.release(i, b1_ok)
        b2_all = param[:, 0:E, :]
        s_b2 = stream("expert_b2")
        b2_in = SP.dma(lambda e: e.dma_start(b2_all, b2.rearrange("(o e) n -> o e n", o=1).to_broadcast([P, E, D])),
                       s_b2, norm2[0][-1], norm2[1][-1], last_kept)

        mbanks = Ring(work + [st2[1][:, 0, :], st2[1][:, 1, :], o_ps[:, :]])
        mbanks.free = [(totals_read, inv_ok, b1_ok)] * 3 + [pairs.free[0] + pairs.free[1]] * 2 + [o_free[0]]
        hid_ring, act_ring, w1_ring = Ring(hid), Ring(act), Ring(w1_now)
        sx_ring, sxT_ring, sy_ring = Ring(slot_x), Ring(slot_xT), Ring(slot_y)
        ybanks = Ring([st2[0][:, 0, :], st2[0][:, 1, :]])
        ybanks.free = [pairs.free[0] + pairs.free[1]] * 2
        s_sx = [stream("slot_x") for _ in slot_x]
        s_sy = [stream("slot_y") for _ in slot_y]
        of_tile = lambda j, streams, i, name: streams[i] if j < NSURE else stream(name, maybe=True)
        attention_free = (attention_done, out_done, norm2[0][-1], norm2[1][-1], last_kept, zeros_in)
        sx_ring.free, sxT_ring.free = [attention_free] * 3, [attention_free] * 2
        tiles = [dict() for _ in range(NSLOT)]

        n_reg = {}

        def if_used(step, j):
            def test(engine, e):
                if engine not in n_reg:
                    n_reg[engine] = e.value_load(n_used[0:1, 0:1], min_val=NSURE, max_val=NSLOT)
                return n_reg[engine] > j
            tiles[j]["test"] = test
            with ExitStack() as conditional:
                if j >= NSURE:
                    for engine in (PE, ACTE, DVE, POOL):
                        engine.wait(ej_ok)
                        conditional.enter_context(engine.only_if(test))
                step(j)

        def load(j):
            t = tiles[j]
            t["xi"], t["x"], free = sx_ring.next()
            t["x_in"] = POOL.dma(lambda e: e.indirect_dma_start(
                t["x"], None, tokens_d, bass.IndirectOffsetOnAxis(ap=rows_in[:, j:j + 1], axis=0)),
                of_tile(j, s_sx, t["xi"], "maybe_x"), rows_ok, *tokens_in, *free)

        def expert(e, j):
            return e.value_load(ej[0:1, j:j + 1], min_val=0, max_val=E - 1)

        def turn(j):
            t = tiles[j]
            i, bank, bfree = mbanks.next()
            PE.wait(t["x_in"], *bfree)
            for c in range(KC):
                m = (PE.mark if c == KC - 1 else PE.do)(lambda e, c=c: e.transpose(
                    bank[:, c * P:(c + 1) * P], t["x"][:, c * P:(c + 1) * P], ident[:, :]))
            sx_ring.release(t["xi"], m)
            t["xTi"], t["xT"], free = sxT_ring.next()
            t["xT_ok"] = ACTE.mark(lambda e: e.copy(
                t["xT"], bank[:, 0:D].rearrange("p (c n) -> p c n", c=KC)), m, *free)
            mbanks.release(i, t["xT_ok"])

        def take_w1(j):
            t = tiles[j]
            t["wi"], w, free = w1_ring.next()
            t["w1"] = w

            def half(e, c):
                return w1_sb[:, bass.ds(expert(e, j) * EW + c * FF, FF)]
            t["w1_ok"] = (
                ACTE.mark(lambda e: e.copy(w[:, 0, :], half(e, 0)), ej_ok, early_in, late_in, *free),
                DVE.mark(lambda e: e.tensor_copy(w[:, 1, :], half(e, 1)), ej_ok, early_in, late_in, *free))

        def up(j):
            t = tiles[j]
            PE.wait(t["xT_ok"], *t["w1_ok"], ej_ok, late_in, last_in)
            hi, hd, hfree = hid_ring.next()
            t["ai"], t["act"], afree = act_ring.next()
            for half in range(2):
                i, bank, bfree = mbanks.next()
                PE.wait(*bfree)
                for f in range(half * FC // 2, (half + 1) * FC // 2):
                    for c in range(KC):
                        def mm(e, f=f, c=c, bank=bank):
                            q = f % (FC // 2)
                            return e.matmul(bank[:, q * P:(q + 1) * P],
                                            t["w1"][:, c, f * P:(f + 1) * P], t["xT"][:, c, :],
                                            start=(c == 0), stop=(c == KC - 1))
                        last = f % (FC // 2) == FC // 2 - 1 and c == KC - 1
                        m = (PE.mark if last else PE.do)(mm)

                def add_bias(e, half=half, bank=bank):
                    if half == 0:
                        t["ex_dve"] = expert(e, j)
                    col = b1_col[:, bass.ds(t["ex_dve"] * FC + half * FC // 2, FC // 2)]
                    return e.tensor_tensor(
                        hd[:, half * FC // 2:(half + 1) * FC // 2, :], bank.rearrange("p (c n) -> p c n", n=P),
                        col.rearrange("p (c o) -> p c o", o=1).to_broadcast([P, FC // 2, P]), ALU.add)
                d = DVE.mark(add_bias, m, ej_ok, b1_ok, *hfree)
                mbanks.release(i, d)
                t["h", half] = ACTE.mark(lambda e, half=half: e.activation(
                    t["act"][:, half * FC // 2:(half + 1) * FC // 2, :],
                    hd[:, half * FC // 2:(half + 1) * FC // 2, :], ACT.Gelu), d, *afree)
            sxT_ring.release(t["xTi"], m)
            w1_ring.release(t["wi"], m)
            hid_ring.release(hi, t["h", 1])

        def down(j):
            t = tiles[j]
            i, bank, bfree = ybanks.next()
            PE.wait(*bfree)
            for c in range(FC):
                PE.wait(t["h", c // (FC // 2)])

                def mm(e, c=c):
                    if c == 0:
                        t["ex_pe"] = expert(e, j)
                    return e.matmul(bank[:, 0:D], t["act"][:, c, :], w2_sb[:, bass.ds(t["ex_pe"] * EW + c * D, D)],
                                    start=(c == 0), stop=(c == FC - 1))
                m = (PE.mark if c == FC - 1 else PE.do)(mm)
            act_ring.release(t["ai"], m)
            yi, y, yfree = sy_ring.next()
            b2_rows = b2_all.rearrange("p e n -> p (e n)")
            d = DVE.mark(lambda e: e.tensor_tensor(y, bank[:, 0:D], b2_rows[:, bass.ds(expert(e, j) * D, D)],
                                                   ALU.add), m, b2_in, *yfree)
            ybanks.release(i, d)
            t["y"], t["yi"] = y, yi
            t["y_ok"] = DVE.mark(lambda e: e.tensor_scalar(y, y, w_slot[:, j:j + 1], None, ALU.mult), d)

        def add_up(j):
            t = tiles[j]
            t["added"] = POOL.dma(lambda e: e.indirect_dma_start(
                sums_d, bass.IndirectOffsetOnAxis(ap=rows_out[:, j:j + 1], axis=0), t["y"], None,
                compute_op=ALU.add), of_tile(j, s_sy, t["yi"], "maybe_y"), t["y_ok"], out_rows_ok,
                *([tiles[j - 1]["added"]] if j else [*tokens_in, zeros_in]))
            sy_ring.release(t["yi"], t["added"])

        w1_ring.free = [attention_free, None]
        load(0)
        weights_pool = place_weights(POOL, 2)
        take_w1(0)
        turn(0)
        load(1)
        i, found_w, weights_m = invert(weight_j, mbanks, weights_dve, weights_pool)
        m = DVE.mark(lambda e: e.tensor_copy(inv_w, found_w), weights_m)
        mbanks.release(i, m)
        m = DVE.mark(lambda e: e.tensor_tensor(w_slot[:, :], inv_w[:, 0, :], inv_w[:, 1, :], ALU.add), m)
        slots_ok = DVE.mark(lambda e: e.tensor_tensor(w_slot[:, :], w_slot[:, :], inv_w[:, 2, :], ALU.add), m)
        tables_free = (*attention_free, slots_ok)
        w1_ring.free[1] = tables_free
        hid_ring.free, act_ring.free, sy_ring.free = [tables_free] * 2, [tables_free] * 2, [tables_free] * 2
        for j in range(NSLOT + 1):
            for step, at_tile in ((turn, j + 1), (take_w1, j + 1), (up, j), (down, j - 1), (load, j + 2),
                                  (add_up, j - 1)):
                if 0 <= at_tile < NSLOT:
                    if_used(step, at_tile)

        PIECE = 4
        s_out = stream("out")
        s_back = [stream("sums") for _ in range(NT // PIECE)]
        rows = lambda ap, t: ap[t * P:(t + PIECE) * P, :].rearrange("(t p) n -> p t n", p=P)
        SP.wait(ej_ok, *(t["added"] for t in tiles[NSURE - 2:NSURE]))
        for t in tiles[NSURE:]:
            with SP.only_if(t["test"]):
                SP.wait(t["added"])
        back = [SP.dma(lambda e, n=n: e.dma_start(res[:, n * PIECE:(n + 1) * PIECE, :], rows(sums_d, n * PIECE)),
                       s_back[n]) for n in range(NT // PIECE)]
        flat_out = out.rearrange("b s n -> (b s) n")
        last = []

        def finish(n):
            for t in range(n * PIECE, (n + 1) * PIECE):
                m = norm_apply(t, last[n], G3, B3N)
            last[n] = SP.dma(lambda e: e.dma_start(rows(flat_out, n * PIECE),
                                                   res[:, n * PIECE:(n + 1) * PIECE, :]), s_out, m)

        for n in range(NT // PIECE):
            for t in range(n * PIECE, (n + 1) * PIECE):
                m = norm_stats(t, res[:, t, :], back[n], t % 2)
            last.append(norm_scale(n * PIECE, PIECE, m))
            if n:
                finish(n - 1)
        finish(NT // PIECE - 1)
        SP.wait(last[-1])

        block = stack.enter_context(nc.Block())

        @block.tensor
        def _(e):
            PE.run(e)

        @block.scalar
        def _(e):
            ACTE.run(e)

        @block.vector
        def _(e):
            DVE.run(e)

        @block.gpsimd
        def _(e):
            POOL.run(e)

        @block.sync
        def _(e):
            SP.run(e)


def kernel(**inputs):
    import concourse.bacc as bacc
    from concourse.bass_utils import run_bass_kernel_spmd

    nc = bacc.Bacc("TRN2", target_bir_lowering=False, num_devices=1)
    arrays, ap = {}, {}
    for name, value in inputs.items():
        a = np.ascontiguousarray(value)
        arrays[f"in_{name}"] = a
        ap[name.removeprefix("L0_xattn_")] = nc.dram_tensor(
            f"in_{name}", a.shape, mybir.dt.from_np(a.dtype), kind="ExternalInput").ap()
    out = nc.dram_tensor("out_0", (B, S, D), mybir.dt.float32, kind="ExternalOutput").ap()
    par = {
        "bq": (ap["sa_bq"], ap["ca_bq"]), "bk": (ap["sa_bk"], ap["ca_bk"]), "rb": ap["router_b"],
        "rows": [ap[n] for n in ("sa_bv", "sa_bo", "ca_bv", "ca_bo", "ln1_g", "ln1_b",
                                 "ln2_g", "ln2_b", "ln3_g", "ln3_b")],
    }
    wts = [ap[f"{a}_w{w}"] for a in ("sa", "ca") for w in "qkvo"]
    build(nc, ap["x"], ap["ctx_1024"], par, wts, ap["router_w"], ap["e_w1"], ap["e_b1"],
          ap["e_w2"], ap["e_b2"], out)
    r = run_bass_kernel_spmd(nc, [arrays], core_ids=[0])
    return r.results[0]["out_0"]
```
